# Optimizing a Trainium2 kernel written in Bass

```python
import numpy as np
import jax
import jax.numpy as jnp

def _softmax(x, axis=-1):
    return jax.nn.softmax(x, axis=axis)

def _gelu(x):
    return jax.nn.gelu(x, approximate=True)

def _silu(x):
    return jax.nn.silu(x)

def _sigmoid(x):
    return jax.nn.sigmoid(x)

def _layernorm(x, axis=-1, eps=1e-05):
    m = jnp.mean(x, axis=axis, keepdims=True)
    v = jnp.var(x, axis=axis, keepdims=True)
    return (x - m) / jnp.sqrt(v + eps)

def _scatter_add(tgt, idx, src, axis=0):
    return tgt.at[idx].add(src)

def _segment_sum(src, seg, n):
    return jax.ops.segment_sum(src, seg, n)
kernel_name = 'mk_gnn_ffn_d2_gnn_r32_3a3f59'

def setup_inputs(seed: int=0):
    np.random.seed(seed)
    _w = jnp.asarray

    def _rec_inputs():
        import jax
        import jax.numpy as jnp
        _gk = jax.random.key(seed)
        x = -0.0003713 + 1 * jax.random.normal(jax.random.fold_in(_gk, 1), (3125, 256), jnp.float32)
        src = jax.random.randint(jax.random.fold_in(_gk, 2), (50000,), 0, 3125, jnp.int32)
        dst = jnp.minimum((3125 * jax.random.uniform(jax.random.fold_in(_gk, 3), (50000,)) ** 2.0).astype(jnp.int32), 99999)
        _o = jnp.argsort(dst, stable=True)
        src = src[_o]
        dst = dst[_o]
        edge_type_64 = jax.random.randint(jax.random.fold_in(_gk, 13), (50000,), 0, 64, jnp.int32)
        return (x, src, dst, edge_type_64)
    x, src, dst, edge_type_64 = _rec_inputs()

    def _L0_gnn_setup():
        import jax, jax.numpy as jnp
        import numpy as np
        N_NODES = 50000
        N_EDGES = 15625
        IN_DIM = 256
        HID = 64
        HEADS = 4
        N_REL = 64
        key = jax.random.key(seed)
        ks = jax.random.split(key, 16)
        s = 0.02
        return {'node_features': jax.random.normal(ks[0], (N_NODES, IN_DIM), jnp.float32), 'edge_index': jax.random.randint(ks[1], (2, N_EDGES), 0, N_NODES, jnp.int32), 'edge_relations': jax.random.randint(ks[2], (N_EDGES,), 0, N_REL, jnp.int32), 'query_emb': jax.random.normal(ks[3], (IN_DIM,), jnp.float32), 'Wq': jax.random.normal(ks[4], (IN_DIM, HID * HEADS), jnp.float32) * s, 'bq': jnp.zeros((HID * HEADS,), jnp.float32), 'Wk': jax.random.normal(ks[5], (IN_DIM, HID * HEADS), jnp.float32) * s, 'bk': jnp.zeros((HID * HEADS,), jnp.float32), 'Wv': jax.random.normal(ks[6], (IN_DIM, HID * HEADS), jnp.float32) * s, 'bv': jnp.zeros((HID * HEADS,), jnp.float32), 'rel_w': jax.random.normal(ks[7], (N_REL, HID), jnp.float32) * s, 'Wo': jax.random.normal(ks[8], (HID * HEADS, IN_DIM), jnp.float32) * s, 'bo': jnp.zeros((IN_DIM,), jnp.float32), 'gamma': jnp.ones((IN_DIM,), jnp.float32), 'beta': jnp.zeros((IN_DIM,), jnp.float32)}
    _L0_gnn_all = _L0_gnn_setup()
    _L0_gnn_in = {k: v for k, v in _L0_gnn_all.items() if k in ('query_emb', 'Wq', 'bq', 'Wk', 'bk', 'Wv', 'bv', 'rel_w', 'Wo', 'bo', 'gamma', 'beta')}
    del _L0_gnn_all

    def _L0_ffn_setup():
        import math
        import jax, jax.numpy as jnp
        import numpy as np
        CAPACITY_FACTOR = 1.25
        key = jax.random.key(seed)
        ks = jax.random.split(key, 5)
        B, L, D, F, E = (8, 256, 256, 1024, 8)
        h = jax.random.normal(ks[0], (B, L, D), dtype=jnp.float32)
        gate_w = jax.random.normal(ks[1], (D, E), dtype=jnp.float32) * 0.02
        gate_b = jnp.zeros((E,), dtype=jnp.float32)
        w1 = jax.random.normal(ks[2], (E, D, F), dtype=jnp.float32) * (1.0 / math.sqrt(D))
        b1 = jnp.zeros((E, F), dtype=jnp.float32)
        w2 = jax.random.normal(ks[3], (E, F, D), dtype=jnp.float32) * (1.0 / math.sqrt(F))
        b2 = jnp.zeros((E, D), dtype=jnp.float32)
        return {'h': h, 'gate_w': gate_w, 'gate_b': gate_b, 'w1': w1, 'b1': b1, 'w2': w2, 'b2': b2}
    _L0_ffn_all = _L0_ffn_setup()
    _L0_ffn_in = {k: v for k, v in _L0_ffn_all.items() if k in ('gate_w', 'gate_b', 'w1', 'b1', 'w2', 'b2')}
    del _L0_ffn_all

    def _L1_gnn_setup():
        import jax, jax.numpy as jnp
        import numpy as np
        N = 625
        E = 10000
        HID = 256
        HEADS = 8
        HD = HID // HEADS
        key = jax.random.key(seed)
        ks = jax.random.split(key, 12)
        scale = 1.0 / np.sqrt(HID).astype(np.float32)

        def lin_w(k):
            return jax.random.normal(k, (HID, HID), jnp.float32) * scale

        def lin_b(k):
            return jax.random.normal(k, (HID,), jnp.float32) * 0.01
        return {'h': jax.random.normal(ks[0], (N, HID), jnp.float32), 'Wq': lin_w(ks[1]), 'bq': lin_b(ks[2]), 'Wk': lin_w(ks[3]), 'bk': lin_b(ks[4]), 'Wv': lin_w(ks[5]), 'bv': lin_b(ks[6]), 'Wo': lin_w(ks[7]), 'bo': lin_b(ks[8]), 'rows': jax.random.randint(ks[9], (E,), 0, N), 'cols': jax.random.randint(ks[10], (E,), 0, N)}
    _L1_gnn_all = _L1_gnn_setup()
    _L1_gnn_in = {k: v for k, v in _L1_gnn_all.items() if k in ('Wq', 'bq', 'Wk', 'bk', 'Wv', 'bv', 'Wo', 'bo')}
    del _L1_gnn_all

    def _L1_ffn_setup():
        import jax, jax.numpy as jnp
        import numpy as np
        B, S, D = (8, 128, 256)
        H = 4 * D
        CAPACITY = 0.5
        key = jax.random.key(seed)
        ks = jax.random.split(key, 6)
        x = jax.random.normal(ks[0], (B, S, D), dtype=jnp.float32)
        attention_mask = jnp.zeros((B, 1, 1, S), dtype=jnp.float32)
        wr = jax.random.normal(ks[1], (D, 1), dtype=jnp.float32) * 0.02
        br = jnp.zeros((1,), dtype=jnp.float32)
        w1 = jax.random.normal(ks[2], (D, H), dtype=jnp.float32) * 0.02
        b1 = jnp.zeros((H,), dtype=jnp.float32)
        w2 = jax.random.normal(ks[3], (H, D), dtype=jnp.float32) * 0.02
        b2 = jnp.zeros((D,), dtype=jnp.float32)
        return {'x': x, 'attention_mask': attention_mask, 'wr': wr, 'br': br, 'w1': w1, 'b1': b1, 'w2': w2, 'b2': b2}
    _L1_ffn_all = _L1_ffn_setup()
    _L1_ffn_in = {k: v for k, v in _L1_ffn_all.items() if k in ('attention_mask', 'wr', 'br', 'w1', 'b1', 'w2', 'b2')}
    del _L1_ffn_all
    return {'x': x, 'src': src, 'dst': dst, 'edge_type_64': edge_type_64, 'L0_gnn_query_emb': _L0_gnn_in['query_emb'], 'L0_gnn_Wq': _L0_gnn_in['Wq'], 'L0_gnn_bq': _L0_gnn_in['bq'], 'L0_gnn_Wk': _L0_gnn_in['Wk'], 'L0_gnn_bk': _L0_gnn_in['bk'], 'L0_gnn_Wv': _L0_gnn_in['Wv'], 'L0_gnn_bv': _L0_gnn_in['bv'], 'L0_gnn_rel_w': _L0_gnn_in['rel_w'], 'L0_gnn_Wo': _L0_gnn_in['Wo'], 'L0_gnn_bo': _L0_gnn_in['bo'], 'L0_gnn_gamma': _L0_gnn_in['gamma'], 'L0_gnn_beta': _L0_gnn_in['beta'], 'L0_ffn_gate_w': _L0_ffn_in['gate_w'], 'L0_ffn_gate_b': _L0_ffn_in['gate_b'], 'L0_ffn_w1': _L0_ffn_in['w1'], 'L0_ffn_b1': _L0_ffn_in['b1'], 'L0_ffn_w2': _L0_ffn_in['w2'], 'L0_ffn_b2': _L0_ffn_in['b2'], 'L1_gnn_Wq': _L1_gnn_in['Wq'], 'L1_gnn_bq': _L1_gnn_in['bq'], 'L1_gnn_Wk': _L1_gnn_in['Wk'], 'L1_gnn_bk': _L1_gnn_in['bk'], 'L1_gnn_Wv': _L1_gnn_in['Wv'], 'L1_gnn_bv': _L1_gnn_in['bv'], 'L1_gnn_Wo': _L1_gnn_in['Wo'], 'L1_gnn_bo': _L1_gnn_in['bo'], 'L1_ffn_attention_mask': _L1_ffn_in['attention_mask'], 'L1_ffn_wr': _L1_ffn_in['wr'], 'L1_ffn_br': _L1_ffn_in['br'], 'L1_ffn_w1': _L1_ffn_in['w1'], 'L1_ffn_b1': _L1_ffn_in['b1'], 'L1_ffn_w2': _L1_ffn_in['w2'], 'L1_ffn_b2': _L1_ffn_in['b2']}

def reference(x, src, dst, edge_type_64, L0_gnn_query_emb, L0_gnn_Wq, L0_gnn_bq, L0_gnn_Wk, L0_gnn_bk, L0_gnn_Wv, L0_gnn_bv, L0_gnn_rel_w, L0_gnn_Wo, L0_gnn_bo, L0_gnn_gamma, L0_gnn_beta, L0_ffn_gate_w, L0_ffn_gate_b, L0_ffn_w1, L0_ffn_b1, L0_ffn_w2, L0_ffn_b2, L1_gnn_Wq, L1_gnn_bq, L1_gnn_Wk, L1_gnn_bk, L1_gnn_Wv, L1_gnn_bv, L1_gnn_Wo, L1_gnn_bo, L1_ffn_attention_mask, L1_ffn_wr, L1_ffn_br, L1_ffn_w1, L1_ffn_b1, L1_ffn_w2, L1_ffn_b2):
    import jax
    import jax.numpy as jnp

    def _L0_gnn_ref(node_features, edge_index, edge_relations, query_emb, Wq, bq, Wk, bk, Wv, bv, rel_w, Wo, bo, gamma, beta):
        import jax, jax.numpy as jnp
        import numpy as np
        N_NODES = 50000
        N_EDGES = 15625
        IN_DIM = 256
        HID = 64
        HEADS = 4
        N_REL = 64
        N = node_features.shape[0]
        D = rel_w.shape[1]
        H = Wq.shape[1] // D
        enh = node_features + 0.1 * query_emb[None, :]
        Q = (enh @ Wq + bq).reshape(N, H, D)
        K = (enh @ Wk + bk).reshape(N, H, D)
        V = (enh @ Wv + bv).reshape(N, H, D)
        src, dst = (edge_index[0], edge_index[1])
        rel = rel_w[edge_relations]
        mod_k = K[src] + 0.2 * rel[:, None, :]
        scores = jnp.einsum('ehd,ehd->eh', Q[dst], mod_k) / D ** 0.5
        seg_max = jax.ops.segment_max(scores, dst, num_segments=N)
        ex = jnp.exp(scores - seg_max[dst])
        denom = jax.ops.segment_sum(ex, dst, num_segments=N)
        w = ex / denom[dst]
        agg = jax.ops.segment_sum(w[:, :, None] * V[src], dst, num_segments=N)
        deg = jax.ops.segment_sum(jnp.ones((src.shape[0],), jnp.float32), dst, num_segments=N)
        msgs = jnp.where(deg[:, None, None] > 0, agg, V)
        out = msgs.reshape(N, H * D) @ Wo + bo
        x = out + node_features
        mu = jnp.mean(x, axis=-1, keepdims=True)
        var = jnp.var(x, axis=-1, keepdims=True)
        return (x - mu) / jnp.sqrt(var + 1e-05) * gamma + beta

    def _L0_ffn_ref(h, gate_w, gate_b, w1, b1, w2, b2):
        import math
        import jax, jax.numpy as jnp
        import numpy as np
        CAPACITY_FACTOR = 1.25
        B, L, D = h.shape
        E = gate_w.shape[1]
        T = B * L
        C = max(1, math.ceil(CAPACITY_FACTOR * T / E))
        x = h.reshape(T, D)
        logits = x @ gate_w + gate_b
        probs = jax.nn.softmax(logits, axis=-1)
        idx = jnp.argmax(probs, axis=-1)
        prb = jnp.take_along_axis(probs, idx[:, None], axis=1)[:, 0]
        one_hot = jax.nn.one_hot(idx, E, dtype=jnp.float32)
        pos = (jnp.cumsum(one_hot, axis=0) * one_hot).sum(-1).astype(jnp.int32) - 1
        kept = pos < C
        pos_safe = jnp.where(kept, pos, C)
        buf = jnp.zeros((E, C, D), dtype=h.dtype).at[idx, pos_safe].set(x, mode='drop')
        hmid = jax.nn.relu(jnp.einsum('ecd,edf->ecf', buf, w1) + b1[:, None, :])
        ybuf = jnp.einsum('ecf,efd->ecd', hmid, w2) + b2[:, None, :]
        pos_g = jnp.minimum(pos, C - 1)
        y_tok = ybuf[idx, pos_g] * (prb * kept)[:, None]
        y = y_tok.reshape(B, L, D)
        y = jnp.nan_to_num(y, nan=0.0, posinf=10000.0, neginf=-10000.0)
        return y

    def _L1_gnn_ref(h, Wq, bq, Wk, bk, Wv, bv, Wo, bo, rows, cols):
        import jax, jax.numpy as jnp
        import numpy as np
        N = 625
        E = 10000
        HID = 256
        HEADS = 8
        HD = HID // HEADS
        n = h.shape[0]
        scaling = HD ** (-0.5)
        q = (h @ Wq + bq).reshape(n, HD, HEADS) * scaling
        k = (h @ Wk + bk).reshape(n, HD, HEADS)
        v = (h @ Wv + bv).reshape(n, HD, HEADS)
        s = jnp.einsum('edh,edh->eh', q[rows], k[cols])
        m = jax.ops.segment_max(s, rows, num_segments=n)
        e = jnp.exp(s - m[rows])
        z = jax.ops.segment_sum(e, rows, num_segments=n)
        attn = e / z[rows]
        out = jax.ops.segment_sum(attn[:, None, :] * v[cols], rows, num_segments=n)
        return out.reshape(n, -1) @ Wo + bo

    def _L1_ffn_ref(x, attention_mask, wr, br, w1, b1, w2, b2):
        import jax, jax.numpy as jnp
        import numpy as np
        B, S, D = (8, 128, 256)
        H = 4 * D
        CAPACITY = 0.5
        b, s, d = x.shape
        weights = (jnp.einsum('bsd,do->bso', x, wr) + br)[..., 0]
        k = max(1, int(CAPACITY * s))
        kk = k - 1 if k > 1 else 1
        _, idx = jax.lax.top_k(weights, k)
        sel_idx = idx[:, :kk]
        sel = jnp.take_along_axis(x, sel_idx[:, :, None], axis=1)
        h = jax.nn.gelu(jnp.einsum('bkd,dh->bkh', sel, w1) + b1)
        y = jnp.einsum('bkh,hd->bkd', h, w2) + b2
        w_sel = jnp.take_along_axis(weights, sel_idx, axis=1)
        y = y * w_sel[..., None]
        batch_idx = jnp.arange(b)[:, None]
        processed = jnp.zeros_like(x).at[batch_idx, sel_idx].set(y)
        return processed + x
    edge_index = jnp.stack([src, dst])
    x = x + _L0_gnn_ref(_layernorm(x, axis=-1), edge_index, edge_type_64, L0_gnn_query_emb, L0_gnn_Wq, L0_gnn_bq, L0_gnn_Wk, L0_gnn_bk, L0_gnn_Wv, L0_gnn_bv, L0_gnn_rel_w, L0_gnn_Wo, L0_gnn_bo, L0_gnn_gamma, L0_gnn_beta)
    x = x + _L0_ffn_ref(_layernorm(x, axis=-1)[None], L0_ffn_gate_w, L0_ffn_gate_b, L0_ffn_w1, L0_ffn_b1, L0_ffn_w2, L0_ffn_b2)[0]
    x = x + _L1_gnn_ref(_layernorm(x, axis=-1), L1_gnn_Wq, L1_gnn_bq, L1_gnn_Wk, L1_gnn_bk, L1_gnn_Wv, L1_gnn_bv, L1_gnn_Wo, L1_gnn_bo, src, dst)
    x = x + _L1_ffn_ref(_layernorm(x, axis=-1)[None], L1_ffn_attention_mask, L1_ffn_wr, L1_ffn_br, L1_ffn_w1, L1_ffn_b1, L1_ffn_w2, L1_ffn_b2)[0]
    return x

_drawn_inputs = setup_inputs


def setup_inputs(seed=0):
    import zlib

    import numpy as np

    out = dict(_drawn_inputs(seed))
    spreads = {'L0_gnn_bq': (0.0, 0.8),
     'L0_gnn_bk': (0.0, 2.0),
     'L0_gnn_bv': (0.0, 0.401),
     'L0_gnn_bo': (0.0, 0.1),
     'L0_gnn_gamma': (1.0, 0.2),
     'L0_gnn_beta': (0.0, 0.1),
     'L0_ffn_gate_b': (0.0, 0.1),
     'L0_ffn_b1': (0.0, 0.8),
     'L0_ffn_b2': (0.0, 0.8),
     'L1_ffn_b1': (0.0, 0.8),
     'L1_ffn_b2': (0.0, 0.8)}
    factors = {'L0_gnn_query_emb': 8.0,
     'L0_gnn_Wq': 8.0,
     'L0_gnn_Wk': 8.0,
     'L0_gnn_Wv': 3.092,
     'L0_gnn_rel_w': 27.939,
     'L1_gnn_bq': 8.0,
     'L1_gnn_bk': 64.0,
     'L1_gnn_bv': 8.0,
     'L1_gnn_bo': 8.0,
     'L1_ffn_wr': 5.596,
     'L1_ffn_w1': 7.026,
     'L1_ffn_w2': 6.523}
    for name, (base, spread) in spreads.items():
        noise = np.random.default_rng([zlib.crc32(name.encode()), seed]).standard_normal(out[name].shape)
        drawn = base * np.exp(spread * noise) if base else spread * noise
        out[name] = jnp.asarray(drawn.astype(out[name].dtype))
    for name, factor in factors.items():
        out[name] = (out[name] * factor).astype(out[name].dtype)
    return out
```

```python
from contextlib import ExitStack

import concourse.bass as bass
from concourse import mybir
import numpy as np

F32 = mybir.dt.float32
BF16 = mybir.dt.bfloat16
I32 = mybir.dt.int32
ALU = mybir.AluOpType
ACT = mybir.ActivationFunctionType
AX = mybir.AxisListType

P = 128
N = 3125
D = 256
C2 = D // P
E = 50000
NT = -(-N // P)
LAST = N - (NT - 1) * P
TB = NT + 1
EC = -(-E // P)
EFULL = E // EC
EREST = E - EFULL * EC
GE = 2 * P
NG = (E - NT) // GE + NT
NS = 2 * NG
SPI = 8
GPI = SPI // 2
TURNS = NS // SPI
SW = NS + SPI
GW = SW // 2
NREL = 64
BIG = 1.0e30
assert NS % SPI == 0 and EREST > 0 and TB % 2 == 0

SCAT = 17
HALF = (12, 11)
assert SCAT * sum(HALF) == EC
HA, HB = 4, 8
EXPERTS, CAP, FF = 8, 489, 1024
CAPW = 512
FC = FF // P


class Steps:

    def __init__(self, eng, sem, start=0):
        self.eng, self.sem, self.n = eng, sem, start

    def __call__(self, ins):
        self.n += 1
        return ins.then_inc(self.sem, 1)

    def sync(self):
        self.eng.wait_ge(self.sem, self.n)

    def link(self, ins):
        self(ins)
        self.sync()


def hold(eng, sem, value):
    eng.wait_ge(sem, value)
    eng.nop(nofuse=True)


class Consts:
    pass


def stage_constants(nc, c, sem, x):
    made = sem("constants_made")
    pooled = sem("constants_pool")
    got = sem("x_loaded")
    with nc.Block() as block:

        @block.gpsimd
        def _(pool):
            st = Steps(pool, pooled)
            st(nc.gpsimd.memset(c.ident[:, :], 0.0))
            st(nc.gpsimd.memset(c.before[:, :], 1.0))
            st(nc.gpsimd.memset(c.upto[:, :], 1.0))
            st(nc.gpsimd.memset(c.ones[:, :], 1.0))
            st(nc.gpsimd.memset(c.sel[:, :, :, :], 1.0))
            st(nc.gpsimd.memset(c.zero[:, :], 0.0))
            st(nc.gpsimd.iota(c.spare_i[:, :], pattern=[[P, TB]], base=EXPERTS * CAPW, channel_multiplier=1))
            st(nc.gpsimd.iota(c.iota_i[:, :], pattern=[[1, 256]], base=0, channel_multiplier=0))
            st.sync()
            st(nc.gpsimd.affine_select(out=c.ident[:, :], in_=c.ident[:, :], compare_op=ALU.not_equal, fill=1.0,
                                       base=0, pattern=[[-1, P]], channel_multiplier=1))
            st(nc.gpsimd.affine_select(out=c.before[:, :], in_=c.before[:, :], compare_op=ALU.is_gt, fill=0.0,
                                       base=0, pattern=[[1, P]], channel_multiplier=-1))
            st(nc.gpsimd.affine_select(out=c.upto[:, :], in_=c.upto[:, :], compare_op=ALU.is_ge, fill=0.0,
                                       base=0, pattern=[[1, P]], channel_multiplier=-1))
            st(nc.gpsimd.affine_select(out=c.sel[:, 0, :, :], in_=c.sel[:, 0, :, :], compare_op=ALU.is_equal,
                                       fill=0.0, base=0, pattern=[[-1, HB], [0, P]], channel_multiplier=1))
            st(nc.gpsimd.affine_select(out=c.sel[:, 1, :, :], in_=c.sel[:, 1, :, :], compare_op=ALU.is_equal,
                                       fill=0.0, base=-HB, pattern=[[-1, HB], [0, P]], channel_multiplier=1))
            st.sync()
            nc.gpsimd.tensor_copy(c.spare[:, :], c.spare_i[:, :]).then_inc(made, 1)
            nc.gpsimd.tensor_copy(c.iota[:, :], c.iota_i[:, :]).then_inc(made, 1)

        @block.vector
        def _(dve):
            nc.vector.memset(c.x[:, NT - 1:TB, :], 0.0).then_inc(got, 1)
            dve.wait_ge(pooled, 13)
            nc.vector.tensor_copy(c.ident_b[:, :], c.ident[:, :]).then_inc(made, 1)
            nc.vector.tensor_scalar(c.big_b[:, :], c.ident[:, :], BIG, None, ALU.mult).then_inc(made, 1)
            nc.vector.tensor_tensor(c.sel_b[:, :, :], c.sel[:, 0, :, :], c.sel[:, 1, :, :],
                                    ALU.add).then_inc(made, 1)

        @block.sync
        def _(sp):
            sp.dma_start(c.x[:, 0:NT - 1, :],
                         x[0:(NT - 1) * P, :].rearrange("(t p) d -> p t d", p=P)).then_inc(got, 16)
            sp.wait_ge(got, 17)
            sp.dma_start(c.x[0:LAST, NT - 1, :], x[(NT - 1) * P:N, :]).then_inc(got, 16)
            sp.wait_ge(got, 33)
            sp.wait_ge(made, 5)


class NormSemaphores:
    def __init__(self, sem, tag):
        self.stats = sem(tag + "norm_stats")
        self.var = sem(tag + "norm_var")
        self.std = sem(tag + "norm_std")
        self.ready = sem(tag + "norm_ready")


def norm_vector(nc, dve, c, norm, x):
    with dve.Fori(0, TB) as t:
        nc.vector.bn_stats(c.stats[:, t, :], x[:, t, :]).then_inc(norm.stats, 1)
    dve.wait_ge(norm.stats, TB)
    st = Steps(dve, norm.stats, TB)
    mean_e, m2_e, mean_o, m2_o = (c.stats[:, :, k] for k in (1, 2, 4, 5))
    st(nc.vector.tensor_tensor(c.norm[:, 0, :], mean_e, mean_o, ALU.add))
    st(nc.vector.tensor_tensor(c.norm[:, 1, :], mean_e, mean_o, ALU.subtract))
    st(nc.vector.tensor_tensor(c.norm[:, 2, :], m2_e, m2_o, ALU.add))
    st.sync()
    st.link(nc.vector.tensor_tensor(c.norm[:, 1, :], c.norm[:, 1, :], c.norm[:, 1, :], ALU.mult))
    st.link(nc.vector.scalar_tensor_tensor(c.norm[:, 2, :], c.norm[:, 1, :], D / 4.0, c.norm[:, 2, :],
                                           ALU.mult, ALU.add))
    nc.vector.tensor_scalar(c.norm[:, 3, :], c.norm[:, 2, :], 1.0 / D, 1e-5, ALU.mult, ALU.add).then_inc(norm.var, 1)
    dve.wait_ge(norm.std, 1)
    st.link(nc.vector.reciprocal(c.rstd[:, :], c.norm[:, 1, :]))
    nc.vector.scalar_tensor_tensor(c.shift[:, :], c.norm[:, 0, :], -0.5, c.rstd[:, :], ALU.mult,
                                   ALU.mult).then_inc(norm.ready, 1)


def norm_scalar(nc, act, norm, c):
    act.wait_ge(norm.var, 1)
    nc.scalar.activation(c.norm[:, 1, :], c.norm[:, 3, :], ACT.Sqrt).then_inc(norm.std, 1)


def stage_place_and_project(nc, c, sem, edges, weights, dram, layer):
    H = HA if layer == 0 else HB
    T = f"L{layer}_"
    with ExitStack() as ctx:
        def sb(name, shape, dt):
            return ctx.enter_context(nc.sbuf_tensor(T + name, shape, dt))

        def ps(name, shape, dt):
            return ctx.enter_context(nc.psum_tensor(T + name, shape, dt))

        w = sb("wqkv", [P, C2, 3 * D], F32)
        bias = sb("bqkv", [P, 3 * D], F32)
        hn = sb("hn", [P, 2, D], F32)
        hT = [sb(f"hT{u}", [P, C2, P], F32) for u in range(2)]
        qkv = sb("qkv", [P, 2, 3 * D], F32)
        rest = sb("rest", [P, 2, D], F32)
        pT = [ps(f"pT{u}", [P, D], F32) for u in range(2)]
        pQK = ps("pQK", [P, 2, 2 * D], F32)
        pV = [ps(f"pV{u}", [P, D], F32) for u in range(2)]
        if layer == 0:
            rel_in = sb("rel_in", [NREL, NREL], F32)
            rel_rest = sb("rel_rest", [NREL, NREL], F32)
            q_col = sb("q_col", [P, C2], F32)
            q_cols = sb("q_cols", [P, C2, P], F32)
        stage_i = [sb(f"stage_i{u}", [P, HALF[u]], I32) for u in range(2)]
        stage_r = [sb(f"stage_r{u}", [P, HALF[u], 4], F32) for u in range(2)]
        dst_i = sb("dst_i", [P, EC], I32)
        src_i = sb("src_i", [P, EC], I32)
        typ_i = sb("typ_i", [P, EC], I32)
        lo_i = sb("lo_i", [P, EC], I32)
        hi_i = sb("hi_i", [P, EC], I32)
        hi_f = sb("hi_f", [P, EC], F32)
        record = sb("record", [P, EC, 4], F32)
        is_b = sb("is_b", [P, TB, EC], BF16)
        rank = sb("rank", [P, TB, EC], F32)
        count = sb("count", [P, TB], F32)
        small = sb("small", [P, 6, TB], F32)
        small_i = sb("small_i", [P, 2, TB], I32)
        pos = sb("pos", [P, EC], F32)
        pos_i = sb("pos_i", [P, 3, EC], I32)
        later = is_b[:, :, :].rearrange("p b e -> p (b e)")[:, 0:GW * NT].rearrange("p (g b) -> p g b", b=NT)
        blank = c.rec
        gb_f = sb("gb_f", [P, GW], F32)
        pC = ps("pC", [P, 2, TB], F32)

        loaded = sem(T + "w_loaded")
        edges_loaded = sem(T + "edges_loaded")
        edges_blank = sem(T + "edges_blank")
        blank_made = sem(T + "blank_made")
        v = sem(T + "dve_steps")
        counted = sem(T + "counted")
        summed = sem(T + "summed")
        placed = sem(T + "placed")
        list_in = sem(T + "list_in")
        staged = sem(T + "staged")
        scattered = [sem(T + f"scattered{u}") for u in range(2)]
        weights_ready = sem(T + "weights_ready")
        query_summed = sem(T + "query_summed")
        norm = NormSemaphores(sem, T)
        hn_ready = sem(T + "hn_ready")
        hT_psum = sem(T + "hT_psum")
        hT_ready = sem(T + "hT_ready")
        qkv_psum = sem(T + "qkv_psum")
        biased = sem(T + "biased")
        tile_steps = sem(T + "tile_steps")
        stored = [sem(T + f"stored{u}") for u in range(2)]
        Wq, bq, Wk, bk, Wv, bv, rel, q_emb = weights
        half = HALF

        with nc.Block() as block:

            @block.sync
            def _(sp):
                src, dst, typ = edges
                sp.wait_ge(edges_blank, 3)
                for tile, a in ((dst_i, dst), (src_i, src), (typ_i, typ)):
                    sp.dma_start(tile[0:EFULL, :],
                                 a[0:EFULL * EC].rearrange("(p e) -> p e", p=EFULL)).then_inc(edges_loaded, 16)
                    sp.dma_start(tile[EFULL:EFULL + 1, 0:EREST],
                                 a[EFULL * EC:E].rearrange("(p e) -> p e", p=1)).then_inc(edges_loaded, 16)
                for k, a in enumerate((Wq, Wk, Wv)):
                    sp.dma_start(w[:, :, k * D:(k + 1) * D],
                                 a.rearrange("(c p) n -> p c n", p=P)).then_inc(loaded, 16)
                for k, a in enumerate((bq, bk, bv)):
                    sp.dma_start(bias[:, k * D:(k + 1) * D],
                                 a.rearrange("(o n) -> o n", o=1).broadcast_to([P, D])).then_inc(loaded, 16)
                if layer == 0:
                    sp.dma_start(q_col[:, :], q_emb.rearrange("(c p) -> p c", p=P), allow_slow_non_contiguous=True).then_inc(loaded, 16)
                    sp.dma_start(rel_in[:, :], rel).then_inc(loaded, 16)
                with sp.Fori(0, TB // 2) as i:
                    for u in range(2):
                        hold(sp, biased, i * 2 + u + 3)
                        rows = bass.ds((i * 2 + u) * P, P)
                        sp.dma_start(dram.k[rows, :], qkv[:, u, D:2 * D]).then_inc(stored[u], 16)
                        sp.dma_start(dram.v[rows, :], qkv[:, u, 2 * D:3 * D]).then_inc(stored[u], 16)
                for u in range(2):
                    sp.wait_ge(stored[u], TB // 2 * 32)
                for u in range(2):
                    sp.wait_ge(scattered[u], SCAT * half[u] * 16 + 16)
                sp.dma_start(c.rec[:, :, :].rearrange("p s f -> p (s f)"),
                             dram.list.rearrange("(p s) f -> p (s f)", p=P)).then_inc(list_in, 16)
                sp.wait_ge(list_in, 16)

            @block.gpsimd
            def _(pool):
                nc.gpsimd.memset(dst_i[:, :], NT * P).then_inc(edges_blank, 1)
                nc.gpsimd.memset(src_i[:, :], 0).then_inc(edges_blank, 1)
                nc.gpsimd.memset(typ_i[:, :], 0).then_inc(edges_blank, 1)
                nc.gpsimd.memset(blank[:, :, 0], 0.0).then_inc(blank_made, 1)
                nc.gpsimd.memset(blank[:, :, 1], 200.0).then_inc(blank_made, 1)
                nc.gpsimd.memset(blank[:, :, 2:4], 100.0).then_inc(blank_made, 1)
                pool.wait_ge(blank_made, 3)
                for u in range(2):
                    nc.gpsimd.dma_start(
                        dram.list.rearrange("(p s) f -> p (s f)", p=P)[u * (P // 2):(u + 1) * (P // 2), :],
                        blank[u * (P // 2):(u + 1) * (P // 2), :, :].rearrange("p s f -> p (s f)")).then_inc(scattered[u], 16)
                pool.wait_ge(placed, 1)
                for u in range(2):
                    pool.wait_ge(scattered[u], 16)
                with pool.Fori(0, SCAT) as i:
                    for u in range(2):
                        col = i * (half[0] + half[1]) + u * half[0]
                        hold(pool, scattered[u], i * (16 * half[u]) + 16)
                        nc.gpsimd.tensor_copy(stage_i[u][:, :], pos_i[:, 2, bass.ds(col, half[u])]).then_inc(staged, 1)
                        nc.gpsimd.tensor_copy(stage_r[u][:, :, :],
                                              record[:, bass.ds(col, half[u]), :]).then_inc(staged, 1)
                        hold(pool, staged, i * 4 + u * 2 + 2)
                        for j in range(half[u]):
                            nc.gpsimd.indirect_dma_start(
                                out=dram.list,
                                out_offset=bass.IndirectOffsetOnAxis(ap=stage_i[u][:, j:j + 1], axis=0),
                                in_=stage_r[u][:, j, :], in_offset=None).then_inc(scattered[u], 16)

            @block.vector
            def _(dve):
                st = Steps(dve, v)
                dve.wait_ge(edges_loaded, 96)
                st(nc.vector.tensor_scalar(lo_i[:, :], dst_i[:, :], P - 1, None, ALU.bitwise_and))
                st(nc.vector.tensor_scalar(hi_i[:, :], dst_i[:, :], 7, None, ALU.arith_shift_right))
                st(nc.vector.tensor_copy(record[:, :, 0].bitcast(I32), src_i[:, :]))
                st(nc.vector.tensor_copy(record[:, :, 2], typ_i[:, :]))
                st(nc.vector.memset(record[:, :, 3], 0.0))
                st.sync()
                st(nc.vector.tensor_copy(record[:, :, 1], lo_i[:, :]))
                st.link(nc.vector.tensor_copy(hi_f[:, :], hi_i[:, :]))
                st.link(nc.vector.tensor_tensor(is_b[:, :, :],
                                                hi_f[:, :].unsqueeze(1).broadcast_to([P, TB, EC]),
                                                c.iota[:, 0:TB].unsqueeze(2).broadcast_to([P, TB, EC]),
                                                ALU.is_equal))
                flat = is_b[:, :, :].rearrange("p b e -> p (b e)")
                st.link(nc.vector.tensor_tensor_scan(rank[:, :, :].rearrange("p b e -> p (b e)"), flat, flat,
                                                     0.0, ALU.add, ALU.bypass))
                ends = rank[:, :, EC - 1]
                st(nc.vector.tensor_copy(count[:, 0:1], ends[:, 0:1]))
                st(nc.vector.tensor_tensor(count[:, 1:TB], ends[:, 1:TB], ends[:, 0:TB - 1], ALU.subtract))
                st.sync()
                nc.vector.tensor_tensor(small[:, 0, :], count[:, :], ends, ALU.subtract).then_inc(counted, 1)
                dve.wait_ge(summed, 2)
                dve.wait_ge(counted, 1)
                st(nc.vector.tensor_tensor(small[:, 1, :], small[:, 0, :], pC[:, 0, :], ALU.add))
                st.link(nc.vector.tensor_scalar(small_i[:, 0, :], pC[:, 1, :], float(GE - 1), None, ALU.add))
                st.link(nc.vector.tensor_scalar(small_i[:, 1, :], small_i[:, 0, :], 8, None,
                                                ALU.arith_shift_right))
                st.link(nc.vector.tensor_copy(small[:, 2, :], small_i[:, 1, :]))
                st.link(nc.vector.tensor_tensor_scan(small[:, 3, :], small[:, 2, :], small[:, 2, :], 0.0,
                                                     ALU.add, ALU.bypass))
                st.link(nc.vector.tensor_tensor(small[:, 4, :], small[:, 3, :], small[:, 2, :], ALU.subtract))
                st.link(nc.vector.tensor_scalar(small[:, 5, :], small[:, 4, :], float(GE), -1.0,
                                                ALU.mult, ALU.add))
                st.link(nc.vector.tensor_tensor(small[:, 4, :], small[:, 5, :], small[:, 1, :], ALU.add))
                st.link(nc.vector.tensor_tensor(rank[:, :, :], rank[:, :, :],
                                                small[:, 4, :].unsqueeze(2).broadcast_to([P, TB, EC]), ALU.add))
                st.link(nc.vector.tensor_tensor(rank[:, :, :], rank[:, :, :], is_b[:, :, :], ALU.mult))
                st.link(nc.vector.tensor_reduce(pos[:, :], rank[:, :, :].rearrange("p b e -> p e b"),
                                                AX.X, ALU.add))
                st.link(nc.vector.tensor_copy(pos_i[:, 0, :], pos[:, :]))
                st(nc.vector.tensor_scalar(pos_i[:, 1, :], pos_i[:, 0, :], P - 1, None, ALU.bitwise_and))
                st.link(nc.vector.tensor_scalar(pos_i[:, 2, :], pos_i[:, 0, :], 7, None, ALU.arith_shift_right))
                st.link(nc.vector.scalar_tensor_tensor(pos[:, :], pos_i[:, 1, :], float(SW), pos_i[:, 2, :],
                                                       ALU.mult, ALU.add))
                st.sync()
                nc.vector.tensor_copy(pos_i[:, 2, :], pos[:, :]).then_inc(placed, 1)
                st.link(nc.vector.tensor_tensor(later,
                                                small[:, 3, 0:NT].unsqueeze(1).broadcast_to([P, GW, NT]),
                                                c.iota[:, 0:GW].unsqueeze(2).broadcast_to([P, GW, NT]),
                                                ALU.is_le))
                st.link(nc.vector.tensor_reduce(gb_f[:, :], later, AX.X, ALU.add))
                st(nc.vector.tensor_copy(c.gb[:, :], gb_f[:, :]))
                st(nc.vector.memset(c.first[:, :], -BIG))
                st(nc.vector.memset(c.final[:, :], -BIG))
                st.sync()
                st(nc.vector.tensor_tensor(c.first[:, 1:NG], gb_f[:, 1:NG], gb_f[:, 0:NG - 1], ALU.not_equal))
                st(nc.vector.tensor_tensor(c.final[:, 0:NG - 1], gb_f[:, 1:NG], gb_f[:, 0:NG - 1],
                                           ALU.not_equal))
                st.sync()
                st(nc.vector.tensor_scalar(c.first[:, 1:NG], c.first[:, 1:NG], -BIG, None, ALU.mult))
                st(nc.vector.tensor_scalar(c.final[:, 0:NG - 1], c.final[:, 0:NG - 1], -BIG, None, ALU.mult))
                if layer == 0:
                    dve.wait_ge(loaded, 128)
                    st.link(nc.vector.tensor_scalar(rel_in[:, :], rel_in[:, :], 0.2, None, ALU.mult))
                    st.link(nc.vector.tensor_copy(c.rel[:, 0, :], rel_in[:, :]))
                    st.link(nc.vector.tensor_tensor(rel_rest[:, :], rel_in[:, :], c.rel[:, 0, :], ALU.subtract))
                    st.link(nc.vector.tensor_copy(c.rel[:, 1, :], rel_rest[:, :]))
                    st(nc.vector.tensor_tensor(c.rel[:, 2, :], rel_rest[:, :], c.rel[:, 1, :], ALU.subtract))
                    st(nc.vector.tensor_scalar(q_cols[:, :, :],
                                               q_col[:, :].unsqueeze(2).broadcast_to([P, C2, P]), 0.1, None,
                                               ALU.mult))
                else:
                    dve.wait_ge(loaded, 96)
                scale = float(D // H) ** -0.5
                st(nc.vector.tensor_scalar(w[:, :, 0:D], w[:, :, 0:D], scale, None, ALU.mult))
                st(nc.vector.tensor_scalar(bias[:, 0:D], bias[:, 0:D], scale, None, ALU.mult))
                st.sync()
                dve.sem_inc(weights_ready, 1)
                norm_vector(nc, dve, c, norm, c.x)
                if layer == 0:
                    dve.wait_ge(query_summed, 2)
                    st(nc.vector.tensor_tensor(bias[:, 0:2 * D], pQK[:, 0, :], bias[:, 0:2 * D], ALU.add))
                    st(nc.vector.tensor_tensor(bias[:, 2 * D:], pV[0][:, :], bias[:, 2 * D:], ALU.add))
                    st.sync()
                dve.sem_inc(biased, 2)
                def pair(i, first=False):
                    for u in range(2):
                        t = i * 2 + u
                        tick = i * 10 + u * 5
                        if not first:
                            dve.wait_ge(stored[u], i * 32)
                        dve.wait_ge(qkv_psum, t + 3)
                        nc.vector.tensor_tensor(qkv[:, u, 0:2 * D], pQK[:, u, :], bias[:, 0:2 * D],
                                                ALU.add).then_inc(tile_steps, 1)
                        nc.vector.tensor_tensor(qkv[:, u, 2 * D:], pV[u][:, :], bias[:, 2 * D:],
                                                ALU.add).then_inc(biased, 1)
                        dve.wait_ge(tile_steps, tick + 1)
                        nc.vector.tensor_copy(c.q[:, t, 0, :], qkv[:, u, 0:D]).then_inc(tile_steps, 1)
                        dve.wait_ge(tile_steps, tick + 2)
                        nc.vector.tensor_tensor(rest[:, u, :], qkv[:, u, 0:D], c.q[:, t, 0, :],
                                                ALU.subtract).then_inc(tile_steps, 1)
                        dve.wait_ge(tile_steps, tick + 3)
                        nc.vector.tensor_copy(c.q[:, t, 1, :], rest[:, u, :]).then_inc(tile_steps, 1)
                        dve.wait_ge(tile_steps, tick + 4)
                        nc.vector.tensor_tensor(c.q[:, t, 2, :], rest[:, u, :], c.q[:, t, 1, :],
                                                ALU.subtract).then_inc(tile_steps, 1)

                pair(0, first=True)
                with dve.Fori(1, TB // 2) as i:
                    pair(i)

            @block.scalar
            def _(act):
                norm_scalar(nc, act, norm, c)
                act.wait_ge(norm.ready, 1)
                with act.Fori(0, TB // 2) as i:
                    for u in range(2):
                        t = i * 2 + u
                        hold(act, qkv_psum, t + 1)
                        nc.scalar.activation(hn[:, u, :], c.x[:, t, :], ACT.Identity, bias=c.shift[:, bass.ds(t, 1)],
                                             scale=c.rstd[:, bass.ds(t, 1)]).then_inc(hn_ready, 1)
                        hold(act, hT_psum, t + 1)
                        nc.scalar.activation(hT[u][:, :, :].rearrange("p c n -> p (c n)"), pT[u][:, :],
                                             ACT.Copy).then_inc(hT_ready, 1)

            @block.tensor
            def _(pe):
                pe.wait_ge(counted, 1)
                nc.tensor.matmul(pC[:, 0, :], c.before[:, :], count[:, :], start=True, stop=True).then_inc(summed, 1)
                nc.tensor.matmul(pC[:, 1, :], c.ones[:, :], count[:, :], start=True, stop=True).then_inc(summed, 1)
                pe.wait_ge(weights_ready, 1)
                if layer == 0:
                    for out, lo, hi in ((pQK[:, 0, :], 0, 2 * D), (pV[0][:, :], 2 * D, 3 * D)):
                        for k in range(C2):
                            last = nc.tensor.matmul(out, q_cols[:, k, :], w[:, k, lo:hi], start=k == 0, stop=k == C2 - 1)
                        last.then_inc(query_summed, 1)
                pe.sem_inc(qkv_psum, 2)
                with pe.Fori(0, TB // 2) as i:
                    for u in range(2):
                        t = i * 2 + u
                        pe.wait_ge(hn_ready, t + 1)
                        for k in range(C2):
                            last = nc.tensor.transpose(pT[u][:, k * P:(k + 1) * P], hn[:, u, k * P:(k + 1) * P],
                                                       c.ident[:, :])
                        last.then_inc(hT_psum, 1)
                        pe.wait_ge(hT_ready, t + 1)
                        pe.wait_ge(biased, t + 1)
                        for out, lo, hi in ((pQK[:, u, :], 0, 2 * D), (pV[u][:, :], 2 * D, 3 * D)):
                            for k in range(C2):
                                last = nc.tensor.matmul(out, hT[u][:, k, :], w[:, k, lo:hi], start=k == 0,
                                                        stop=k == C2 - 1)
                        last.then_inc(qkv_psum, 1)


def gather_rows(nc, pool, sem, T, table, rec, stage, ring, gathered, used):
    staged = sem(T + "indices_staged")
    with pool.Fori(0, TURNS) as i:
        for half in range(2):
            hold(pool, used, i * GPI + 2 * half + 2)
            nc.gpsimd.tensor_copy(stage[half][:, :],
                                  rec[:, bass.ds(i * SPI + half * 4, 4), 0].bitcast(I32)).then_inc(staged, 1)
            hold(pool, staged, i * 2 + half + 1)
            for q in (2 * half, 2 * half + 1):
                for k in range(2):
                    nc.gpsimd.indirect_dma_start(
                        out=ring[:, 2 * q + k, :], out_offset=None, in_=table,
                        in_offset=bass.IndirectOffsetOnAxis(ap=stage[half][:, 2 * (q % 2) + k:2 * (q % 2) + k + 1],
                                                            axis=0)).then_inc(gathered[q], 16)


def stage_scores(nc, c, sem, dram, layer):
    H = HA if layer == 0 else HB
    NH = H // HA
    T = f"L{layer}_score_"
    with ExitStack() as ctx:
        def sb(name, shape, dt):
            return ctx.enter_context(nc.sbuf_tensor(T + name, shape, dt))

        def ps(name, shape, dt):
            return ctx.enter_context(nc.psum_tensor(T + name, shape, dt))

        kg = sb("kg", [P, SPI, D], F32)
        stage = [sb(f"stage{u}", [P, 4], I32) for u in range(2)]
        oh = sb("oh", [P, SPI, P], BF16)
        ty = sb("ty", [P, SPI, NREL], BF16)
        ohT = sb("ohT", [P, GPI, GE], BF16)
        ohTm = sb("ohTm", [P, GPI, GE], BF16)
        tyT = sb("tyT", [NREL, 2, GE], BF16)
        prod = sb("prod", [P, 2, 2 * D], F32)
        sp2 = sb("sp2", [P, 2, 2, 2 * HB], BF16)
        sT = sb("sT", [2 * HB, 2, GE], BF16)
        mp = sb("mp", [P, HB, GW], F32)
        fw = sb("fw", [P, HB, GW], F32)
        BT, BM = (2, 1) if layer == 0 else (1, 2)
        pT = [ps(f"pT{u}", [P, 2, GE], BF16) for u in range(BT)]
        if layer == 0:
            pR = ps("pR", [P, 2, NREL], F32)
        pS = ps("pS", [2 * HB, GE], BF16)
        pQ = [ps(f"pQ{u}", [P, 2 * D], F32) for u in range(2)]
        pM = [ps(f"pM{u}", [P, HA * GE], F32) for u in range(BM)]

        gathered = [sem(T + f"k_gathered{q}") for q in range(GPI)]
        cleared = sem(T + "cleared")
        oh_made = sem(T + "onehot_made")
        tr_done = sem(T + "onehot_transposed")
        ohT_ready = sem(T + "onehotT_ready")
        qe_ready = sem(T + "q_of_edges_ready")
        added = sem(T + "relation_added")
        prod_done = sem(T + "product_done")
        s_ready = sem(T + "scores_ready")
        hi_ready = sem(T + "score_high_ready")
        mid_done = sem(T + "score_low_ready")
        st_psum = sem(T + "scores_transposed")
        sT_ready = sem(T + "scoresT_ready")
        spread = sem(T + "scores_spread")
        max_done = sem(T + "maxima_done")
        joined = sem(T + "maxima_joined")

        with nc.Block() as block:

            @block.gpsimd
            def _(pool):
                gather_rows(nc, pool, sem, T, dram.k, c.rec, stage, kg, gathered, prod_done)

            @block.vector
            def _(dve):
                def onehot(i, q):
                    r = (q + 2) % GPI
                    slots = bass.ds(i * SPI + 2 * q + 4, 2)
                    dve.wait_ge(tr_done, i * GPI + q + 1)
                    make(slots, r)

                def make(slots, r):
                    dst = c.rec[:, slots, 1].unsqueeze(2)
                    last = nc.vector.tensor_tensor(oh[:, 2 * r:2 * r + 2, :],
                                                   c.iota[:, 0:P].unsqueeze(1).broadcast_to([P, 2, P]),
                                                   dst.broadcast_to([P, 2, P]), ALU.is_equal)
                    if layer == 0:
                        kind = c.rec[:, slots, 2].unsqueeze(2)
                        last = nc.vector.tensor_tensor(ty[:, 2 * r:2 * r + 2, :],
                                                       c.iota[:, 0:NREL].unsqueeze(1).broadcast_to([P, 2, NREL]),
                                                       kind.broadcast_to([P, 2, NREL]), ALU.is_equal)
                    last.then_inc(oh_made, 1)

                def relation(i, q):
                    dve.wait_ge(qe_ready, i * GPI + q + 1)
                    dve.wait_ge(gathered[q], i * 32 + 32)
                    if layer == 0:
                        k = kg[:, 2 * q:2 * q + 2, :].rearrange("p s (h d) -> p s h d", h=H)
                        r = pR[:, :, :].unsqueeze(2).broadcast_to([P, 2, H, D // H])
                        nc.vector.tensor_tensor(k, k, r, ALU.add).then_inc(added, 1)

                def product(i, q):
                    if layer == 0:
                        dve.wait_ge(added, i * GPI + q + 2)
                    nc.vector.tensor_tensor(prod[:, q % 2, :], pQ[q % 2][:, :],
                                            kg[:, 2 * q:2 * q + 2, :].rearrange("p s d -> p (s d)"),
                                            ALU.mult).then_inc(prod_done, 1)

                def head_sums(i, q):
                    dve.wait_ge(prod_done, i * GPI + q + 5)
                    nc.vector.tensor_reduce(c.s[:, bass.ds((i * SPI + 2 * q) * H, 2 * H)],
                                            prod[:, q % 2, :].rearrange("p (g d) -> p g d", d=D // H),
                                            AX.X, ALU.add).then_inc(s_ready, 1)

                def low_part(i, q):
                    dve.wait_ge(hi_ready, i * GPI + q + 1)
                    nc.vector.tensor_tensor(
                        sp2[:, q % 2, :, HB:HB + H],
                        c.s[:, bass.ds((i * SPI + 2 * q) * H, 2 * H)].rearrange("p (s h) -> p s h", h=H),
                        sp2[:, q % 2, :, 0:H], ALU.subtract).then_inc(mid_done, 1)

                def maxima(i, q):
                    for hf in range(NH):
                        at = (i * GPI + q) * NH + hf
                        dve.wait_ge(spread, at + 1 + GPI * NH)
                        buf = pM[(q * NH + hf) % BM]
                        nc.vector.tensor_reduce(
                            mp[:, HA * hf:HA * hf + HA, bass.ds(i * GPI + q, 1)].rearrange("p h o -> p (h o)"),
                            buf[:, :].rearrange("p (h e) -> p h e", h=HA), AX.X, ALU.max).then_inc(max_done, 1)

                nc.vector.memset(sp2[:, :, :, :], 0.0).then_inc(cleared, 1)
                dve.sem_inc(prod_done, GPI)
                dve.sem_inc(max_done, 2)
                dve.sem_inc(added, 1)
                make(slice(0, 2), 0)
                make(slice(2, 4), 1)
                with dve.Fori(0, TURNS) as i:
                    relation(i, 0)
                    onehot(i, 0)
                    product(i, 0)
                    head_sums(i, 0)
                    relation(i, 1)
                    low_part(i, 0)
                    product(i, 1)
                    onehot(i, 1)
                    head_sums(i, 1)
                    for q in (2, 3):
                        relation(i, q)
                        low_part(i, q - 1)
                        product(i, q)
                        maxima(i, q - 2)
                        onehot(i, q)
                        head_sums(i, q)
                    maxima(i, 2)
                    low_part(i, 3)
                    maxima(i, 3)
                dve.wait_ge(max_done, NG * NH + 2)
                st = Steps(dve, joined)
                for h in range(H):
                    st(nc.vector.tensor_tensor_scan(fw[:, h, 0:NG], c.first[:, 0:NG], mp[:, h, 0:NG], -BIG,
                                                    ALU.add, ALU.max))
                st.sync()
                for h in range(H):
                    st(nc.vector.tensor_tensor_scan(mp[:, h, 0:NG][:, ::-1], c.final[:, 0:NG][:, ::-1],
                                                    fw[:, h, 0:NG][:, ::-1], -BIG, ALU.add, ALU.max))
                st.sync()
                joined_max = mp[:, 0:H, 0:NG].rearrange("p h g -> p g h")
                st.link(nc.vector.tensor_copy(c.m[:, :, 0, 0:H], joined_max))
                st.link(nc.vector.tensor_tensor(c.m[:, :, 1, 0:H], joined_max, c.m[:, :, 0, 0:H], ALU.subtract))

            @block.scalar
            def _(act):
                def copies(i, q, ahead=0):
                    t = i * GPI + q + ahead
                    hold(act, tr_done, t + 3)
                    hold(act, spread, (t + 1) * NH)
                    if layer == 0:
                        nc.scalar.activation(tyT[:, q % 2, :], pT[q % BT][0:NREL, 1, :], ACT.Copy)
                    nc.scalar.activation(ohTm[:, q, :], pT[q % BT][:, 0, :], ACT.Copy, bias=-1.0)
                    nc.scalar.activation(ohT[:, q, :], pT[q % BT][:, 0, :], ACT.Copy).then_inc(ohT_ready, 1)

                def high_part(i, q):
                    hold(act, s_ready, i * GPI + q + 1)
                    hold(act, st_psum, i * GPI + q + 1)
                    nc.scalar.activation(
                        sp2[:, q % 2, :, 0:H],
                        c.s[:, bass.ds((i * SPI + 2 * q) * H, 2 * H)].rearrange("p (s h) -> p s h", h=H),
                        ACT.Copy).then_inc(hi_ready, 1)

                def scoresT(i, q):
                    hold(act, st_psum, i * GPI + q + 3)
                    hold(act, spread, (i * GPI + q + 3) * NH)
                    nc.scalar.activation(sT[:, q % 2, :], pS[:, :], ACT.Copy).then_inc(sT_ready, 1)

                act.sem_inc(ohT_ready, 2)
                act.sem_inc(sT_ready, 2)
                act.wait_ge(cleared, 1)
                copies(0, 0)
                with act.Fori(0, TURNS) as i:
                    copies(i, 1)
                    high_part(i, 0)
                    copies(i, 2)
                    scoresT(i, 0)
                    high_part(i, 1)
                    copies(i, 3)
                    scoresT(i, 1)
                    high_part(i, 2)
                    copies(i, 0, GPI)
                    scoresT(i, 2)
                    high_part(i, 3)
                    scoresT(i, 3)

            @block.tensor
            def _(pe):
                def turn(i, q, ahead=0):
                    t = i * GPI + q + ahead
                    pe.wait_ge(oh_made, t + 1)
                    pe.wait_ge(ohT_ready, t + 3 - BT)
                    for k in range(2):
                        last = nc.tensor.transpose(pT[q % BT][:, 0, k * P:(k + 1) * P], oh[:, 2 * q + k, :], c.ident_b[:, :])
                        if layer == 0:
                            last = nc.tensor.transpose(pT[q % BT][0:NREL, 1, k * P:(k + 1) * P],
                                                       ty[:, 2 * q + k, :], c.ident_b[:, :])
                    last.then_inc(tr_done, 1)

                def q_of_edges(i, q, b):
                    t = i * GPI + q
                    pe.wait_ge(ohT_ready, t + 3)
                    pe.wait_ge(prod_done, t + 3)
                    for k in range(2):
                        for part in range(3):
                            last = nc.tensor.matmul(pQ[q % 2][:, k * D:(k + 1) * D], ohT[:, q, k * P:(k + 1) * P],
                                                    c.q[:, bass.ds(b, 1), part, :].rearrange("p o d -> p (o d)"),
                                                    start=part == 0, stop=part == 2)
                    if layer == 0:
                        pe.wait_ge(added, t + 1)
                        for k in range(2):
                            for part in range(3):
                                last = nc.tensor.matmul(pR[:, k, :],
                                                        tyT[:, q % 2, k * P:(k + 1) * P], c.rel[:, part, :],
                                                        start=part == 0, stop=part == 2)
                    last.then_inc(qe_ready, 1)

                def spread_scores(i, q):
                    t = i * GPI + q
                    pe.wait_ge(mid_done, t + 1)
                    pe.wait_ge(sT_ready, t + 2)
                    for k in range(2):
                        last = nc.tensor.transpose(pS[:, k * P:(k + 1) * P], sp2[:, q % 2, k, :],
                                                   c.ident_b[:, :])
                    last.then_inc(st_psum, 1)
                    pe.wait_ge(sT_ready, t + 3)
                    for hf in range(NH):
                        buf = pM[(q * NH + hf) % BM]
                        pe.wait_ge(max_done, t * NH + hf + 3 - BM)
                        for pair in range(2):
                            nc.tensor.matmul(buf[:, pair * 2 * GE:(pair + 1) * 2 * GE], c.big_b[:, :],
                                             ohTm[:, q, :].unsqueeze(1).broadcast_to([P, 2, GE]),
                                             start=True, stop=False)
                            for one in range(2):
                                h = HA * hf + 2 * pair + one
                                at = (2 * pair + one) * GE
                                last = nc.tensor.matmul(buf[:, at:at + GE], c.sel_b[0:2 * HB, h, :],
                                                        sT[:, q % 2, :], start=False, stop=one == 1)
                        last.then_inc(spread, 1)

                pe.sem_inc(tr_done, 2)
                pe.sem_inc(st_psum, 2)
                pe.sem_inc(spread, GPI * NH)
                turn(0, 0)
                with pe.Fori(0, TURNS) as i:
                    b = [pe.value_load(c.gb[0:1, bass.ds(i * GPI + q, 1)], min_val=0, max_val=TB - 1)
                         for q in range(GPI)]
                    q_of_edges(i, 0, b[0])
                    turn(i, 1)
                    q_of_edges(i, 1, b[1])
                    turn(i, 2)
                    spread_scores(i, 0)
                    q_of_edges(i, 2, b[2])
                    turn(i, 3)
                    q_of_edges(i, 3, b[3])
                    spread_scores(i, 1)
                    turn(i, 0, GPI)
                    spread_scores(i, 2)
                    spread_scores(i, 3)


def stage_aggregate(nc, c, sem, dram, layer):
    H = HA if layer == 0 else HB
    W = D + H
    T = f"L{layer}_sum_"
    with ExitStack() as ctx:
        def sb(name, shape, dt):
            return ctx.enter_context(nc.sbuf_tensor(T + name, shape, dt))

        def ps(name, shape, dt):
            return ctx.enter_context(nc.psum_tensor(T + name, shape, dt))

        vg = sb("vg", [P, SPI, D], F32)
        stage = [sb(f"stage{u}", [P, 4], I32) for u in range(2)]
        oh = [sb(f"oh{q}", [P, 2, P], F32) for q in range(GPI)]
        ohT = sb("ohT", [P, 2, GE], BF16)
        diff = sb("diff", [P, 2, 2, H], F32)
        rhs = sb("rhs", [P, 2, 2, W], F32)
        pT = [ps(f"pT{u}", [P, GE], F32) for u in range(2)]
        pE = [ps(f"pE{u}", [P, 2, H], F32) for u in range(2)]
        pA = [ps(f"pA{u}", [P, W], F32) for u in range(2)]

        gathered = [sem(T + f"v_gathered{q}") for q in range(GPI)]
        zeroed = sem(T + "sums_zeroed")
        oh_made = sem(T + "onehot_made")
        tr_done = sem(T + "onehot_transposed")
        ohT_ready = sem(T + "onehotT_ready")
        me_ready = sem(T + "maxima_of_edges_ready")
        diff_done = sem(T + "difference_done")
        exp_done = sem(T + "exp_done")
        v_done = sem(T + "weighted_v_done")
        agg_done = sem(T + "group_sum_done")
        acc_done = sem(T + "added_to_bucket")

        with nc.Block() as block:

            @block.gpsimd
            def _(pool):
                gather_rows(nc, pool, sem, T, dram.v, c.rec, stage, vg, gathered, v_done)

            @block.vector
            def _(dve):
                def make(slots, r):
                    nc.vector.tensor_tensor(oh[r][:, :, :], c.iota[:, 0:P].unsqueeze(1).broadcast_to([P, 2, P]),
                                            c.rec[:, slots, 1].unsqueeze(2).broadcast_to([P, 2, P]),
                                            ALU.is_equal).then_inc(oh_made, 1)

                def onehot(i, q):
                    dve.wait_ge(agg_done, i * GPI + q + 1)
                    make(bass.ds(i * SPI + 2 * q + 4, 2), (q + 2) % GPI)

                def difference(i, q):
                    t = i * GPI + q
                    dve.wait_ge(me_ready, t + 3)
                    dve.wait_ge(exp_done, t + 1)
                    nc.vector.tensor_tensor(
                        diff[:, q % 2, :, :],
                        c.s[:, bass.ds((i * SPI + 2 * q) * H, 2 * H)].rearrange("p (s h) -> p s h", h=H),
                        pE[q % 2][:, :, :], ALU.subtract).then_inc(diff_done, 1)

                def weighted(i, q):
                    t = i * GPI + q
                    dve.wait_ge(gathered[q], i * 32 + 32)
                    dve.wait_ge(exp_done, t + 3)
                    for k in range(2):
                        ins = nc.vector.tensor_tensor(
                            rhs[:, q % 2, k, 0:D].rearrange("p (h d) -> p h d", h=H),
                            vg[:, 2 * q + k, :].rearrange("p (h d) -> p h d", h=H),
                            rhs[:, q % 2, k, D:W].unsqueeze(2).broadcast_to([P, H, D // H]), ALU.mult)
                    ins.then_inc(v_done, 1)

                def accumulate(i, q, b):
                    t = i * GPI + q
                    dve.wait_ge(agg_done, t + 3)
                    dve.wait_ge(acc_done, t + 2)
                    row = c.acc[:, bass.ds(b, 1), 0:W].rearrange("p o w -> p (o w)")
                    nc.vector.tensor_tensor(row, pA[q % 2][:, :], row, ALU.add).then_inc(acc_done, 1)

                nc.vector.memset(c.acc[:, :, :], 0.0).then_inc(zeroed, 1)
                dve.wait_ge(zeroed, 1)
                dve.sem_inc(v_done, GPI)
                dve.sem_inc(diff_done, 2)
                dve.sem_inc(acc_done, 2)
                make(slice(0, 2), 0)
                make(slice(2, 4), 1)
                with dve.Fori(0, TURNS) as i:
                    b = [dve.value_load(c.gb[0:1, bass.ds(i * GPI + q, 1)], min_val=0, max_val=TB - 1)
                         for q in range(GPI)]
                    difference(i, 0)
                    onehot(i, 0)
                    weighted(i, 0)
                    for q in (1, 2, 3):
                        difference(i, q)
                        onehot(i, q)
                        if q > 1:
                            accumulate(i, q - 2, b[q - 2])
                        weighted(i, q)
                    accumulate(i, 2, b[2])
                    accumulate(i, 3, b[3])

            @block.scalar
            def _(act):
                def copy(i, q, ahead=0):
                    t = i * GPI + q + ahead
                    hold(act, tr_done, t + 1)
                    hold(act, me_ready, t + 1)
                    nc.scalar.activation(ohT[:, q % 2, :], pT[q % 2][:, :], ACT.Copy).then_inc(ohT_ready, 1)

                def exponent(i, q):
                    t = i * GPI + q
                    hold(act, diff_done, t + 3)
                    hold(act, agg_done, t + 1)
                    nc.scalar.activation(rhs[:, q % 2, :, D:W], diff[:, q % 2, :, :], ACT.Exp).then_inc(exp_done, 1)

                act.sem_inc(ohT_ready, 2)
                act.sem_inc(exp_done, 2)
                copy(0, 0)
                with act.Fori(0, TURNS) as i:
                    for q in range(GPI):
                        exponent(i, q)
                        copy(i, (q + 1) % GPI, GPI if q == GPI - 1 else 0)

            @block.tensor
            def _(pe):
                def turn(i, q, ahead=0):
                    t = i * GPI + q + ahead
                    pe.wait_ge(oh_made, t + 1)
                    pe.wait_ge(ohT_ready, t + 1)
                    for k in range(2):
                        last = nc.tensor.transpose(pT[q % 2][:, k * P:(k + 1) * P], oh[q][:, k, :], c.ident[:, :])
                    last.then_inc(tr_done, 1)

                def maxima_of_edges(i, q):
                    t = i * GPI + q
                    pe.wait_ge(ohT_ready, t + 3)
                    pe.wait_ge(diff_done, t + 1)
                    for k in range(2):
                        for part in range(2):
                            last = nc.tensor.matmul(pE[q % 2][:, k, :], ohT[:, q % 2, k * P:(k + 1) * P],
                                                    c.m[:, bass.ds(t, 1), part, 0:H].rearrange("p o h -> p (o h)"),
                                                    start=part == 0, stop=part == 1)
                    last.then_inc(me_ready, 1)

                def group_sum(i, q):
                    t = i * GPI + q
                    pe.wait_ge(v_done, t + 5)
                    pe.wait_ge(acc_done, t + 1)
                    for k in range(2):
                        last = nc.tensor.matmul(pA[q % 2][:, :], oh[q][:, k, :], rhs[:, q % 2, k, :],
                                                start=k == 0, stop=k == 1)
                    last.then_inc(agg_done, 1)

                pe.sem_inc(me_ready, 2)
                pe.sem_inc(agg_done, 2)
                turn(0, 0)
                with pe.Fori(0, TURNS) as i:
                    maxima_of_edges(i, 0)
                    turn(i, 1)
                    maxima_of_edges(i, 1)
                    turn(i, 2)
                    group_sum(i, 0)
                    maxima_of_edges(i, 2)
                    turn(i, 3)
                    group_sum(i, 1)
                    maxima_of_edges(i, 3)
                    group_sum(i, 2)
                    turn(i, 0, GPI)
                    group_sum(i, 3)


def stage_output(nc, c, sem, dram, weights, layer):
    H = HA if layer == 0 else HB
    T = f"L{layer}_out_"
    Wo, bo, gamma, beta = weights
    with ExitStack() as ctx:
        def sb(name, shape, dt):
            return ctx.enter_context(nc.sbuf_tensor(T + name, shape, dt))

        def ps(name, shape, dt):
            return ctx.enter_context(nc.psum_tensor(T + name, shape, dt))

        w = sb("wo", [P, C2, D], F32)
        b = sb("bo", [P, D], F32)
        z = sb("z", [P, TB, H], F32)
        empty = sb("empty", [P, TB, H], F32)
        msg = sb("msg", [P, 2, D], F32)
        mT = [sb(f"mT{u}", [P, C2, P], F32) for u in range(2)]
        hn = sb("hn", [P, 2, D], F32)
        part = sb("part", [P, 2, D], F32)
        if layer == 0:
            vt = sb("vt", [P, 2, D], F32)
            gb = sb("gamma_beta", [P, 2, D], F32)
            y = sb("y", [P, TB, D], F32)
        pT = [ps(f"pT{u}", [P, D], F32) for u in range(2)]
        pO = [ps(f"pO{u}", [P, D], F32) for u in range(2)]

        loaded = sem(T + "w_loaded")
        steps = sem(T + "dve_steps")
        v_loaded = [sem(T + f"v_loaded{u}") for u in range(2)]
        scaled = sem(T + "scaled")
        msg_done = sem(T + "messages_done")
        mT_psum = sem(T + "messages_transposed")
        mT_ready = sem(T + "messagesT_ready")
        hn_ready = sem(T + "hn_ready")
        out_psum = sem(T + "out_psum")
        projected = sem(T + "projected")
        out_done = sem(T + "out_done")
        norm = NormSemaphores(sem, T)
        scaled_y = sem(T + "normalised")
        affine = sem(T + "affine")

        with nc.Block() as block:

            @block.sync
            def _(sp):
                sp.dma_start(w[:, :, :], Wo.rearrange("(c p) n -> p c n", p=P)).then_inc(loaded, 16)
                sp.dma_start(b[:, :], bo.rearrange("(o n) -> o n", o=1).broadcast_to([P, D])).then_inc(loaded, 16)
                if layer == 0:
                    for k, a in enumerate((gamma, beta)):
                        sp.dma_start(gb[:, k, :],
                                     a.rearrange("(o n) -> o n", o=1).broadcast_to([P, D])).then_inc(loaded, 16)
                    with sp.Fori(0, TB // 2) as i:
                        for u in range(2):
                            hold(sp, msg_done, i * 2 + u + 1)
                            sp.dma_start(vt[:, u, :], dram.v[bass.ds((i * 2 + u) * P, P), :]).then_inc(v_loaded[u], 16)

            @block.vector
            def _(dve):
                st = Steps(dve, steps)
                sums = c.acc[:, :, D:D + H]
                st(nc.vector.tensor_scalar(empty[:, :, :], sums, 0.0, None, ALU.is_equal))
                st.link(nc.vector.tensor_scalar(z[:, :, :], sums, 1e-30, None, ALU.max))
                st.link(nc.vector.reciprocal(z[:, :, :], z[:, :, :]))
                dve.wait_ge(loaded, 64 if layer == 0 else 32)
                dve.sem_inc(msg_done, 2)
                with dve.Fori(0, TB // 2) as i:
                    for u in range(2):
                        t = i * 2 + u
                        def heads(a):
                            return a.rearrange("p (h d) -> p h d", h=H)
                        def of_tile(a):
                            return a[:, bass.ds(t, 1), :].rearrange("p o h -> p (o h)").unsqueeze(2).broadcast_to(
                                [P, H, D // H])
                        acc = c.acc[:, bass.ds(t, 1), 0:D].rearrange("p o d -> p (o d)")
                        first = nc.vector.tensor_tensor(heads(msg[:, u, :]), heads(acc), of_tile(z), ALU.mult)
                        if layer == 0:
                            first.then_inc(scaled, 1)
                            dve.wait_ge(v_loaded[u], i * 16 + 16)
                            nc.vector.tensor_tensor(heads(vt[:, u, :]), heads(vt[:, u, :]), of_tile(empty),
                                                    ALU.mult).then_inc(scaled, 1)
                            dve.wait_ge(scaled, 2 * t + 2)
                            first = nc.vector.tensor_tensor(msg[:, u, :], msg[:, u, :], vt[:, u, :], ALU.add)
                        first.then_inc(msg_done, 1)
                    for u in range(2):
                        t = i * 2 + u
                        dve.wait_ge(out_psum, t + 1)
                        nc.vector.tensor_tensor(part[:, u, :], pO[u][:, :], b[:, :], ALU.add).then_inc(projected, 1)
                        dve.wait_ge(projected, t + 1)
                        if layer == 0:
                            dve.wait_ge(hn_ready, t + 1)
                            nc.vector.tensor_tensor(y[:, t, :], part[:, u, :], hn[:, u, :],
                                                    ALU.add).then_inc(out_done, 1)
                        else:
                            nc.vector.tensor_tensor(c.x[:, t, :], part[:, u, :], c.x[:, t, :],
                                                    ALU.add).then_inc(out_done, 1)
                dve.wait_ge(out_done, TB)
                if layer == 0:
                    norm_vector(nc, dve, c, norm, y)
                    with dve.Fori(0, NT) as t:
                        dve.wait_ge(scaled_y, t + 1)
                        nc.vector.tensor_tensor(y[:, t, :], y[:, t, :], gb[:, 0, :], ALU.mult).then_inc(affine, 1)
                        nc.vector.tensor_tensor(c.x[:, t, :], c.x[:, t, :], gb[:, 1, :], ALU.add).then_inc(affine, 1)
                        dve.wait_ge(affine, 3 * t + 2)
                        nc.vector.tensor_tensor(c.x[:, t, :], c.x[:, t, :], y[:, t, :], ALU.add).then_inc(affine, 1)
                    dve.wait_ge(affine, 3 * NT)

            @block.scalar
            def _(act):
                with act.Fori(0, TB // 2) as i:
                    for u in range(2):
                        t = i * 2 + u
                        hold(act, mT_psum, t + 1)
                        nc.scalar.activation(mT[u][:, :, :].rearrange("p c n -> p (c n)"), pT[u][:, :],
                                             ACT.Copy).then_inc(mT_ready, 1)
                        if layer == 0:
                            nc.scalar.activation(hn[:, u, :], c.x[:, t, :], ACT.Identity,
                                                 bias=c.shift[:, bass.ds(t, 1)],
                                                 scale=c.rstd[:, bass.ds(t, 1)]).then_inc(hn_ready, 1)
                if layer == 0:
                    norm_scalar(nc, act, norm, c)
                    act.wait_ge(norm.ready, 1)
                    with act.Fori(0, NT) as t:
                        nc.scalar.activation(y[:, t, :], y[:, t, :], ACT.Identity, bias=c.shift[:, bass.ds(t, 1)],
                                             scale=c.rstd[:, bass.ds(t, 1)]).then_inc(scaled_y, 1)

            @block.tensor
            def _(pe):
                pe.wait_ge(loaded, 64 if layer == 0 else 32)
                with pe.Fori(0, TB // 2) as i:
                    for u in range(2):
                        t = i * 2 + u
                        pe.wait_ge(msg_done, t + 3)
                        for k in range(C2):
                            last = nc.tensor.transpose(pT[u][:, k * P:(k + 1) * P], msg[:, u, k * P:(k + 1) * P],
                                                       c.ident[:, :])
                        last.then_inc(mT_psum, 1)
                    for u in range(2):
                        t = i * 2 + u
                        pe.wait_ge(mT_ready, t + 1)
                        for k in range(C2):
                            last = nc.tensor.matmul(pO[u][:, :], mT[u][:, k, :], w[:, k, :], start=k == 0,
                                                    stop=k == C2 - 1)
                        last.then_inc(out_psum, 1)


def stage_gate(nc, c, sem, dram, weights):
    T = "gate_"
    EX = EXPERTS
    gate_w, gate_b, b1 = weights
    with ExitStack() as ctx:
        def sb(name, shape, dt):
            return ctx.enter_context(nc.sbuf_tensor(T + name, shape, dt))

        def ps(name, shape, dt):
            return ctx.enter_context(nc.psum_tensor(T + name, shape, dt))

        h = sb("h", [P, TB, D], F32)
        hn = sb("hn", [P, 2, D], F32)
        gw = sb("gw", [P, C2, EX], F32)
        gb = sb("gb", [P, EX], F32)
        b1_rows = sb("b1_rows", [EX * FC, P], F32)
        hT = [sb(f"hT{u}", [P, C2, P], F32) for u in range(2)]
        zeros = sb("zeros", [P, 8 * D], F32)
        lg = sb("logits", [P, TB, EX], F32)
        one = sb("one_hot", [P, TB, EX], F32)
        tmp = sb("tmp", [P, TB, EX], F32)
        before = sb("before_tile", [P, EX, TB], F32)
        col = sb("columns", [P, 8, TB], F32)
        pT = [ps(f"pT{u}", [P, D], F32) for u in range(2)]
        pG = ps("pG", [P, TB, EX], F32)
        pC = ps("pC", [P, TB, EX], F32)
        pN = ps("pN", [P, TB, EX], F32)
        pB = ps("pB", [P, EX * FC], F32)
        loaded = sem(T + "w_loaded")
        zeroed = sem(T + "zeros_made")
        cleared = sem(T + "buffers_cleared")
        norm = NormSemaphores(sem, T)
        hn_ready = sem(T + "h_ready")
        hT_psum = sem(T + "h_transposed")
        hT_ready = sem(T + "hT_ready")
        logits_done = sem(T + "logits_done")
        b1_psum = sem(T + "b1_transposed")
        steps = sem(T + "dve_steps")
        shifted = sem(T + "logits_shifted")
        exp_done = sem(T + "exp_done")
        chosen = sem(T + "expert_chosen")
        counted = sem(T + "counted")
        placed = sem(T + "placed")
        sent = sem(T + "h_sent")

        with nc.Block() as block:

            @block.sync
            def _(sp):
                sp.dma_start(gw[:, :, :], gate_w.rearrange("(c p) e -> p c e", p=P)).then_inc(loaded, 16)
                sp.dma_start(gb[:, :], gate_b.rearrange("(o n) -> o n", o=1).broadcast_to([P, EX])).then_inc(loaded, 16)
                sp.dma_start(b1_rows[:, :], b1.rearrange("e (f p) -> (e f) p", p=P)).then_inc(loaded, 16)
                sp.wait_ge(zeroed, 1)
                for k in range(EX * CAPW // (8 * P)):
                    sp.dma_start(dram.buf[k * 8 * P:(k + 1) * 8 * P, :].rearrange("(p r) d -> p (r d)", r=8),
                                 zeros[:, :]).then_inc(cleared, 16)

            @block.gpsimd
            def _(pool):
                nc.gpsimd.memset(zeros[:, :], 0.0).then_inc(zeroed, 1)
                pool.wait_ge(placed, 1)
                pool.wait_ge(cleared, EX * CAPW // (8 * P) * 16)
                for t in range(NT):
                    nc.gpsimd.indirect_dma_start(out=dram.buf, out_offset=bass.IndirectOffsetOnAxis(
                        ap=c.place[:, 0, t:t + 1], axis=0), in_=h[:, t, :], in_offset=None).then_inc(sent, 16)
                pool.wait_ge(sent, NT * 16)

            @block.vector
            def _(dve):
                norm_vector(nc, dve, c, norm, c.x)
                st = Steps(dve, steps)
                shape = [P, TB, EX]
                def each(a):
                    return a.unsqueeze(2).broadcast_to(shape)
                numbers = c.iota[:, 0:EX].unsqueeze(1).broadcast_to(shape)
                dve.wait_ge(loaded, 48)
                dve.wait_ge(b1_psum, 1)
                st(nc.vector.tensor_copy(c.b1T[:, :], pB[:, :]))
                dve.wait_ge(logits_done, TB + 1)
                st.link(nc.vector.tensor_tensor(lg[:, :, :], pG[:, :, :], gb[:, :].unsqueeze(1).broadcast_to(shape), ALU.add))
                st.link(nc.vector.tensor_reduce(col[:, 0, :], lg[:, :, :], AX.X, ALU.max))
                nc.vector.tensor_tensor(lg[:, :, :], lg[:, :, :], each(col[:, 0, :]), ALU.subtract).then_inc(shifted, 1)
                dve.wait_ge(exp_done, 1)
                st.link(nc.vector.tensor_reduce(col[:, 1, :], lg[:, :, :], AX.X, ALU.add))
                st(nc.vector.reciprocal(col[:, 2, :], col[:, 1, :]))
                st(nc.vector.tensor_scalar(one[:, :, :], lg[:, :, :], 1.0, None, ALU.is_ge))
                st.link(nc.vector.tensor_scalar(tmp[:, :, :], numbers, -1.0, float(EX), ALU.mult, ALU.add))
                st.link(nc.vector.tensor_tensor(tmp[:, :, :], tmp[:, :, :], one[:, :, :], ALU.mult))
                st.link(nc.vector.tensor_reduce(col[:, 3, :], tmp[:, :, :], AX.X, ALU.max))
                nc.vector.tensor_tensor(one[:, :, :], tmp[:, :, :], each(col[:, 3, :]), ALU.is_equal).then_inc(chosen, 1)
                dve.wait_ge(counted, 2)
                dve.wait_ge(chosen, 1)
                for e in range(EX):
                    st(nc.vector.tensor_tensor_scan(before[:, e, :], pN[:, :, e], c.zero[:, 0:TB], 0.0, ALU.add,
                                                    ALU.add))
                st.sync()
                st.link(nc.vector.tensor_tensor(tmp[:, :, :], before[:, :, :].rearrange("p e t -> p t e"),
                                                pN[:, :, :], ALU.subtract))
                st.link(nc.vector.tensor_tensor(tmp[:, :, :], tmp[:, :, :], pC[:, :, :], ALU.add))
                st.link(nc.vector.tensor_tensor(tmp[:, :, :], tmp[:, :, :], one[:, :, :], ALU.mult))
                st.link(nc.vector.tensor_reduce(col[:, 4, :], tmp[:, :, :], AX.X, ALU.add))
                st(nc.vector.tensor_scalar(col[:, 0, :], col[:, 3, :], -float(CAPW), float(CAPW * EX), ALU.mult, ALU.add))
                st(nc.vector.tensor_scalar(col[:, 1, :], col[:, 4, :], float(CAP), None, ALU.is_le))
                st(nc.vector.tensor_scalar(col[:, 5, :], col[:, 4, :], float(CAP), -1.0, ALU.min, ALU.add))
                st.sync()
                st(nc.vector.tensor_tensor(c.weight[:, :], col[:, 2, :], col[:, 1, :], ALU.mult))
                st.link(nc.vector.tensor_tensor(col[:, 5, :], col[:, 5, :], col[:, 0, :], ALU.add))
                st(nc.vector.tensor_copy(c.place[:, 1, :], col[:, 5, :]))
                st.link(nc.vector.tensor_tensor(col[:, 6, :], col[:, 5, :], c.spare[:, :], ALU.subtract))
                st.link(nc.vector.tensor_tensor(col[:, 6, :], col[:, 6, :], col[:, 1, :], ALU.mult))
                st.link(nc.vector.tensor_tensor(col[:, 7, :], col[:, 6, :], c.spare[:, :], ALU.add))
                nc.vector.tensor_copy(c.place[:, 0, :], col[:, 7, :]).then_inc(placed, 1)

            @block.scalar
            def _(act):
                norm_scalar(nc, act, norm, c)
                act.wait_ge(norm.ready, 1)
                with act.Fori(0, TB // 2) as i:
                    for u in range(2):
                        t = i * 2 + u
                        nc.scalar.activation(h[:, t, :], c.x[:, t, :], ACT.Identity, bias=c.shift[:, bass.ds(t, 1)],
                                             scale=c.rstd[:, bass.ds(t, 1)])
                        nc.scalar.activation(hn[:, u, :], c.x[:, t, :], ACT.Identity, bias=c.shift[:, bass.ds(t, 1)],
                                             scale=c.rstd[:, bass.ds(t, 1)]).then_inc(hn_ready, 1)
                        hold(act, hT_psum, t + 1)
                        hold(act, logits_done, t + 1)
                        nc.scalar.activation(hT[u][:, :, :].rearrange("p c n -> p (c n)"), pT[u][:, :],
                                             ACT.Copy).then_inc(hT_ready, 1)
                act.wait_ge(shifted, 1)
                nc.scalar.activation(lg[:, :, :], lg[:, :, :], ACT.Exp).then_inc(exp_done, 1)

            @block.tensor
            def _(pe):
                pe.wait_ge(loaded, 48)
                nc.tensor.transpose(pB[:, :], b1_rows[:, :], c.ident[0:EX * FC, 0:EX * FC]).then_inc(b1_psum, 1)
                pe.sem_inc(logits_done, 1)
                with pe.Fori(0, TB // 2) as i:
                    for u in range(2):
                        t = i * 2 + u
                        pe.wait_ge(hn_ready, t + 1)
                        for k in range(C2):
                            last = nc.tensor.transpose(pT[u][:, k * P:(k + 1) * P],
                                                       hn[:, u, k * P:(k + 1) * P],
                                                       c.ident[:, :])
                        last.then_inc(hT_psum, 1)
                        pe.wait_ge(hT_ready, t + 1)
                        for k in range(C2):
                            last = nc.tensor.matmul(pG[:, bass.ds(t, 1), :].rearrange("p o e -> p (o e)"),
                                                    hT[u][:, k, :], gw[:, k, :], start=k == 0, stop=k == C2 - 1)
                        last.then_inc(logits_done, 1)
                pe.wait_ge(chosen, 1)
                for out, m in ((pC, c.upto), (pN, c.ones)):
                    nc.tensor.matmul(out[:, :, :].rearrange("p t e -> p (t e)"), m[:, :],
                                     one[:, :, :].rearrange("p t e -> p (t e)"), start=True,
                                     stop=True).then_inc(counted, 1)


def stage_experts(nc, c, sem, dram, weights):
    T = "experts_"
    EX = EXPERTS
    w1_d, w2_d, b2_d = weights
    A = CAPW // P
    with ExitStack() as ctx:
        def sb(name, shape, dt):
            return ctx.enter_context(nc.sbuf_tensor(T + name, shape, dt))

        def ps(name, shape, dt):
            return ctx.enter_context(nc.psum_tensor(T + name, shape, dt))

        w1 = [sb(f"w1_{u}", [P, C2, FF], F32) for u in range(2)]
        w2 = [sb(f"w2_{u}", [P, FC, D], F32) for u in range(2)]
        b2 = [sb(f"b2_{u}", [P, D], F32) for u in range(2)]
        xe = [sb(f"x_{u}", [P, A, D], F32) for u in range(2)]
        xT = sb("xT", [P, C2, CAPW], F32)
        hT = sb("hT", [P, FC, CAPW], F32)
        y = [sb(f"y_{u}", [P, A, D], F32) for u in range(2)]
        pX = [ps(f"pX{k}", [P, CAPW], F32) for k in range(C2)]
        pH = [ps(f"pH{u}", [P, CAPW], F32) for u in range(2)]
        pY = [ps(f"pY{u}", [P, D], F32) for u in range(2)]
        loaded = [sem(T + f"loaded{u}") for u in range(2)]
        x_psum = sem(T + "x_transposed")
        xT_ready = sem(T + "xT_ready")
        h_psum = sem(T + "hidden_psum")
        relu_done = sem(T + "relu_done")
        y_psum = sem(T + "y_psum")
        y_done = sem(T + "y_done")
        stored = [sem(T + f"stored{u}") for u in range(2)]

        with nc.Block() as block:

            @block.sync
            def _(sp):
                def load(e, u):
                    sp.dma_start(w1[u][:, :, :],
                                 w1_d[bass.ds(e, 1), :, :].rearrange("o (c p) f -> p (o c) f", p=P)).then_inc(loaded[u], 16)
                    sp.dma_start(w2[u][:, :, :],
                                 w2_d[bass.ds(e, 1), :, :].rearrange("o (f p) d -> p (o f) d", p=P)).then_inc(loaded[u], 16)
                    sp.dma_start(b2[u][:, :], b2_d[bass.ds(e, 1), :].broadcast_to([P, D])).then_inc(loaded[u], 16)
                    sp.dma_start(xe[u][:, :, :], dram.buf[bass.ds(e * CAPW, CAPW), :].rearrange(
                        "(a p) d -> p a d", p=P)).then_inc(loaded[u], 16)

                def store(e, u, n):
                    hold(sp, y_done, n + 2)
                    sp.dma_start(dram.ybuf[bass.ds(e * CAPW, CAPW), :].rearrange("(a p) d -> p a d", p=P),
                                 y[u][:, :, :]).then_inc(stored[u], 16)

                load(0, 0)
                load(1, 1)
                with sp.Fori(0, EX // 2 - 1) as i:
                    for u in range(2):
                        store(i * 2 + u, u, (i * 2 + u + 1) * A)
                        load(i * 2 + u + 2, u)
                for u in range(2):
                    sp.wait_ge(y_done, (EX - 2 + u + 1) * A + 2)
                    sp.dma_start(dram.ybuf[(EX - 2 + u) * CAPW:(EX - 1 + u) * CAPW, :].rearrange("(a p) d -> p a d", p=P),
                                 y[u][:, :, :]).then_inc(stored[u], 16)
                for u in range(2):
                    sp.wait_ge(stored[u], EX // 2 * 16)

            @block.tensor
            def _(pe):
                with pe.Fori(0, EX // 2) as i:
                    for u in range(2):
                        e = i * 2 + u
                        pe.wait_ge(loaded[u], (i + 1) * 64)
                        for k in range(C2):
                            for a in range(A):
                                last = nc.tensor.transpose(pX[k][:, a * P:(a + 1) * P],
                                                           xe[u][:, a, k * P:(k + 1) * P], c.ident[:, :])
                        last.then_inc(x_psum, 1)
                        pe.wait_ge(xT_ready, e + 1)
                        for f in range(FC):
                            pe.wait_ge(relu_done, e * FC + f + 1)
                            for k in range(C2):
                                last = nc.tensor.matmul(pH[f % 2][:, :], w1[u][:, k, f * P:(f + 1) * P], xT[:, k, :],
                                                        start=k == 0, stop=k == C2 - 1)
                            last.then_inc(h_psum, 1)
                        pe.wait_ge(relu_done, e * FC + FC + 2)
                        for a in range(A):
                            pe.wait_ge(y_done, e * A + a + 1)
                            for f in range(FC):
                                last = nc.tensor.matmul(pY[a % 2][:, :], hT[:, f, a * P:(a + 1) * P], w2[u][:, f, :],
                                                        start=f == 0, stop=f == FC - 1)
                            last.then_inc(y_psum, 1)

            @block.scalar
            def _(act):
                act.sem_inc(relu_done, 2)
                with act.Fori(0, EX // 2) as i:
                    for u in range(2):
                        e = i * 2 + u
                        hold(act, x_psum, e + 1)
                        nc.scalar.activation(xT[:, 0, :], pX[0][:, :], ACT.Copy)
                        nc.scalar.activation(xT[:, 1, :], pX[1][:, :], ACT.Copy).then_inc(xT_ready, 1)
                        for f in range(FC):
                            hold(act, h_psum, e * FC + f + 1)
                            nc.scalar.activation(hT[:, f, :], pH[f % 2][:, :], ACT.Relu,
                                                 bias=c.b1T[:, bass.ds(e * FC + f, 1)]).then_inc(relu_done, 1)

            @block.vector
            def _(dve):
                dve.sem_inc(y_done, 2)
                def pair(i, first=False):
                    for u in range(2):
                        e = i * 2 + u
                        if not first:
                            dve.wait_ge(stored[u], i * 16)
                        for a in range(A):
                            dve.wait_ge(y_psum, e * A + a + 1)
                            nc.vector.tensor_tensor(y[u][:, a, :], pY[a % 2][:, :], b2[u][:, :],
                                                    ALU.add).then_inc(y_done, 1)

                pair(0, first=True)
                with dve.Fori(1, EX // 2) as i:
                    pair(i)


def stage_combine(nc, c, sem, dram):
    T = "combine_"
    RING = 5
    LIMIT = 3.4028234e38
    with ExitStack() as ctx:
        def sb(name, shape, dt):
            return ctx.enter_context(nc.sbuf_tensor(T + name, shape, dt))

        y = sb("y", [P, RING, D], F32)
        ok = sb("ok", [P, RING, D], I32)
        clean = sb("clean", [P, RING, D], F32)
        limit = sb("limit", [P, 2, D], F32)
        got = [sem(T + f"got{r}") for r in range(RING)]
        made = sem(T + "limits_made")
        weighted = sem(T + "weighted")
        steps = sem(T + "dve_steps")
        used = sem(T + "used")
        with nc.Block() as block:

            @block.gpsimd
            def _(pool):
                for t in range(NT):
                    if t >= RING:
                        pool.wait_ge(used, t - RING + 1)
                    nc.gpsimd.indirect_dma_start(
                        out=y[:, t % RING, :], out_offset=None, in_=dram.ybuf,
                        in_offset=bass.IndirectOffsetOnAxis(ap=c.place[:, 1, t:t + 1], axis=0)).then_inc(got[t % RING], 16)

            @block.scalar
            def _(act):
                for t in range(NT):
                    act.wait_ge(got[t % RING], (t // RING + 1) * 16)
                    nc.scalar.activation(y[:, t % RING, :], y[:, t % RING, :], ACT.Copy,
                                         scale=c.weight[:, t:t + 1]).then_inc(weighted, 1)

            @block.vector
            def _(dve):
                nc.vector.memset(limit[:, 0, :], 1e4).then_inc(made, 1)
                nc.vector.memset(limit[:, 1, :], -1e4).then_inc(made, 1)
                dve.wait_ge(made, 2)
                st = Steps(dve, steps)
                for t in range(NT):
                    r = t % RING
                    dve.wait_ge(weighted, t + 1)
                    st(nc.vector.memset(clean[:, r, :], 0.0))
                    st.link(nc.vector.tensor_tensor(ok[:, r, :], y[:, r, :], y[:, r, :], ALU.is_equal))
                    st.link(nc.vector.copy_predicated(clean[:, r, :], ok[:, r, :], y[:, r, :]))
                    st.link(nc.vector.tensor_scalar(ok[:, r, :], clean[:, r, :], LIMIT, None, ALU.is_gt))
                    st.link(nc.vector.copy_predicated(clean[:, r, :], ok[:, r, :], limit[:, 0, :]))
                    st.link(nc.vector.tensor_scalar(ok[:, r, :], clean[:, r, :], -LIMIT, None, ALU.is_lt))
                    st.link(nc.vector.copy_predicated(clean[:, r, :], ok[:, r, :], limit[:, 1, :]))
                    nc.vector.tensor_tensor(c.x[:, t, :], c.x[:, t, :], clean[:, r, :], ALU.add).then_inc(used, 1)
                dve.wait_ge(used, NT)


KEEP = N // 2 - 1
G4 = 4 * P


def stage_last(nc, c, sem, dram, weights, out):
    T = "last_"
    wr_d, br_d, w1_d, b1_d, w2_d, b2_d = weights
    NP = TB * P
    with ExitStack() as ctx:
        def sb(name, shape, dt):
            return ctx.enter_context(nc.sbuf_tensor(T + name, shape, dt))

        def ps(name, shape, dt):
            return ctx.enter_context(nc.psum_tensor(T + name, shape, dt))

        h = [sb(f"h{u}", [P, D], F32) for u in range(2)]
        hT = sb("hT", [P, C2, NP], F32)
        wr = sb("wr", [P, C2], F32)
        br = sb("br", [P, 1], F32)
        w1 = sb("w1", [P, C2, FF], F32)
        w2 = sb("w2", [P, FC, D], F32)
        b1_rows = sb("b1_rows", [FC, P], F32)
        b1T = sb("b1T", [P, FC], F32)
        b2 = sb("b2", [1, D], F32)
        gT = sb("gT", [P, FC, G4], F32)
        y = sb("y", [P, TB, D], F32)
        wcol = sb("wcol", [P, TB], F32)
        wrow = sb("wrow", [TB, P], F32)
        wall = sb("wall", [P, N], F32)
        earlier = sb("earlier", [P, 2 * NP], BF16)
        flags = sb("flags", [P, N], F32)
        rank = sb("rank", [P, 2, TB], F32)
        coef = sb("coef", [P, 3, TB], F32)
        pT = [ps(f"pT{u}", [P, D], F32) for u in range(2)]
        pW = ps("pW", [P, TB], F32)
        pS = ps("pS", [P, P], F32)
        pH = [ps(f"pH{u}", [P, G4], F32) for u in range(2)]
        pY = [ps(f"pY{u}", [P, D], F32) for u in range(2)]
        loaded = sem(T + "w_loaded")
        norm = NormSemaphores(sem, T)
        mask_made = sem(T + "mask_made")
        h_ready = sem(T + "h_ready")
        h_psum = sem(T + "h_transposed")
        hT_ready = sem(T + "hT_ready")
        h_added = sem(T + "h_added")
        w_psum = sem(T + "w_psum")
        w_ready = sem(T + "w_ready")
        row_psum = sem(T + "w_transposed")
        row_ready = sem(T + "w_row_ready")
        b1_ready = sem(T + "b1_ready")
        row_out = sem(T + "w_row_stored")
        row_in = sem(T + "w_row_loaded")
        steps = sem(T + "dve_steps")
        hid_psum = sem(T + "hidden_psum")
        gelu_done = sem(T + "gelu_done")
        y_psum = sem(T + "y_psum")
        y_ready = sem(T + "y_ready")
        final = sem(T + "final")
        stored = sem(T + "stored")
        turns = [(i, 4) for i in range(NT // 4)] + [(NT // 4, NT % 4)]

        with nc.Block() as block:

            @block.sync
            def _(sp):
                sp.dma_start(wr[:, :], wr_d.rearrange("(c p) o -> p (c o)", p=P),
                             allow_slow_non_contiguous=True).then_inc(loaded, 16)
                sp.dma_start(br[:, :], br_d.rearrange("(o n) -> o n", o=1).broadcast_to([P, 1])).then_inc(loaded, 16)
                sp.dma_start(b1_rows[:, :], b1_d.rearrange("(f p) -> f p", p=P)).then_inc(loaded, 16)
                sp.dma_start(b2[:, :], b2_d.rearrange("(o n) -> o n", o=1)).then_inc(loaded, 16)
                sp.dma_start(w1[:, :, :], w1_d.rearrange("(c p) f -> p c f", p=P)).then_inc(loaded, 16)
                sp.dma_start(w2[:, :, :], w2_d.rearrange("(f p) d -> p f d", p=P)).then_inc(loaded, 16)
                sp.wait_ge(row_ready, 1)
                sp.dma_start(dram.wrow.rearrange("(t p) -> t p", p=P), wrow[:, :]).then_inc(row_out, 16)
                sp.wait_ge(row_out, 16)
                sp.dma_start(wall[:, :], dram.wrow[0:N].rearrange("(o n) -> o n", o=1).broadcast_to([P, N])).then_inc(row_in, 16)
                for t in range(0, NT - 1, 4):
                    sp.wait_ge(final, t + 4)
                    sp.dma_start(out[t * P:(t + 4) * P, :].rearrange("(t p) d -> p t d", p=P),
                                 y[:, t:t + 4, :]).then_inc(stored, 16)
                sp.wait_ge(final, NT)
                sp.dma_start(out[(NT - 1) * P:N, :], y[0:LAST, NT - 1, :]).then_inc(stored, 16)
                sp.wait_ge(stored, (NT - 1) // 4 * 16 + 16)

            @block.gpsimd
            def _(pool):
                nc.gpsimd.memset(earlier[:, :], 1.0).then_inc(mask_made, 1)
                pool.wait_ge(mask_made, 1)
                nc.gpsimd.affine_select(out=earlier[:, :], in_=earlier[:, :], compare_op=ALU.is_gt, fill=0.0,
                                        base=NP, pattern=[[-1, 2 * NP]], channel_multiplier=1).then_inc(mask_made, 1)
                with pool.Fori(0, TB // 2) as i:
                    for u in range(2):
                        t = i * 2 + u
                        hold(pool, h_ready, t + 1)
                        nc.gpsimd.tensor_tensor(c.x[:, t, :], c.x[:, t, :], h[u][:, :], ALU.add).then_inc(h_added, 1)

            @block.vector
            def _(dve):
                dve.sem_inc(h_added, 2)
                norm_vector(nc, dve, c, norm, c.x)
                st = Steps(dve, steps)
                dve.wait_ge(w_psum, TB)
                nc.vector.tensor_scalar(wcol[:, :], pW[:, :], br[:, 0:1], None, ALU.add).then_inc(w_ready, 1)
                dve.wait_ge(row_psum, 1)
                nc.vector.tensor_copy(wrow[:, :], pS[0:TB, :]).then_inc(row_ready, 1)
                dve.wait_ge(row_in, 16)
                dve.wait_ge(mask_made, 2)
                with dve.Fori(0, NT) as t:
                    nc.vector.tensor_scalar(flags[:, :], wall[:, :], wcol[:, bass.ds(t, 1)], 0.0, ALU.is_gt, ALU.add,
                                            accum_out=rank[:, 0, bass.ds(t, 1)]).then_inc(steps, 1)
                    dve.wait_ge(steps, t * 2 + 1)
                    nc.vector.scalar_tensor_tensor(flags[:, :], wall[:, :], wcol[:, bass.ds(t, 1)],
                                                   earlier[:, bass.ds(NP - t * P, N)], ALU.is_equal, ALU.mult,
                                                   accum_out=rank[:, 1, bass.ds(t, 1)]).then_inc(steps, 1)
                    dve.wait_ge(steps, t * 2 + 2)
                st.n = 2 * NT
                st.link(nc.vector.tensor_tensor(coef[:, 0, 0:NT], rank[:, 0, 0:NT], rank[:, 1, 0:NT], ALU.add))
                st.link(nc.vector.tensor_scalar(coef[:, 1, 0:NT], coef[:, 0, 0:NT], float(KEEP), None, ALU.is_lt))
                st.link(nc.vector.tensor_tensor(coef[:, 2, 0:NT], coef[:, 1, 0:NT], wcol[:, 0:NT], ALU.mult))
                dve.wait_ge(h_added, TB + 2)
                with dve.Fori(0, NT) as t:
                    dve.wait_ge(y_ready, t + 1 + 2)
                    nc.vector.scalar_tensor_tensor(y[:, t, :], y[:, t, :], coef[:, 2, bass.ds(t, 1)], c.x[:, t, :],
                                                   ALU.mult, ALU.add).then_inc(final, 1)

            @block.scalar
            def _(act):
                norm_scalar(nc, act, norm, c)
                act.wait_ge(norm.ready, 1)
                act.wait_ge(b1_ready, 1)
                nc.scalar.activation(b1T[:, :], pS[:, 0:FC], ACT.Copy).then_inc(b1_ready, 1)
                with act.Fori(0, TB // 2) as i:
                    for u in range(2):
                        t = i * 2 + u
                        hold(act, h_added, t + 1)
                        nc.scalar.activation(h[u][:, :], c.x[:, t, :], ACT.Identity, bias=c.shift[:, bass.ds(t, 1)],
                                             scale=c.rstd[:, bass.ds(t, 1)]).then_inc(h_ready, 1)
                        hold(act, h_psum, t + 1)
                        nc.scalar.activation(hT[:, :, bass.ds(t * P, P)],
                                             pT[u][:, :].rearrange("p (c n) -> p c n", n=P),
                                             ACT.Copy).then_inc(hT_ready, 1)
                act.sem_inc(gelu_done, 2)
                act.sem_inc(y_ready, 2)

                def mlp(g, tiles, wait):
                    for f in range(FC):
                        wait(act, hid_psum, g * FC + f + 1)
                        nc.scalar.activation(gT[:, f, 0:tiles * P], pH[f % 2][:, 0:tiles * P], ACT.Gelu_apprx_tanh,
                                             bias=b1T[:, f:f + 1]).then_inc(gelu_done, 1)
                    for a in range(tiles):
                        wait(act, y_psum, g * 4 + a + 1)
                        at = g * 4 + a
                        dst = y[:, at, :]
                        nc.scalar.activation(dst, pY[a % 2][:, :], ACT.Copy).then_inc(y_ready, 1)

                with act.Fori(0, NT // 4) as g:
                    mlp(g, 4, hold)
                mlp(NT // 4, NT % 4, lambda e, s, v: e.wait_ge(s, v))

            @block.tensor
            def _(pe):
                pe.wait_ge(loaded, 96)
                nc.tensor.transpose(pS[:, 0:FC], b1_rows[:, :], c.ident[0:FC, 0:FC]).then_inc(b1_ready, 1)
                with pe.Fori(0, TB // 2) as i:
                    for u in range(2):
                        t = i * 2 + u
                        pe.wait_ge(h_ready, t + 1)
                        for k in range(C2):
                            last = nc.tensor.transpose(pT[u][:, k * P:(k + 1) * P], h[u][:, k * P:(k + 1) * P],
                                                       c.ident[:, :])
                        last.then_inc(h_psum, 1)
                pe.wait_ge(hT_ready, TB)
                for t in range(TB):
                    for k in range(C2):
                        last = nc.tensor.matmul(pW[:, t:t + 1], hT[:, k, t * P:(t + 1) * P], wr[:, k:k + 1],
                                                start=k == 0, stop=k == C2 - 1)
                    last.then_inc(w_psum, 1)
                pe.wait_ge(w_ready, 1)
                pe.wait_ge(b1_ready, 2)
                nc.tensor.transpose(pS[0:TB, :], wcol[:, :], c.ident[:, :]).then_inc(row_psum, 1)

                def mlp(g, tiles):
                    cols = bass.ds(g * G4, tiles * P)
                    for f in range(FC):
                        pe.wait_ge(gelu_done, g * FC + f + 1)
                        for k in range(C2):
                            last = nc.tensor.matmul(pH[f % 2][:, 0:tiles * P], w1[:, k, f * P:(f + 1) * P],
                                                    hT[:, k, cols], start=k == 0, stop=k == C2 - 1)
                        last.then_inc(hid_psum, 1)
                    pe.wait_ge(gelu_done, g * FC + FC + 2)
                    for a in range(tiles):
                        pe.wait_ge(y_ready, g * 4 + a + 1)
                        nc.tensor.matmul(pY[a % 2][:, :], c.ones[0:1, :], b2[:, :], start=True, stop=False)
                        for f in range(FC):
                            last = nc.tensor.matmul(pY[a % 2][:, :], gT[:, f, a * P:(a + 1) * P], w2[:, f, :],
                                                    start=False, stop=f == FC - 1)
                        last.then_inc(y_psum, 1)

                with pe.Fori(0, NT // 4) as g:
                    mlp(g, 4)
                mlp(NT // 4, NT % 4)


class Dram:
    pass


def gnn_ffn_kernel(nc, a, out):
    with ExitStack() as ctx:
        def sb(name, shape, dt):
            return ctx.enter_context(nc.sbuf_tensor(name, shape, dt))

        open_sems = []

        def sem(name):
            open_sems.append(nc.alloc_semaphore(name))
            return open_sems[-1]

        def stage(program, *args):
            program(nc, c, sem, *args)
            nc.clear_and_free_semaphores(open_sems)
            open_sems.clear()
            nc.all_engine_barrier()

        c, dram = Consts(), Dram()
        dram.k = nc.dram_tensor("k_table", [TB * P, D], F32, kind="Internal").ap()
        dram.v = nc.dram_tensor("v_table", [TB * P, D], F32, kind="Internal").ap()
        dram.buf = nc.dram_tensor("expert_in", [EXPERTS * CAPW + TB * P, D], F32, kind="Internal").ap()
        dram.ybuf = nc.dram_tensor("expert_out", [EXPERTS * CAPW, D], F32, kind="Internal").ap()
        dram.wrow = nc.dram_tensor("node_weights", [TB * P], F32, kind="Internal").ap()
        dram.list = nc.dram_tensor("edge_list", [P * SW, 4], F32, kind="Internal").ap()
        c.ident = sb("ident", [P, P], F32)
        c.ident_b = sb("ident_b", [P, P], BF16)
        c.big_b = sb("big_b", [P, P], BF16)
        c.before = sb("before", [P, P], F32)
        c.upto = sb("upto", [P, P], F32)
        c.ones = sb("ones", [P, P], F32)
        c.sel = sb("sel", [P, 2, HB, P], BF16)
        c.sel_b = sb("sel_b", [P, HB, P], BF16)
        c.iota_i = sb("iota_i", [P, 256], I32)
        c.iota = sb("iota", [P, 256], F32)
        c.x = sb("x", [P, TB, D], F32)
        c.stats = sb("stats", [P, TB, 6], F32)
        c.norm = sb("norm", [P, 4, TB], F32)
        c.rstd = sb("rstd", [P, TB], F32)
        c.shift = sb("shift", [P, TB], F32)
        c.zero = sb("zero", [P, TB], F32)
        c.spare = sb("spare", [P, TB], F32)
        c.spare_i = sb("spare_i", [P, TB], I32)
        attention = ctx.enter_context(ExitStack())

        def sb(name, shape, dt):
            return attention.enter_context(nc.sbuf_tensor(name, shape, dt))

        c.rec = sb("rec", [P, SW, 4], F32)
        c.gb = sb("group_bucket", [P, GW], I32)
        c.first = sb("first_of_bucket", [P, GW], F32)
        c.final = sb("last_of_bucket", [P, GW], F32)
        c.rel = sb("rel_parts", [NREL, 3, NREL], BF16)
        c.q = sb("q_parts", [P, TB, 3, D], BF16)
        stage(stage_constants, a["x"])
        for layer in range(2):
            tag = f"L{layer}_gnn_"
            ws = [a[tag + n] for n in ("Wq", "bq", "Wk", "bk", "Wv", "bv")]
            ws += [a[tag + "rel_w"], a[tag + "query_emb"]] if layer == 0 else [None, None]
            ends = (a["src"], a["dst"]) if layer == 0 else (a["dst"], a["src"])
            stage(stage_place_and_project, (*ends, a["edge_type_64"]), ws, dram, layer)
            lay = ctx.enter_context(ExitStack())
            c.s = lay.enter_context(nc.sbuf_tensor(f"scores{layer}", [P, SW * HB], F32))
            c.m = lay.enter_context(nc.sbuf_tensor(f"maxima{layer}", [P, NG, 2, HB], BF16))
            stage(stage_scores, dram, layer)
            with ExitStack() as agg:
                c.acc = agg.enter_context(nc.sbuf_tensor(f"sums{layer}", [P, TB, D + HB], F32))
                stage(stage_aggregate, dram, layer)
                ws = [a[tag + "Wo"], a[tag + "bo"]]
                ws += [a[tag + "gamma"], a[tag + "beta"]] if layer == 0 else [None, None]
                stage(stage_output, dram, ws, layer)
            lay.close()
            if layer == 0:
                with ExitStack() as moe:
                    c.b1T = moe.enter_context(nc.sbuf_tensor("b1T", [P, EXPERTS * FC], F32))
                    c.place = moe.enter_context(nc.sbuf_tensor("place", [P, 2, TB], I32))
                    c.weight = moe.enter_context(nc.sbuf_tensor("weight", [P, TB], F32))
                    stage(stage_gate, dram, (a["L0_ffn_gate_w"], a["L0_ffn_gate_b"], a["L0_ffn_b1"]))
                    stage(stage_experts, dram, (a["L0_ffn_w1"], a["L0_ffn_w2"], a["L0_ffn_b2"]))
                    stage(stage_combine, dram)
        attention.close()
        stage(stage_last, dram, [a["L1_ffn_" + n] for n in ("wr", "br", "w1", "b1", "w2", "b2")], out)


_INS = ['x', 'src', 'dst', 'edge_type_64', 'L0_gnn_query_emb', 'L0_gnn_Wq', 'L0_gnn_bq', 'L0_gnn_Wk', 'L0_gnn_bk',
        'L0_gnn_Wv', 'L0_gnn_bv', 'L0_gnn_rel_w', 'L0_gnn_Wo', 'L0_gnn_bo', 'L0_gnn_gamma', 'L0_gnn_beta',
        'L0_ffn_gate_w', 'L0_ffn_gate_b', 'L0_ffn_w1', 'L0_ffn_b1', 'L0_ffn_w2', 'L0_ffn_b2', 'L1_gnn_Wq',
        'L1_gnn_bq', 'L1_gnn_Wk', 'L1_gnn_bk', 'L1_gnn_Wv', 'L1_gnn_bv', 'L1_gnn_Wo', 'L1_gnn_bo',
        'L1_ffn_attention_mask', 'L1_ffn_wr', 'L1_ffn_br', 'L1_ffn_w1', 'L1_ffn_b1', 'L1_ffn_w2', 'L1_ffn_b2']


def laid_out(inputs):
    a = {name: np.ascontiguousarray(inputs[name]) for name in _INS}
    for n in ("Wq", "Wk", "Wv"):
        w = a["L1_gnn_" + n]
        a["L1_gnn_" + n] = np.ascontiguousarray(w.reshape(D, D // HB, HB).transpose(0, 2, 1).reshape(D, D))
        b = a["L1_gnn_b" + n[1]]
        a["L1_gnn_b" + n[1]] = np.ascontiguousarray(b.reshape(D // HB, HB).transpose(1, 0).reshape(D))
    w = a["L1_gnn_Wo"]
    a["L1_gnn_Wo"] = np.ascontiguousarray(w.reshape(D // HB, HB, D).transpose(1, 0, 2).reshape(D, D))
    return a


def kernel(**inputs):
    import concourse.bacc as bacc
    from concourse.bass_utils import run_bass_kernel_spmd

    nc = bacc.Bacc("TRN2", target_bir_lowering=False, num_devices=1)
    arrays, args = {}, {}
    for name, a in laid_out(inputs).items():
        arrays[f"in_{name}"] = a
        args[name] = nc.dram_tensor(f"in_{name}", a.shape, mybir.dt.from_np(a.dtype), kind="ExternalInput").ap()
    out = nc.dram_tensor("out_x", [N, D], F32, kind="ExternalOutput").ap()
    gnn_ffn_kernel(nc, args, out)
    r = run_bass_kernel_spmd(nc, [arrays], core_ids=[0])
    return r.results[0]["out_x"]
```

```python
from contextlib import ExitStack

import concourse.bass as bass
from concourse import mybir
import numpy as np

F32 = mybir.dt.float32
BF16 = mybir.dt.bfloat16
I32 = mybir.dt.int32
ALU = mybir.AluOpType
ACT = mybir.ActivationFunctionType
AX = mybir.AxisListType

P = 128
N = 3125
D = 256
C2 = D // P
E = 50000
NT = -(-N // P)
LAST = N - (NT - 1) * P
TB = NT + 1
EC = -(-E // P)
EFULL = E // EC
EREST = E - EFULL * EC
BN = 64
NB = -(-N // BN)
BB = 2 * TB
BK = NB + 1
GE = 2 * P
NG = (E - NB) // GE + NB
NS = 2 * NG
SPI = 8
GPI = SPI // 2
TURNS = NS // SPI
SW = NS + SPI
GW = SW // 2
NREL = 64
BIG = 1.0e30
assert NS % SPI == 0 and EREST > 0 and TB % 2 == 0

SCAT = 17
HALF = (12, 11)
assert SCAT * sum(HALF) == EC
HA, HB = 4, 8
SR = BN + 2 * HB
EXPERTS, CAP, FF = 8, 489, 1024
CAPW = 512
FC = FF // P


class Steps:

    def __init__(self, eng, sem, start=0):
        self.eng, self.sem, self.n = eng, sem, start

    def __call__(self, ins):
        self.n += 1
        return ins.then_inc(self.sem, 1)

    def sync(self):
        self.eng.wait_ge(self.sem, self.n)

    def link(self, ins):
        self(ins)
        self.sync()


def hold(eng, sem, value):
    eng.wait_ge(sem, value)
    eng.nop(nofuse=True)


def need(eng, sem, value, wait=None):
    if not isinstance(value, int) or value > 0:
        (wait or eng.wait_ge)(*(() if wait is None else (eng,)), sem, value)


def pipeline(eng, step, ends):
    for q in range(GPI):
        step(0, q)
    with eng.Fori(1, TURNS) as i:
        for q in range(GPI):
            step(i, q)
    for q in range(ends):
        step(TURNS, q)


def lives(i, q, ahead=0):
    return not isinstance(i, int) or 0 <= i * GPI + q + ahead < NG


class Consts:
    pass


def stage_constants(nc, c, sem, x):
    made = sem("constants_made")
    pooled = sem("constants_pool")
    got = sem("x_loaded")
    summed = sem("constants_summed")
    halves = [(layer, part) for layer in range(2) for part in range(2)]
    with ExitStack() as ctx:
        member = ctx.enter_context(nc.sbuf_tensor("member", [SR, 2, BN], BF16))
        pick = ctx.enter_context(nc.sbuf_tensor("pick", [SR, 2, 2, HB // 2, 2, BN], BF16))
        _constants(nc, c, x, made, pooled, got, summed, halves, member, pick)


def _constants(nc, c, x, made, pooled, got, summed, halves, member, pick):
    with nc.Block() as block:

        @block.gpsimd
        def _(pool):
            st = Steps(pool, pooled)
            st(nc.gpsimd.memset(c.ident[:, :], 0.0))
            st(nc.gpsimd.memset(c.before[:, :], 1.0))
            st(nc.gpsimd.memset(c.upto[:, :], 1.0))
            st(nc.gpsimd.memset(c.ones[:, :], 1.0))
            st(nc.gpsimd.memset(member[:, :, :], 1.0))
            st(nc.gpsimd.memset(pick[:, :, :, :, :, :], 1.0))
            st(nc.gpsimd.memset(c.zero[:, :], 0.0))
            st(nc.gpsimd.iota(c.spare_i[:, :], pattern=[[P, TB]], base=EXPERTS * CAPW, channel_multiplier=1))
            st(nc.gpsimd.iota(c.iota_i[:, :], pattern=[[1, 256]], base=0, channel_multiplier=0))
            st.sync()
            st(nc.gpsimd.affine_select(out=c.ident[:, :], in_=c.ident[:, :], compare_op=ALU.not_equal, fill=1.0,
                                       base=0, pattern=[[-1, P]], channel_multiplier=1))
            st(nc.gpsimd.affine_select(out=c.before[:, :], in_=c.before[:, :], compare_op=ALU.is_gt, fill=0.0,
                                       base=0, pattern=[[1, P]], channel_multiplier=-1))
            st(nc.gpsimd.affine_select(out=c.upto[:, :], in_=c.upto[:, :], compare_op=ALU.is_ge, fill=0.0,
                                       base=0, pattern=[[1, P]], channel_multiplier=-1))
            st(nc.gpsimd.affine_select(out=member[:, :, :], in_=member[:, :, :], compare_op=ALU.is_equal, fill=0.0,
                                       base=0, pattern=[[0, 2], [-1, BN]], channel_multiplier=1))
            for layer, part in halves:
                HH = (HA, HB)[layer] // 2
                a = pick[:, layer, part, 0:HH, :, :]
                st(nc.gpsimd.affine_select(out=a, in_=a, compare_op=ALU.is_equal, fill=0.0, base=-BN - part * HB,
                                           pattern=[[-1, HH], [-HH, 2], [0, BN]], channel_multiplier=1))
            st.sync()
            nc.gpsimd.tensor_copy(c.spare[:, :], c.spare_i[:, :]).then_inc(made, 1)
            nc.gpsimd.tensor_copy(c.iota[:, :], c.iota_i[:, :]).then_inc(made, 1)

        @block.vector
        def _(dve):
            nc.vector.memset(c.x[:, NT - 1:TB, :], 0.0).then_inc(got, 1)
            dve.wait_ge(pooled, 17)
            nc.vector.tensor_copy(c.ident_b[:, :], c.ident[:, :]).then_inc(made, 1)
            st = Steps(dve, summed)
            for layer in range(2):
                for j in range((HA, HB)[layer] // 2):
                    out = c.spread[:, layer, j, :]
                    st.link(nc.vector.tensor_tensor(out, pick[:, layer, 0, j, :, :].rearrange("p f n -> p (f n)"),
                                                    pick[:, layer, 1, j, :, :].rearrange("p f n -> p (f n)"), ALU.add))
                    st.link(nc.vector.scalar_tensor_tensor(out, member[:, :, :].rearrange("p f n -> p (f n)"), BIG,
                                                           out, ALU.mult, ALU.add))

        @block.sync
        def _(sp):
            sp.dma_start(c.x[:, 0:NT - 1, :],
                         x[0:(NT - 1) * P, :].rearrange("(t p) d -> p t d", p=P)).then_inc(got, 16)
            sp.wait_ge(got, 17)
            sp.dma_start(c.x[0:LAST, NT - 1, :], x[(NT - 1) * P:N, :]).then_inc(got, 16)
            sp.wait_ge(got, 33)
            sp.wait_ge(made, 3)


class NormSemaphores:
    def __init__(self, sem, tag):
        self.stats = sem(tag + "norm_stats")
        self.var = sem(tag + "norm_var")
        self.std = sem(tag + "norm_std")
        self.ready = sem(tag + "norm_ready")


def norm_vector(nc, dve, c, norm, x):
    with dve.Fori(0, TB) as t:
        nc.vector.bn_stats(c.stats[:, t, :], x[:, t, :]).then_inc(norm.stats, 1)
    dve.wait_ge(norm.stats, TB)
    st = Steps(dve, norm.stats, TB)
    mean_e, m2_e, mean_o, m2_o = (c.stats[:, :, k] for k in (1, 2, 4, 5))
    st(nc.vector.tensor_tensor(c.norm[:, 0, :], mean_e, mean_o, ALU.add))
    st(nc.vector.tensor_tensor(c.norm[:, 1, :], mean_e, mean_o, ALU.subtract))
    st(nc.vector.tensor_tensor(c.norm[:, 2, :], m2_e, m2_o, ALU.add))
    st.sync()
    st.link(nc.vector.tensor_tensor(c.norm[:, 1, :], c.norm[:, 1, :], c.norm[:, 1, :], ALU.mult))
    st.link(nc.vector.scalar_tensor_tensor(c.norm[:, 2, :], c.norm[:, 1, :], D / 4.0, c.norm[:, 2, :],
                                           ALU.mult, ALU.add))
    nc.vector.tensor_scalar(c.norm[:, 3, :], c.norm[:, 2, :], 1.0 / D, 1e-5, ALU.mult, ALU.add).then_inc(norm.var, 1)
    dve.wait_ge(norm.std, 1)
    st.link(nc.vector.reciprocal(c.rstd[:, :], c.norm[:, 1, :]))
    nc.vector.scalar_tensor_tensor(c.shift[:, :], c.norm[:, 0, :], -0.5, c.rstd[:, :], ALU.mult,
                                   ALU.mult).then_inc(norm.ready, 1)


def norm_scalar(nc, act, norm, c):
    act.wait_ge(norm.var, 1)
    nc.scalar.activation(c.norm[:, 1, :], c.norm[:, 3, :], ACT.Sqrt).then_inc(norm.std, 1)


def stage_place_and_project(nc, c, sem, edges, weights, dram, layer):
    H = HA if layer == 0 else HB
    T = f"L{layer}_"
    with ExitStack() as ctx:
        def sb(name, shape, dt):
            return ctx.enter_context(nc.sbuf_tensor(T + name, shape, dt))

        def ps(name, shape, dt):
            return ctx.enter_context(nc.psum_tensor(T + name, shape, dt))

        w = sb("wqkv", [P, C2, 3 * D], F32)
        bias = sb("bqkv", [P, 3 * D], F32)
        hn = sb("hn", [P, 2, D], F32)
        hT = [sb(f"hT{u}", [P, C2, P], F32) for u in range(2)]
        qkv = sb("qkv", [P, 2, 3 * D], F32)
        rest = sb("rest", [P, 2, D], F32)
        qp = sb("qp", [P, 2, 3, D], BF16)
        pT = [ps(f"pT{u}", [P, D], F32) for u in range(2)]
        pQK = ps("pQK", [P, 2, 2 * D], F32)
        pV = [ps(f"pV{u}", [P, D], F32) for u in range(2)]
        if layer == 0:
            rel_in = sb("rel_in", [P, NREL], F32)
            rel_rest = sb("rel_rest", [P, NREL], F32)
            q_col = sb("q_col", [P, C2], F32)
            q_cols = sb("q_cols", [P, C2, P], F32)
        stage_i = [sb(f"stage_i{u}", [P, HALF[u]], I32) for u in range(2)]
        stage_r = [sb(f"stage_r{u}", [P, HALF[u], 4], F32) for u in range(2)]
        dst_i = sb("dst_i", [P, EC], I32)
        src_i = sb("src_i", [P, EC], I32)
        typ_i = sb("typ_i", [P, EC], I32)
        lo_i = sb("lo_i", [P, EC], I32)
        hi_i = sb("hi_i", [P, EC], I32)
        hi_f = sb("hi_f", [P, EC], F32)
        record = sb("record", [P, EC, 4], F32)
        is_b = sb("is_b", [P, BK, EC], BF16)
        rank = c.q_place[:, 0:BK * EC].rearrange("p (b e) -> p b e", b=BK)
        count = sb("count", [P, BK], F32)
        small = sb("small", [P, 6, BK], F32)
        small_i = sb("small_i", [P, 2, BK], I32)
        pos, at, lane = hi_f, hi_i, lo_i
        row_i = sb("row_i", [P, EC], I32)
        later = is_b[:, :, :].rearrange("p b e -> p (b e)")[:, 0:GW * NB].rearrange("p (g b) -> p g b", b=NB)
        blank = c.rec
        gb_f = sb("gb_f", [P, GW], F32)
        pC = ps("pC", [P, 2, BK], F32)

        loaded = sem(T + "w_loaded")
        edges_loaded = sem(T + "edges_loaded")
        edges_blank = sem(T + "edges_blank")
        blank_made = sem(T + "blank_made")
        v = sem(T + "dve_steps")
        counted = sem(T + "counted")
        summed = sem(T + "summed")
        placed = sem(T + "placed")
        list_in = sem(T + "list_in")
        staged = sem(T + "staged")
        scattered = [sem(T + f"scattered{u}") for u in range(2)]
        weights_ready = sem(T + "weights_ready")
        query_summed = sem(T + "query_summed")
        norm = NormSemaphores(sem, T)
        hn_ready = sem(T + "hn_ready")
        hT_psum = sem(T + "hT_psum")
        hT_ready = sem(T + "hT_ready")
        qkv_psum = sem(T + "qkv_psum")
        biased = sem(T + "biased")
        tile_steps = sem(T + "tile_steps")
        split = sem(T + "q_split")
        stored = [sem(T + f"stored{u}") for u in range(2)]
        q_stored = [sem(T + f"q_stored{u}") for u in range(2)]
        Wq, bq, Wk, bk, Wv, bv, rel, q_emb = weights
        half = HALF

        with nc.Block() as block:

            @block.sync
            def _(sp):
                src, dst, typ = edges
                sp.wait_ge(edges_blank, 3)
                for tile, a in ((dst_i, dst), (src_i, src), (typ_i, typ)):
                    sp.dma_start(tile[0:EFULL, :],
                                 a[0:EFULL * EC].rearrange("(p e) -> p e", p=EFULL)).then_inc(edges_loaded, 16)
                    sp.dma_start(tile[EFULL:EFULL + 1, 0:EREST],
                                 a[EFULL * EC:E].rearrange("(p e) -> p e", p=1)).then_inc(edges_loaded, 16)
                for k, a in enumerate((Wq, Wk, Wv)):
                    sp.dma_start(w[:, :, k * D:(k + 1) * D],
                                 a.rearrange("(c p) n -> p c n", p=P)).then_inc(loaded, 16)
                for k, a in enumerate((bq, bk, bv)):
                    sp.dma_start(bias[:, k * D:(k + 1) * D],
                                 a.rearrange("(o n) -> o n", o=1).broadcast_to([P, D])).then_inc(loaded, 16)
                if layer == 0:
                    sp.dma_start(q_col[:, :], q_emb.rearrange("(c p) -> p c", p=P), allow_slow_non_contiguous=True).then_inc(loaded, 16)
                    sp.dma_start(rel_in[BN:P, :], rel).then_inc(loaded, 16)
                with sp.Fori(0, TB // 2) as i:
                    for u in range(2):
                        hold(sp, biased, i * 2 + u + 3)
                        rows = bass.ds((i * 2 + u) * P, P)
                        sp.dma_start(dram.k[rows, :], qkv[:, u, D:2 * D]).then_inc(stored[u], 16)
                        sp.dma_start(dram.v[rows, :], qkv[:, u, 2 * D:3 * D]).then_inc(stored[u], 16)
                        hold(sp, split, i * 2 + u + 1)
                        for part in range(2):
                            sp.dma_start(c.q[:, bass.ds(i * 4 + u * 2 + part, 1), :, :].rearrange("p o k d -> p (o k d)"),
                                         qp[part * BN:(part + 1) * BN, u, :, :].rearrange("p k d -> p (k d)")
                                         ).then_inc(q_stored[u], 16)
                for u in range(2):
                    sp.wait_ge(stored[u], TB // 2 * 32)
                    sp.wait_ge(q_stored[u], TB // 2 * 32)
                for u in range(2):
                    sp.wait_ge(scattered[u], SCAT * half[u] * 16 + 16)
                sp.dma_start(c.rec[:, :, :].rearrange("p s f -> p (s f)"),
                             dram.list.rearrange("(p s) f -> p (s f)", p=P)).then_inc(list_in, 16)
                sp.wait_ge(list_in, 16)

            @block.gpsimd
            def _(pool):
                nc.gpsimd.memset(dst_i[:, :], NB * BN).then_inc(edges_blank, 1)
                nc.gpsimd.memset(src_i[:, :], 0).then_inc(edges_blank, 1)
                nc.gpsimd.memset(typ_i[:, :], 0).then_inc(edges_blank, 1)
                nc.gpsimd.memset(blank[:, :, 0], 0.0).then_inc(blank_made, 1)
                nc.gpsimd.memset(blank[:, :, 1], 200.0).then_inc(blank_made, 1)
                nc.gpsimd.memset(blank[:, :, 2:4], 100.0).then_inc(blank_made, 1)
                pool.wait_ge(blank_made, 3)
                for u in range(2):
                    nc.gpsimd.dma_start(
                        dram.list.rearrange("(p s) f -> p (s f)", p=P)[u * (P // 2):(u + 1) * (P // 2), :],
                        blank[u * (P // 2):(u + 1) * (P // 2), :, :].rearrange("p s f -> p (s f)")).then_inc(scattered[u], 16)
                pool.wait_ge(placed, 1)
                for u in range(2):
                    pool.wait_ge(scattered[u], 16)
                with pool.Fori(0, SCAT) as i:
                    for u in range(2):
                        col = i * (half[0] + half[1]) + u * half[0]
                        hold(pool, scattered[u], i * (16 * half[u]) + 16)
                        nc.gpsimd.tensor_copy(stage_i[u][:, :], row_i[:, bass.ds(col, half[u])]).then_inc(staged, 1)
                        nc.gpsimd.tensor_copy(stage_r[u][:, :, :],
                                              record[:, bass.ds(col, half[u]), :]).then_inc(staged, 1)
                        hold(pool, staged, i * 4 + u * 2 + 2)
                        for j in range(half[u]):
                            nc.gpsimd.indirect_dma_start(
                                out=dram.list,
                                out_offset=bass.IndirectOffsetOnAxis(ap=stage_i[u][:, j:j + 1], axis=0),
                                in_=stage_r[u][:, j, :], in_offset=None).then_inc(scattered[u], 16)

            @block.vector
            def _(dve):
                st = Steps(dve, v)
                dve.wait_ge(edges_loaded, 96)
                st(nc.vector.tensor_scalar(lo_i[:, :], dst_i[:, :], BN - 1, None, ALU.bitwise_and))
                st(nc.vector.tensor_scalar(hi_i[:, :], dst_i[:, :], 6, None, ALU.arith_shift_right))
                st(nc.vector.tensor_copy(record[:, :, 0].bitcast(I32), src_i[:, :]))
                st(nc.vector.tensor_copy(record[:, :, 2], typ_i[:, :]))
                st(nc.vector.memset(record[:, :, 3], 0.0))
                st.sync()
                st(nc.vector.tensor_copy(record[:, :, 1], lo_i[:, :]))
                st.link(nc.vector.tensor_copy(hi_f[:, :], hi_i[:, :]))
                st.link(nc.vector.tensor_tensor(is_b[:, :, :],
                                                hi_f[:, :].unsqueeze(1).broadcast_to([P, BK, EC]),
                                                c.iota[:, 0:BK].unsqueeze(2).broadcast_to([P, BK, EC]),
                                                ALU.is_equal))
                flat = is_b[:, :, :].rearrange("p b e -> p (b e)")
                st.link(nc.vector.tensor_tensor_scan(rank.rearrange("p b e -> p (b e)"), flat, flat,
                                                     0.0, ALU.add, ALU.bypass))
                ends = rank[:, :, EC - 1]
                st(nc.vector.tensor_copy(count[:, 0:1], ends[:, 0:1]))
                st(nc.vector.tensor_tensor(count[:, 1:BK], ends[:, 1:BK], ends[:, 0:BK - 1], ALU.subtract))
                st.sync()
                nc.vector.tensor_tensor(small[:, 0, :], count[:, :], ends, ALU.subtract).then_inc(counted, 1)
                dve.wait_ge(summed, 2)
                dve.wait_ge(counted, 1)
                st(nc.vector.tensor_tensor(small[:, 1, :], small[:, 0, :], pC[:, 0, :], ALU.add))
                st.link(nc.vector.tensor_scalar(small_i[:, 0, :], pC[:, 1, :], float(GE - 1), None, ALU.add))
                st.link(nc.vector.tensor_scalar(small_i[:, 1, :], small_i[:, 0, :], 8, None,
                                                ALU.arith_shift_right))
                st.link(nc.vector.tensor_copy(small[:, 2, :], small_i[:, 1, :]))
                st.link(nc.vector.tensor_tensor_scan(small[:, 3, :], small[:, 2, :], small[:, 2, :], 0.0,
                                                     ALU.add, ALU.bypass))
                st.link(nc.vector.tensor_tensor(small[:, 4, :], small[:, 3, :], small[:, 2, :], ALU.subtract))
                st.link(nc.vector.tensor_scalar(small[:, 5, :], small[:, 4, :], float(GE), -1.0,
                                                ALU.mult, ALU.add))
                st.link(nc.vector.tensor_tensor(small[:, 4, :], small[:, 5, :], small[:, 1, :], ALU.add))
                st.link(nc.vector.tensor_tensor(rank, rank,
                                                small[:, 4, :].unsqueeze(2).broadcast_to([P, BK, EC]), ALU.add))
                st.link(nc.vector.tensor_tensor(rank, rank, is_b[:, :, :], ALU.mult))
                st.link(nc.vector.tensor_reduce(pos[:, :], rank.rearrange("p b e -> p e b"),
                                                AX.X, ALU.add))
                st.link(nc.vector.tensor_copy(at[:, :], pos[:, :]))
                st(nc.vector.tensor_scalar(lane[:, :], at[:, :], P - 1, None, ALU.bitwise_and))
                st.link(nc.vector.tensor_scalar(row_i[:, :], at[:, :], 7, None, ALU.arith_shift_right))
                st.link(nc.vector.scalar_tensor_tensor(pos[:, :], lane[:, :], float(SW), row_i[:, :],
                                                       ALU.mult, ALU.add))
                st.sync()
                nc.vector.tensor_copy(row_i[:, :], pos[:, :]).then_inc(placed, 1)
                st.link(nc.vector.tensor_tensor(later,
                                                small[:, 3, 0:NB].unsqueeze(1).broadcast_to([P, GW, NB]),
                                                c.iota[:, 0:GW].unsqueeze(2).broadcast_to([P, GW, NB]),
                                                ALU.is_le))
                st.link(nc.vector.tensor_reduce(gb_f[:, :], later, AX.X, ALU.add))
                st(nc.vector.tensor_copy(c.gb[:, :], gb_f[:, :]))
                st(nc.vector.memset(c.first[:, :], -BIG))
                st(nc.vector.memset(c.final[:, :], -BIG))
                st.sync()
                st(nc.vector.tensor_tensor(c.first[:, 1:NG], gb_f[:, 1:NG], gb_f[:, 0:NG - 1], ALU.not_equal))
                st(nc.vector.tensor_tensor(c.final[:, 0:NG - 1], gb_f[:, 1:NG], gb_f[:, 0:NG - 1],
                                           ALU.not_equal))
                st.sync()
                st(nc.vector.tensor_scalar(c.first[:, 1:NG], c.first[:, 1:NG], -BIG, None, ALU.mult))
                st(nc.vector.tensor_scalar(c.final[:, 0:NG - 1], c.final[:, 0:NG - 1], -BIG, None, ALU.mult))
                if layer == 0:
                    dve.wait_ge(loaded, 128)
                    st.link(nc.vector.tensor_scalar(rel_in[BN:P, :], rel_in[BN:P, :], 0.2, None, ALU.mult))
                    st.link(nc.vector.tensor_copy(c.rel[BN:P, 0, :], rel_in[BN:P, :]))
                    st.link(nc.vector.tensor_tensor(rel_rest[BN:P, :], rel_in[BN:P, :], c.rel[BN:P, 0, :], ALU.subtract))
                    st.link(nc.vector.tensor_copy(c.rel[BN:P, 1, :], rel_rest[BN:P, :]))
                    st(nc.vector.tensor_tensor(c.rel[BN:P, 2, :], rel_rest[BN:P, :], c.rel[BN:P, 1, :], ALU.subtract))
                    st(nc.vector.tensor_scalar(q_cols[:, :, :],
                                               q_col[:, :].unsqueeze(2).broadcast_to([P, C2, P]), 0.1, None,
                                               ALU.mult))
                else:
                    dve.wait_ge(loaded, 96)
                scale = float(D // H) ** -0.5
                st(nc.vector.tensor_scalar(w[:, :, 0:D], w[:, :, 0:D], scale, None, ALU.mult))
                st(nc.vector.tensor_scalar(bias[:, 0:D], bias[:, 0:D], scale, None, ALU.mult))
                st.sync()
                dve.sem_inc(weights_ready, 1)
                norm_vector(nc, dve, c, norm, c.x)
                if layer == 0:
                    dve.wait_ge(query_summed, 2)
                    st(nc.vector.tensor_tensor(bias[:, 0:2 * D], pQK[:, 0, :], bias[:, 0:2 * D], ALU.add))
                    st(nc.vector.tensor_tensor(bias[:, 2 * D:], pV[0][:, :], bias[:, 2 * D:], ALU.add))
                    st.sync()
                dve.sem_inc(biased, 2)
                def pair(i, first=False):
                    for u in range(2):
                        t = i * 2 + u
                        tick = i * 8 + u * 4
                        if not first:
                            dve.wait_ge(stored[u], i * 32)
                            dve.wait_ge(q_stored[u], i * 32)
                        dve.wait_ge(qkv_psum, t + 3)
                        nc.vector.tensor_tensor(qkv[:, u, 0:2 * D], pQK[:, u, :], bias[:, 0:2 * D],
                                                ALU.add).then_inc(tile_steps, 1)
                        nc.vector.tensor_tensor(qkv[:, u, 2 * D:], pV[u][:, :], bias[:, 2 * D:],
                                                ALU.add).then_inc(biased, 1)
                        dve.wait_ge(tile_steps, tick + 1)
                        nc.vector.tensor_copy(qp[:, u, 0, :], qkv[:, u, 0:D]).then_inc(tile_steps, 1)
                        dve.wait_ge(tile_steps, tick + 2)
                        nc.vector.tensor_tensor(rest[:, u, :], qkv[:, u, 0:D], qp[:, u, 0, :],
                                                ALU.subtract).then_inc(tile_steps, 1)
                        dve.wait_ge(tile_steps, tick + 3)
                        nc.vector.tensor_copy(qp[:, u, 1, :], rest[:, u, :]).then_inc(tile_steps, 1)
                        dve.wait_ge(tile_steps, tick + 4)
                        nc.vector.tensor_tensor(qp[:, u, 2, :], rest[:, u, :], qp[:, u, 1, :],
                                                ALU.subtract).then_inc(split, 1)

                pair(0, first=True)
                with dve.Fori(1, TB // 2) as i:
                    pair(i)

            @block.scalar
            def _(act):
                norm_scalar(nc, act, norm, c)
                act.wait_ge(norm.ready, 1)
                with act.Fori(0, TB // 2) as i:
                    for u in range(2):
                        t = i * 2 + u
                        hold(act, qkv_psum, t + 1)
                        nc.scalar.activation(hn[:, u, :], c.x[:, t, :], ACT.Identity, bias=c.shift[:, bass.ds(t, 1)],
                                             scale=c.rstd[:, bass.ds(t, 1)]).then_inc(hn_ready, 1)
                        hold(act, hT_psum, t + 1)
                        nc.scalar.activation(hT[u][:, :, :].rearrange("p c n -> p (c n)"), pT[u][:, :],
                                             ACT.Copy).then_inc(hT_ready, 1)

            @block.tensor
            def _(pe):
                pe.wait_ge(counted, 1)
                nc.tensor.matmul(pC[:, 0, :], c.before[:, :], count[:, :], start=True, stop=True).then_inc(summed, 1)
                nc.tensor.matmul(pC[:, 1, :], c.ones[:, :], count[:, :], start=True, stop=True).then_inc(summed, 1)
                pe.wait_ge(weights_ready, 1)
                if layer == 0:
                    for out, lo, hi in ((pQK[:, 0, :], 0, 2 * D), (pV[0][:, :], 2 * D, 3 * D)):
                        for k in range(C2):
                            last = nc.tensor.matmul(out, q_cols[:, k, :], w[:, k, lo:hi], start=k == 0, stop=k == C2 - 1)
                        last.then_inc(query_summed, 1)
                pe.sem_inc(qkv_psum, 2)
                with pe.Fori(0, TB // 2) as i:
                    for u in range(2):
                        t = i * 2 + u
                        pe.wait_ge(hn_ready, t + 1)
                        for k in range(C2):
                            last = nc.tensor.transpose(pT[u][:, k * P:(k + 1) * P], hn[:, u, k * P:(k + 1) * P],
                                                       c.ident[:, :])
                        last.then_inc(hT_psum, 1)
                        pe.wait_ge(hT_ready, t + 1)
                        pe.wait_ge(biased, t + 1)
                        for out, lo, hi in ((pQK[:, u, :], 0, 2 * D), (pV[u][:, :], 2 * D, 3 * D)):
                            for k in range(C2):
                                last = nc.tensor.matmul(out, hT[u][:, k, :], w[:, k, lo:hi], start=k == 0,
                                                        stop=k == C2 - 1)
                        last.then_inc(qkv_psum, 1)


def gather_rows(nc, pool, sem, T, table, rec, stage, ring, gathered, used):
    staged = sem(T + "indices_staged")

    def turn(i, first=False):
        for half in range(2):
            if not first:
                hold(pool, used, i * GPI + 2 * half - 2)
            nc.gpsimd.tensor_copy(stage[half][:, :],
                                  rec[:, bass.ds(i * SPI + half * 4, 4), 0].bitcast(I32)).then_inc(staged, 1)
            hold(pool, staged, i * 2 + half + 1)
            for q in (2 * half, 2 * half + 1):
                for k in range(2):
                    nc.gpsimd.indirect_dma_start(
                        out=ring[:, 2 * q + k, :], out_offset=None, in_=table,
                        in_offset=bass.IndirectOffsetOnAxis(ap=stage[half][:, 2 * (q % 2) + k:2 * (q % 2) + k + 1],
                                                            axis=0)).then_inc(gathered[q], 16)

    turn(0, first=True)
    with pool.Fori(1, TURNS) as i:
        turn(i)


def stage_scores(nc, c, sem, dram, layer):
    H = HA if layer == 0 else HB
    HH = H // 2
    KINDS = 2 if layer == 0 else 1
    T = f"L{layer}_score_"
    with ExitStack() as ctx:
        def sb(name, shape, dt):
            return ctx.enter_context(nc.sbuf_tensor(T + name, shape, dt))

        def ps(name, shape, dt):
            return ctx.enter_context(nc.psum_tensor(T + name, shape, dt))

        kg = sb("kg", [P, SPI, D], F32)
        stage = [sb(f"stage{u}", [P, 4], I32) for u in range(2)]
        oh = sb("oh", [P, SPI, KINDS, BN], BF16)
        ohT = sb("ohT", [P, GPI, GE], BF16)
        prod = sb("prod", [P, 2, 2 * D], F32)
        sp2 = sb("sp2", [P, 2, 2, SR], BF16)
        rhs = sb("spread_rhs", [SR, GPI, GE], BF16)
        mp = sb("mp", [P, HH, GW], F32)
        fw = sb("fw", [P, HH, GW], F32)
        m2 = sb("m2", [P, NG, 2, HH], BF16)
        BT = 2 if layer == 0 else 1
        pT = [ps(f"pT{u}", [P, GE], BF16) for u in range(BT)]
        if layer == 0:
            pR = ps("pR", [P, 2, NREL], F32)
        pS = ps("pS", [SR, GE], BF16)
        pQ = [ps(f"pQ{u}", [P, 2 * D], F32) for u in range(2)]
        pM = [ps(f"pM{u}", [P, HH * GE], F32) for u in range(2)]

        gathered = [sem(T + f"k_gathered{q}") for q in range(GPI)]
        cleared = sem(T + "cleared")
        oh_made = sem(T + "onehot_made")
        tr_done = sem(T + "onehot_transposed")
        ohT_ready = sem(T + "onehotT_ready")
        mask_ready = sem(T + "mask_ready")
        qe_ready = sem(T + "q_of_edges_ready")
        rel_ready = sem(T + "relation_of_edges_ready")
        added = sem(T + "relation_added")
        prod_done = sem(T + "product_done")
        s_ready = sem(T + "scores_ready")
        hi_ready = sem(T + "score_high_ready")
        lo_ready = sem(T + "score_low_ready")
        st_psum = sem(T + "scores_transposed")
        sT_ready = sem(T + "scoresT_ready")
        spread = sem(T + "scores_spread")
        max_done = sem(T + "maxima_done")
        joined = sem(T + "maxima_joined")
        moved = sem(T + "maxima_moved")

        with nc.Block() as block:

            @block.gpsimd
            def _(pool):
                gather_rows(nc, pool, sem, T, dram.k, c.rec, stage, kg, gathered, prod_done)

            @block.sync
            def _(sp):
                sp.wait_ge(joined, 2 * HH + 2)
                sp.dma_start(c.m[:, 1, :, :, :], m2[BN:P, :, :, :]).then_inc(moved, 16)
                sp.wait_ge(moved, 16)

            @block.vector
            def _(dve):
                def onehot(i, q, slots):
                    nc.vector.tensor_tensor(oh[:, 2 * q:2 * q + 2, :, :],
                                            c.iota[:, 0:BN].unsqueeze(1).unsqueeze(1).broadcast_to([P, 2, KINDS, BN]),
                                            c.rec[:, slots, 1:1 + KINDS].unsqueeze(3).broadcast_to([P, 2, KINDS, BN]),
                                            ALU.is_equal).then_inc(oh_made, 1)

                def low_part(i, q, ahead):
                    if not lives(i, q, ahead):
                        return
                    r = (q + ahead) % GPI
                    dve.wait_ge(hi_ready, i * GPI + q + ahead + 1)
                    nc.vector.tensor_tensor(
                        sp2[:, r % 2, :, BN + HB:BN + HB + H],
                        c.s[:, bass.ds((i * SPI + 2 * (q + ahead)) * H, 2 * H)].rearrange("p (s h) -> p s h", h=H),
                        sp2[:, r % 2, :, BN:BN + H], ALU.subtract).then_inc(lo_ready, 1)

                def maxima(i, q, ahead):
                    if not lives(i, q, ahead):
                        return
                    g = i * GPI + q + ahead
                    dve.wait_ge(spread, g + 1)
                    nc.vector.tensor_reduce(
                        mp[:, :, bass.ds(g, 1)].rearrange("p h o -> p (h o)"),
                        pM[(q + ahead) % 2][:, :].rearrange("p (h e) -> p h e", h=HH), AX.X,
                        ALU.max).then_inc(max_done, 1)

                def step(i, q):
                    t = i * GPI + q
                    main = lives(i, q)
                    if main and layer == 0:
                        dve.wait_ge(gathered[q], i * 32 + 32)
                        dve.wait_ge(rel_ready, t + 1)
                        k = kg[:, 2 * q:2 * q + 2, :].rearrange("p s (h d) -> p s h d", h=H)
                        r = pR[:, :, :].unsqueeze(2).broadcast_to([P, 2, H, D // H])
                        nc.vector.tensor_tensor(k, k, r, ALU.add).then_inc(added, 1)
                    low_part(i, q, -1)
                    if main:
                        if layer == 0:
                            dve.wait_ge(added, t + 1)
                        else:
                            dve.wait_ge(gathered[q], i * 32 + 32)
                        dve.wait_ge(qe_ready, t + 1)
                        nc.vector.tensor_tensor(prod[:, q % 2, :], pQ[q % 2][:, :],
                                                kg[:, 2 * q:2 * q + 2, :].rearrange("p s d -> p (s d)"),
                                                ALU.mult).then_inc(prod_done, 1)
                        if lives(i, q, GPI - 1):
                            dve.wait_ge(tr_done, t + 1)
                            onehot(i, q, bass.ds(i * SPI + 2 * q + SPI, 2))
                        dve.wait_ge(prod_done, t + 1)
                        nc.vector.tensor_reduce(c.s[:, bass.ds((i * SPI + 2 * q) * H, 2 * H)],
                                                prod[:, q % 2, :].rearrange("p (g d) -> p g d", d=D // H),
                                                AX.X, ALU.add).then_inc(s_ready, 1)
                    maxima(i, q, -3)

                nc.vector.memset(sp2[:, :, :, :], 0.0).then_inc(cleared, 1)
                for q in range(GPI):
                    onehot(0, q, slice(2 * q, 2 * q + 2))
                pipeline(dve, step, 3)
                dve.wait_ge(max_done, NG)
                st = Steps(dve, joined)
                for h in range(HH):
                    st(nc.vector.tensor_tensor_scan(fw[:, h, 0:NG], c.first[:, 0:NG], mp[:, h, 0:NG], -BIG,
                                                    ALU.add, ALU.max))
                st.sync()
                for h in range(HH):
                    st(nc.vector.tensor_tensor_scan(mp[:, h, 0:NG][:, ::-1], c.final[:, 0:NG][:, ::-1],
                                                    fw[:, h, 0:NG][:, ::-1], -BIG, ALU.add, ALU.max))
                st.sync()
                joined_max = mp[:, :, 0:NG].rearrange("p h g -> p g h")
                st.link(nc.vector.tensor_copy(m2[:, :, 0, :], joined_max))
                st.link(nc.vector.tensor_tensor(m2[:, :, 1, :], joined_max, m2[:, :, 0, :], ALU.subtract))
                nc.vector.tensor_copy(c.m[:, 0, :, :, :], m2[0:BN, :, :, :]).then_inc(joined, 1)

            @block.scalar
            def _(act):
                def copy(i, q, ahead):
                    if not lives(i, q, ahead):
                        return
                    g = i * GPI + q + ahead
                    r = (q + ahead) % GPI
                    hold(act, tr_done, g + 1)
                    need(act, mask_ready, g - 3, hold)
                    need(act, qe_ready, g - 3, hold)
                    if layer == 0:
                        need(act, rel_ready, g - 3, hold)
                    rows = KINDS * BN
                    nc.scalar.activation(ohT[0:rows, r, :], pT[r % BT][0:rows, :], ACT.Copy).then_inc(ohT_ready, 1)

                def mask(i, q, ahead):
                    if not lives(i, q, ahead):
                        return
                    g = i * GPI + q + ahead
                    r = (q + ahead) % GPI
                    hold(act, ohT_ready, g + 1)
                    need(act, spread, g - 3, hold)
                    nc.scalar.activation(rhs[0:BN, r, :], ohT[0:BN, r, :], ACT.Copy, bias=-1.0).then_inc(mask_ready, 1)

                def scoresT(i, q, ahead):
                    if not lives(i, q, ahead):
                        return
                    g = i * GPI + q + ahead
                    r = (q + ahead) % GPI
                    hold(act, st_psum, g + 1)
                    nc.scalar.activation(rhs[BN:SR, r, :], pS[BN:SR, :], ACT.Copy).then_inc(sT_ready, 1)

                def high_part(i, q, ahead):
                    if not lives(i, q, ahead):
                        return
                    g = i * GPI + q + ahead
                    r = (q + ahead) % GPI
                    hold(act, s_ready, g + 1)
                    need(act, st_psum, g - 1, hold)
                    nc.scalar.activation(
                        sp2[:, r % 2, :, BN:BN + H],
                        c.s[:, bass.ds((i * SPI + 2 * (q + ahead)) * H, 2 * H)].rearrange("p (s h) -> p s h", h=H),
                        ACT.Copy).then_inc(hi_ready, 1)

                def step(i, q):
                    scoresT(i, q, -3)
                    copy(i, q, 1)
                    mask(i, q, -1)
                    high_part(i, q, -1)

                act.wait_ge(cleared, 1)
                copy(0, 0, 0)
                pipeline(act, step, 3)

            @block.tensor
            def _(pe):
                def turn(i, q, ahead):
                    if not lives(i, q, ahead):
                        return
                    g = i * GPI + q + ahead
                    r = (q + ahead) % GPI
                    hold(pe, oh_made, g + 1)
                    need(pe, ohT_ready, g + 1 - BT, hold)
                    for k in range(2):
                        last = nc.tensor.transpose(pT[r % BT][0:KINDS * BN, k * P:(k + 1) * P],
                                                   oh[:, 2 * r + k, :, :].rearrange("p k n -> p (k n)"),
                                                   c.ident_b[:, :])
                    last.then_inc(tr_done, 1)

                def q_of_edges(i, q, b):
                    if not lives(i, q):
                        return
                    t = i * GPI + q
                    pe.wait_ge(ohT_ready, t + 1)
                    need(pe, prod_done, t - 1)
                    for k in range(2):
                        for part in range(3):
                            last = nc.tensor.matmul(pQ[q % 2][:, k * D:(k + 1) * D],
                                                    ohT[0:BN, q, k * P:(k + 1) * P],
                                                    c.q[:, bass.ds(b, 1), part, :].rearrange("p o d -> p (o d)"),
                                                    start=part == 0, stop=part == 2)
                    last.then_inc(qe_ready, 1)

                def relation_of_edges(i, q):
                    if layer != 0 or not lives(i, q):
                        return
                    t = i * GPI + q
                    need(pe, added, t)
                    for k in range(2):
                        for part in range(3):
                            last = nc.tensor.matmul(pR[:, k, :], ohT[BN:P, q, k * P:(k + 1) * P],
                                                    c.rel[BN:P, part, :], start=part == 0, stop=part == 2)
                    last.then_inc(rel_ready, 1)

                def turn_scores(i, q, ahead):
                    if not lives(i, q, ahead):
                        return
                    g = i * GPI + q + ahead
                    r = (q + ahead) % GPI
                    pe.wait_ge(lo_ready, g + 1)
                    need(pe, sT_ready, g)
                    for k in range(2):
                        last = nc.tensor.transpose(pS[:, k * P:(k + 1) * P], sp2[:, r % 2, k, :], c.ident_b[:, :])
                    last.then_inc(st_psum, 1)

                def spread_scores(i, q, ahead):
                    if not lives(i, q, ahead):
                        return
                    g = i * GPI + q + ahead
                    r = (q + ahead) % GPI
                    pe.wait_ge(sT_ready, g + 1)
                    pe.wait_ge(mask_ready, g + 1)
                    need(pe, max_done, g - 1)
                    for j in range(HH):
                        last = nc.tensor.matmul(pM[r % 2][:, j * GE:(j + 1) * GE], c.spread[:, layer, j, :],
                                                rhs[:, r, :], start=True, stop=True)
                    last.then_inc(spread, 1)

                def step(i, q):
                    b = None
                    if lives(i, q):
                        b = pe.value_load(c.gb[0:1, bass.ds(i * GPI + q, 1)], min_val=0, max_val=BB - 1)
                    q_of_edges(i, q, b)
                    spread_scores(i, q, -3)
                    relation_of_edges(i, q)
                    turn(i, q, 2)
                    turn_scores(i, q, -2)

                turn(0, 0, 0)
                turn(0, 1, 0)
                pipeline(pe, step, 3)


def stage_aggregate(nc, c, sem, dram, layer):
    H = HA if layer == 0 else HB
    W = D + H
    T = f"L{layer}_sum_"
    with ExitStack() as ctx:
        def sb(name, shape, dt):
            return ctx.enter_context(nc.sbuf_tensor(T + name, shape, dt))

        def ps(name, shape, dt):
            return ctx.enter_context(nc.psum_tensor(T + name, shape, dt))

        vg = sb("vg", [P, SPI, D], F32)
        stage = [sb(f"stage{u}", [P, 4], I32) for u in range(2)]
        oh = [sb(f"oh{q}", [P, 2, BN], F32) for q in range(GPI)]
        ohT = sb("ohT", [BN, 2, GE], BF16)
        diff = sb("diff", [P, 2, 2, H], F32)
        rhs = sb("rhs", [P, 4, 2, W], F32)
        sums = c.q_place[0:BN, 0:BB * W].rearrange("p (b w) -> p b w", w=W)
        pT = [ps(f"pT{u}", [BN, GE], F32) for u in range(2)]
        pE = [ps(f"pE{u}", [P, 2, H], F32) for u in range(2)]
        pA = [ps(f"pA{u}", [BN, W], F32) for u in range(2)]

        gathered = [sem(T + f"v_gathered{q}") for q in range(GPI)]
        zeroed = sem(T + "sums_zeroed")
        oh_made = sem(T + "onehot_made")
        tr_done = sem(T + "onehot_transposed")
        ohT_ready = sem(T + "onehotT_ready")
        me_ready = sem(T + "maxima_of_edges_ready")
        diff_done = sem(T + "difference_done")
        exp_done = sem(T + "exp_done")
        v_done = sem(T + "weighted_v_done")
        agg_done = sem(T + "group_sum_done")
        acc_done = sem(T + "added_to_bucket")
        moved = sem(T + "sums_moved")

        with nc.Block() as block:

            @block.gpsimd
            def _(pool):
                gather_rows(nc, pool, sem, T, dram.v, c.rec, stage, vg, gathered, v_done)

            @block.sync
            def _(sp):
                sp.wait_ge(acc_done, NG)
                for part in range(2):
                    sp.dma_start(c.acc[part * BN:(part + 1) * BN, :, 0:W],
                                 sums.rearrange("p (t k) w -> p t k w", k=2)[:, :, part, :]
                                 ).then_inc(moved, 16)
                sp.wait_ge(moved, 32)

            @block.vector
            def _(dve):
                def onehot(r, slots):
                    nc.vector.tensor_tensor(oh[r][:, :, :], c.iota[:, 0:BN].unsqueeze(1).broadcast_to([P, 2, BN]),
                                            c.rec[:, slots, 1].unsqueeze(2).broadcast_to([P, 2, BN]),
                                            ALU.is_equal).then_inc(oh_made, 1)

                def difference(i, q):
                    if not lives(i, q):
                        return
                    t = i * GPI + q
                    dve.wait_ge(me_ready, t + 1)
                    need(dve, exp_done, t - 1)
                    nc.vector.tensor_tensor(
                        diff[:, q % 2, :, :],
                        c.s[:, bass.ds((i * SPI + 2 * q) * H, 2 * H)].rearrange("p (s h) -> p s h", h=H),
                        pE[q % 2][:, :, :], ALU.subtract).then_inc(diff_done, 1)

                def weighted(i, q, ahead):
                    if not lives(i, q, ahead):
                        return
                    g = i * GPI + q + ahead
                    r = (q + ahead) % GPI
                    dve.wait_ge(gathered[r], (i + (q + ahead - r) // GPI) * 32 + 32)
                    dve.wait_ge(exp_done, g + 1)
                    for k in range(2):
                        ins = nc.vector.tensor_tensor(
                            rhs[:, r, k, 0:D].rearrange("p (h d) -> p h d", h=H),
                            vg[:, 2 * r + k, :].rearrange("p (h d) -> p h d", h=H),
                            rhs[:, r, k, D:W].unsqueeze(2).broadcast_to([P, H, D // H]), ALU.mult)
                    ins.then_inc(v_done, 1)

                def accumulate(i, q, ahead):
                    if not lives(i, q, ahead):
                        return
                    g = i * GPI + q + ahead
                    b = dve.value_load(c.gb[0:1, bass.ds(g, 1)], min_val=0, max_val=BB - 1)
                    dve.wait_ge(agg_done, g + 1)
                    need(dve, acc_done, g)
                    row = sums[:, bass.ds(b, 1), :].rearrange("p o w -> p (o w)")
                    nc.vector.tensor_tensor(row, pA[(q + ahead) % 2][:, :], row, ALU.add).then_inc(acc_done, 1)

                def step(i, q):
                    difference(i, q)
                    weighted(i, q, -1)
                    accumulate(i, q, -2)
                    if lives(i, q, 2):
                        need(dve, agg_done, i * GPI + q - 1)
                        onehot((q + 2) % GPI, bass.ds(i * SPI + 2 * q + 4, 2))

                nc.vector.memset(sums[:, :, :], 0.0).then_inc(zeroed, 1)
                dve.wait_ge(zeroed, 1)
                onehot(0, slice(0, 2))
                onehot(1, slice(2, 4))
                pipeline(dve, step, 2)

            @block.scalar
            def _(act):
                def copy(i, q, ahead):
                    if not lives(i, q, ahead):
                        return
                    g = i * GPI + q + ahead
                    r = (q + ahead) % 2
                    hold(act, tr_done, g + 1)
                    need(act, me_ready, g - 1, hold)
                    nc.scalar.activation(ohT[:, r, :], pT[r][:, :], ACT.Copy).then_inc(ohT_ready, 1)

                def exponent(i, q):
                    if not lives(i, q):
                        return
                    t = i * GPI + q
                    hold(act, diff_done, t + 1)
                    need(act, agg_done, t - 3, hold)
                    nc.scalar.activation(rhs[:, q, :, D:W], diff[:, q % 2, :, :], ACT.Exp).then_inc(exp_done, 1)

                def step(i, q):
                    copy(i, q, 1)
                    exponent(i, q)

                copy(0, 0, 0)
                pipeline(act, step, 0)

            @block.tensor
            def _(pe):
                def turn(i, q, ahead):
                    if not lives(i, q, ahead):
                        return
                    g = i * GPI + q + ahead
                    r = (q + ahead) % GPI
                    hold(pe, oh_made, g + 1)
                    need(pe, ohT_ready, g - 1, hold)
                    for k in range(2):
                        last = nc.tensor.transpose(pT[r % 2][:, k * P:(k + 1) * P], oh[r][:, k, :], c.ident[:, :])
                    last.then_inc(tr_done, 1)

                def maxima_of_edges(i, q):
                    if not lives(i, q):
                        return
                    t = i * GPI + q
                    pe.wait_ge(ohT_ready, t + 1)
                    need(pe, diff_done, t - 1)
                    for k in range(2):
                        for part in range(2):
                            last = nc.tensor.matmul(pE[q % 2][:, k, :], ohT[:, q % 2, k * P:(k + 1) * P],
                                                    c.m[:, :, bass.ds(t, 1), part, :].rearrange("p f o h -> p f (o h)"),
                                                    start=part == 0, stop=part == 1)
                    last.then_inc(me_ready, 1)

                def group_sum(i, q, ahead):
                    if not lives(i, q, ahead):
                        return
                    g = i * GPI + q + ahead
                    r = (q + ahead) % GPI
                    pe.wait_ge(v_done, g + 1)
                    need(pe, acc_done, g - 1)
                    for k in range(2):
                        last = nc.tensor.matmul(pA[r % 2][:, :], oh[r][:, k, :], rhs[:, r, k, :],
                                                start=k == 0, stop=k == 1)
                    last.then_inc(agg_done, 1)

                def step(i, q):
                    maxima_of_edges(i, q)
                    group_sum(i, q, -2)
                    turn(i, q, 1)

                turn(0, 0, 0)
                pipeline(pe, step, 2)


def stage_output(nc, c, sem, dram, weights, layer):
    H = HA if layer == 0 else HB
    T = f"L{layer}_out_"
    Wo, bo, gamma, beta = weights
    with ExitStack() as ctx:
        def sb(name, shape, dt):
            return ctx.enter_context(nc.sbuf_tensor(T + name, shape, dt))

        def ps(name, shape, dt):
            return ctx.enter_context(nc.psum_tensor(T + name, shape, dt))

        w = sb("wo", [P, C2, D], F32)
        b = sb("bo", [P, D], F32)
        z = sb("z", [P, TB, H], F32)
        empty = sb("empty", [P, TB, H], F32)
        msg = sb("msg", [P, 2, D], F32)
        mT = [sb(f"mT{u}", [P, C2, P], F32) for u in range(2)]
        hn = sb("hn", [P, 2, D], F32)
        part = sb("part", [P, 2, D], F32)
        if layer == 0:
            vt = sb("vt", [P, 2, D], F32)
            gb = sb("gamma_beta", [P, 2, D], F32)
            y = c.q_place[:, 0:TB * D].rearrange("p (t d) -> p t d", d=D)
        pT = [ps(f"pT{u}", [P, D], F32) for u in range(2)]
        pO = [ps(f"pO{u}", [P, D], F32) for u in range(2)]

        loaded = sem(T + "w_loaded")
        steps = sem(T + "dve_steps")
        v_loaded = [sem(T + f"v_loaded{u}") for u in range(2)]
        scaled = sem(T + "scaled")
        msg_done = sem(T + "messages_done")
        mT_psum = sem(T + "messages_transposed")
        mT_ready = sem(T + "messagesT_ready")
        hn_ready = sem(T + "hn_ready")
        out_psum = sem(T + "out_psum")
        projected = sem(T + "projected")
        out_done = sem(T + "out_done")
        norm = NormSemaphores(sem, T)
        scaled_y = sem(T + "normalised")
        affine = sem(T + "affine")

        with nc.Block() as block:

            @block.sync
            def _(sp):
                sp.dma_start(w[:, :, :], Wo.rearrange("(c p) n -> p c n", p=P)).then_inc(loaded, 16)
                sp.dma_start(b[:, :], bo.rearrange("(o n) -> o n", o=1).broadcast_to([P, D])).then_inc(loaded, 16)
                if layer == 0:
                    for k, a in enumerate((gamma, beta)):
                        sp.dma_start(gb[:, k, :],
                                     a.rearrange("(o n) -> o n", o=1).broadcast_to([P, D])).then_inc(loaded, 16)
                    with sp.Fori(0, TB // 2) as i:
                        for u in range(2):
                            hold(sp, msg_done, i * 2 + u + 1)
                            sp.dma_start(vt[:, u, :], dram.v[bass.ds((i * 2 + u) * P, P), :]).then_inc(v_loaded[u], 16)

            @block.vector
            def _(dve):
                st = Steps(dve, steps)
                sums = c.acc[:, :, D:D + H]
                st(nc.vector.tensor_scalar(empty[:, :, :], sums, 0.0, None, ALU.is_equal))
                st.link(nc.vector.tensor_scalar(z[:, :, :], sums, 1e-30, None, ALU.max))
                st.link(nc.vector.reciprocal(z[:, :, :], z[:, :, :]))
                dve.wait_ge(loaded, 64 if layer == 0 else 32)
                dve.sem_inc(msg_done, 2)
                with dve.Fori(0, TB // 2) as i:
                    for u in range(2):
                        t = i * 2 + u
                        def heads(a):
                            return a.rearrange("p (h d) -> p h d", h=H)
                        def of_tile(a):
                            return a[:, bass.ds(t, 1), :].rearrange("p o h -> p (o h)").unsqueeze(2).broadcast_to(
                                [P, H, D // H])
                        acc = c.acc[:, bass.ds(t, 1), 0:D].rearrange("p o d -> p (o d)")
                        first = nc.vector.tensor_tensor(heads(msg[:, u, :]), heads(acc), of_tile(z), ALU.mult)
                        if layer == 0:
                            first.then_inc(scaled, 1)
                            dve.wait_ge(v_loaded[u], i * 16 + 16)
                            nc.vector.tensor_tensor(heads(vt[:, u, :]), heads(vt[:, u, :]), of_tile(empty),
                                                    ALU.mult).then_inc(scaled, 1)
                            dve.wait_ge(scaled, 2 * t + 2)
                            first = nc.vector.tensor_tensor(msg[:, u, :], msg[:, u, :], vt[:, u, :], ALU.add)
                        first.then_inc(msg_done, 1)
                    for u in range(2):
                        t = i * 2 + u
                        dve.wait_ge(out_psum, t + 1)
                        nc.vector.tensor_tensor(part[:, u, :], pO[u][:, :], b[:, :], ALU.add).then_inc(projected, 1)
                        dve.wait_ge(projected, t + 1)
                        if layer == 0:
                            dve.wait_ge(hn_ready, t + 1)
                            nc.vector.tensor_tensor(y[:, t, :], part[:, u, :], hn[:, u, :],
                                                    ALU.add).then_inc(out_done, 1)
                        else:
                            nc.vector.tensor_tensor(c.x[:, t, :], part[:, u, :], c.x[:, t, :],
                                                    ALU.add).then_inc(out_done, 1)
                dve.wait_ge(out_done, TB)
                if layer == 0:
                    norm_vector(nc, dve, c, norm, y)
                    with dve.Fori(0, NT) as t:
                        dve.wait_ge(scaled_y, t + 1)
                        nc.vector.tensor_tensor(y[:, t, :], y[:, t, :], gb[:, 0, :], ALU.mult).then_inc(affine, 1)
                        nc.vector.tensor_tensor(c.x[:, t, :], c.x[:, t, :], gb[:, 1, :], ALU.add).then_inc(affine, 1)
                        dve.wait_ge(affine, 3 * t + 2)
                        nc.vector.tensor_tensor(c.x[:, t, :], c.x[:, t, :], y[:, t, :], ALU.add).then_inc(affine, 1)
                    dve.wait_ge(affine, 3 * NT)

            @block.scalar
            def _(act):
                with act.Fori(0, TB // 2) as i:
                    for u in range(2):
                        t = i * 2 + u
                        hold(act, mT_psum, t + 1)
                        nc.scalar.activation(mT[u][:, :, :].rearrange("p c n -> p (c n)"), pT[u][:, :],
                                             ACT.Copy).then_inc(mT_ready, 1)
                        if layer == 0:
                            nc.scalar.activation(hn[:, u, :], c.x[:, t, :], ACT.Identity,
                                                 bias=c.shift[:, bass.ds(t, 1)],
                                                 scale=c.rstd[:, bass.ds(t, 1)]).then_inc(hn_ready, 1)
                if layer == 0:
                    norm_scalar(nc, act, norm, c)
                    act.wait_ge(norm.ready, 1)
                    with act.Fori(0, NT) as t:
                        nc.scalar.activation(y[:, t, :], y[:, t, :], ACT.Identity, bias=c.shift[:, bass.ds(t, 1)],
                                             scale=c.rstd[:, bass.ds(t, 1)]).then_inc(scaled_y, 1)

            @block.tensor
            def _(pe):
                pe.wait_ge(loaded, 64 if layer == 0 else 32)
                with pe.Fori(0, TB // 2) as i:
                    for u in range(2):
                        t = i * 2 + u
                        pe.wait_ge(msg_done, t + 3)
                        for k in range(C2):
                            last = nc.tensor.transpose(pT[u][:, k * P:(k + 1) * P], msg[:, u, k * P:(k + 1) * P],
                                                       c.ident[:, :])
                        last.then_inc(mT_psum, 1)
                    for u in range(2):
                        t = i * 2 + u
                        pe.wait_ge(mT_ready, t + 1)
                        for k in range(C2):
                            last = nc.tensor.matmul(pO[u][:, :], mT[u][:, k, :], w[:, k, :], start=k == 0,
                                                    stop=k == C2 - 1)
                        last.then_inc(out_psum, 1)


def stage_gate(nc, c, sem, dram, weights):
    T = "gate_"
    EX = EXPERTS
    gate_w, gate_b, b1 = weights
    with ExitStack() as ctx:
        def sb(name, shape, dt):
            return ctx.enter_context(nc.sbuf_tensor(T + name, shape, dt))

        def ps(name, shape, dt):
            return ctx.enter_context(nc.psum_tensor(T + name, shape, dt))

        h = sb("h", [P, TB, D], F32)
        hn = sb("hn", [P, 2, D], F32)
        gw = sb("gw", [P, C2, EX], F32)
        gb = sb("gb", [P, EX], F32)
        b1_rows = sb("b1_rows", [EX * FC, P], F32)
        hT = [sb(f"hT{u}", [P, C2, P], F32) for u in range(2)]
        zeros = sb("zeros", [P, 8 * D], F32)
        lg = sb("logits", [P, TB, EX], F32)
        one = sb("one_hot", [P, TB, EX], F32)
        tmp = sb("tmp", [P, TB, EX], F32)
        before = sb("before_tile", [P, EX, TB], F32)
        col = sb("columns", [P, 8, TB], F32)
        pT = [ps(f"pT{u}", [P, D], F32) for u in range(2)]
        pG = ps("pG", [P, TB, EX], F32)
        pC = ps("pC", [P, TB, EX], F32)
        pN = ps("pN", [P, TB, EX], F32)
        pB = ps("pB", [P, EX * FC], F32)
        loaded = sem(T + "w_loaded")
        zeroed = sem(T + "zeros_made")
        cleared = sem(T + "buffers_cleared")
        norm = NormSemaphores(sem, T)
        hn_ready = sem(T + "h_ready")
        hT_psum = sem(T + "h_transposed")
        hT_ready = sem(T + "hT_ready")
        logits_done = sem(T + "logits_done")
        b1_psum = sem(T + "b1_transposed")
        steps = sem(T + "dve_steps")
        shifted = sem(T + "logits_shifted")
        exp_done = sem(T + "exp_done")
        chosen = sem(T + "expert_chosen")
        counted = sem(T + "counted")
        placed = sem(T + "placed")
        sent = sem(T + "h_sent")

        with nc.Block() as block:

            @block.sync
            def _(sp):
                sp.dma_start(gw[:, :, :], gate_w.rearrange("(c p) e -> p c e", p=P)).then_inc(loaded, 16)
                sp.dma_start(gb[:, :], gate_b.rearrange("(o n) -> o n", o=1).broadcast_to([P, EX])).then_inc(loaded, 16)
                sp.dma_start(b1_rows[:, :], b1.rearrange("e (f p) -> (e f) p", p=P)).then_inc(loaded, 16)
                sp.wait_ge(zeroed, 1)
                for k in range(EX * CAPW // (8 * P)):
                    sp.dma_start(dram.buf[k * 8 * P:(k + 1) * 8 * P, :].rearrange("(p r) d -> p (r d)", r=8),
                                 zeros[:, :]).then_inc(cleared, 16)

            @block.gpsimd
            def _(pool):
                nc.gpsimd.memset(zeros[:, :], 0.0).then_inc(zeroed, 1)
                pool.wait_ge(placed, 1)
                pool.wait_ge(cleared, EX * CAPW // (8 * P) * 16)
                for t in range(NT):
                    nc.gpsimd.indirect_dma_start(out=dram.buf, out_offset=bass.IndirectOffsetOnAxis(
                        ap=c.place[:, 0, t:t + 1], axis=0), in_=h[:, t, :], in_offset=None).then_inc(sent, 16)
                pool.wait_ge(sent, NT * 16)

            @block.vector
            def _(dve):
                norm_vector(nc, dve, c, norm, c.x)
                st = Steps(dve, steps)
                shape = [P, TB, EX]
                def each(a):
                    return a.unsqueeze(2).broadcast_to(shape)
                numbers = c.iota[:, 0:EX].unsqueeze(1).broadcast_to(shape)
                dve.wait_ge(loaded, 48)
                dve.wait_ge(b1_psum, 1)
                st(nc.vector.tensor_copy(c.b1T[:, :], pB[:, :]))
                dve.wait_ge(logits_done, TB + 1)
                st.link(nc.vector.tensor_tensor(lg[:, :, :], pG[:, :, :], gb[:, :].unsqueeze(1).broadcast_to(shape), ALU.add))
                st.link(nc.vector.tensor_reduce(col[:, 0, :], lg[:, :, :], AX.X, ALU.max))
                nc.vector.tensor_tensor(lg[:, :, :], lg[:, :, :], each(col[:, 0, :]), ALU.subtract).then_inc(shifted, 1)
                dve.wait_ge(exp_done, 1)
                st.link(nc.vector.tensor_reduce(col[:, 1, :], lg[:, :, :], AX.X, ALU.add))
                st(nc.vector.reciprocal(col[:, 2, :], col[:, 1, :]))
                st(nc.vector.tensor_scalar(one[:, :, :], lg[:, :, :], 1.0, None, ALU.is_ge))
                st.link(nc.vector.tensor_scalar(tmp[:, :, :], numbers, -1.0, float(EX), ALU.mult, ALU.add))
                st.link(nc.vector.tensor_tensor(tmp[:, :, :], tmp[:, :, :], one[:, :, :], ALU.mult))
                st.link(nc.vector.tensor_reduce(col[:, 3, :], tmp[:, :, :], AX.X, ALU.max))
                nc.vector.tensor_tensor(one[:, :, :], tmp[:, :, :], each(col[:, 3, :]), ALU.is_equal).then_inc(chosen, 1)
                dve.wait_ge(counted, 2)
                dve.wait_ge(chosen, 1)
                for e in range(EX):
                    st(nc.vector.tensor_tensor_scan(before[:, e, :], pN[:, :, e], c.zero[:, 0:TB], 0.0, ALU.add,
                                                    ALU.add))
                st.sync()
                st.link(nc.vector.tensor_tensor(tmp[:, :, :], before[:, :, :].rearrange("p e t -> p t e"),
                                                pN[:, :, :], ALU.subtract))
                st.link(nc.vector.tensor_tensor(tmp[:, :, :], tmp[:, :, :], pC[:, :, :], ALU.add))
                st.link(nc.vector.tensor_tensor(tmp[:, :, :], tmp[:, :, :], one[:, :, :], ALU.mult))
                st.link(nc.vector.tensor_reduce(col[:, 4, :], tmp[:, :, :], AX.X, ALU.add))
                st(nc.vector.tensor_scalar(col[:, 0, :], col[:, 3, :], -float(CAPW), float(CAPW * EX), ALU.mult, ALU.add))
                st(nc.vector.tensor_scalar(col[:, 1, :], col[:, 4, :], float(CAP), None, ALU.is_le))
                st(nc.vector.tensor_scalar(col[:, 5, :], col[:, 4, :], float(CAP), -1.0, ALU.min, ALU.add))
                st.sync()
                st(nc.vector.tensor_tensor(c.weight[:, :], col[:, 2, :], col[:, 1, :], ALU.mult))
                st.link(nc.vector.tensor_tensor(col[:, 5, :], col[:, 5, :], col[:, 0, :], ALU.add))
                st(nc.vector.tensor_copy(c.place[:, 1, :], col[:, 5, :]))
                st.link(nc.vector.tensor_tensor(col[:, 6, :], col[:, 5, :], c.spare[:, :], ALU.subtract))
                st.link(nc.vector.tensor_tensor(col[:, 6, :], col[:, 6, :], col[:, 1, :], ALU.mult))
                st.link(nc.vector.tensor_tensor(col[:, 7, :], col[:, 6, :], c.spare[:, :], ALU.add))
                nc.vector.tensor_copy(c.place[:, 0, :], col[:, 7, :]).then_inc(placed, 1)

            @block.scalar
            def _(act):
                norm_scalar(nc, act, norm, c)
                act.wait_ge(norm.ready, 1)
                with act.Fori(0, TB // 2) as i:
                    for u in range(2):
                        t = i * 2 + u
                        nc.scalar.activation(h[:, t, :], c.x[:, t, :], ACT.Identity, bias=c.shift[:, bass.ds(t, 1)],
                                             scale=c.rstd[:, bass.ds(t, 1)])
                        nc.scalar.activation(hn[:, u, :], c.x[:, t, :], ACT.Identity, bias=c.shift[:, bass.ds(t, 1)],
                                             scale=c.rstd[:, bass.ds(t, 1)]).then_inc(hn_ready, 1)
                        hold(act, hT_psum, t + 1)
                        hold(act, logits_done, t + 1)
                        nc.scalar.activation(hT[u][:, :, :].rearrange("p c n -> p (c n)"), pT[u][:, :],
                                             ACT.Copy).then_inc(hT_ready, 1)
                act.wait_ge(shifted, 1)
                nc.scalar.activation(lg[:, :, :], lg[:, :, :], ACT.Exp).then_inc(exp_done, 1)

            @block.tensor
            def _(pe):
                pe.wait_ge(loaded, 48)
                nc.tensor.transpose(pB[:, :], b1_rows[:, :], c.ident[0:EX * FC, 0:EX * FC]).then_inc(b1_psum, 1)
                pe.sem_inc(logits_done, 1)
                with pe.Fori(0, TB // 2) as i:
                    for u in range(2):
                        t = i * 2 + u
                        pe.wait_ge(hn_ready, t + 1)
                        for k in range(C2):
                            last = nc.tensor.transpose(pT[u][:, k * P:(k + 1) * P],
                                                       hn[:, u, k * P:(k + 1) * P],
                                                       c.ident[:, :])
                        last.then_inc(hT_psum, 1)
                        pe.wait_ge(hT_ready, t + 1)
                        for k in range(C2):
                            last = nc.tensor.matmul(pG[:, bass.ds(t, 1), :].rearrange("p o e -> p (o e)"),
                                                    hT[u][:, k, :], gw[:, k, :], start=k == 0, stop=k == C2 - 1)
                        last.then_inc(logits_done, 1)
                pe.wait_ge(chosen, 1)
                for out, m in ((pC, c.upto), (pN, c.ones)):
                    nc.tensor.matmul(out[:, :, :].rearrange("p t e -> p (t e)"), m[:, :],
                                     one[:, :, :].rearrange("p t e -> p (t e)"), start=True,
                                     stop=True).then_inc(counted, 1)


def stage_experts(nc, c, sem, dram, weights):
    T = "experts_"
    EX = EXPERTS
    w1_d, w2_d, b2_d = weights
    A = CAPW // P
    with ExitStack() as ctx:
        def sb(name, shape, dt):
            return ctx.enter_context(nc.sbuf_tensor(T + name, shape, dt))

        def ps(name, shape, dt):
            return ctx.enter_context(nc.psum_tensor(T + name, shape, dt))

        w1 = [sb(f"w1_{u}", [P, C2, FF], F32) for u in range(2)]
        w2 = [sb(f"w2_{u}", [P, FC, D], F32) for u in range(2)]
        b2 = [sb(f"b2_{u}", [P, D], F32) for u in range(2)]
        xe = [sb(f"x_{u}", [P, A, D], F32) for u in range(2)]
        xT = sb("xT", [P, C2, CAPW], F32)
        hT = sb("hT", [P, FC, CAPW], F32)
        y = [sb(f"y_{u}", [P, A, D], F32) for u in range(2)]
        pX = [ps(f"pX{k}", [P, CAPW], F32) for k in range(C2)]
        pH = [ps(f"pH{u}", [P, CAPW], F32) for u in range(2)]
        pY = [ps(f"pY{u}", [P, D], F32) for u in range(2)]
        loaded = [sem(T + f"loaded{u}") for u in range(2)]
        x_psum = sem(T + "x_transposed")
        xT_ready = sem(T + "xT_ready")
        h_psum = sem(T + "hidden_psum")
        relu_done = sem(T + "relu_done")
        y_psum = sem(T + "y_psum")
        y_done = sem(T + "y_done")
        stored = [sem(T + f"stored{u}") for u in range(2)]

        with nc.Block() as block:

            @block.sync
            def _(sp):
                def load(e, u):
                    sp.dma_start(w1[u][:, :, :],
                                 w1_d[bass.ds(e, 1), :, :].rearrange("o (c p) f -> p (o c) f", p=P)).then_inc(loaded[u], 16)
                    sp.dma_start(w2[u][:, :, :],
                                 w2_d[bass.ds(e, 1), :, :].rearrange("o (f p) d -> p (o f) d", p=P)).then_inc(loaded[u], 16)
                    sp.dma_start(b2[u][:, :], b2_d[bass.ds(e, 1), :].broadcast_to([P, D])).then_inc(loaded[u], 16)
                    sp.dma_start(xe[u][:, :, :], dram.buf[bass.ds(e * CAPW, CAPW), :].rearrange(
                        "(a p) d -> p a d", p=P)).then_inc(loaded[u], 16)

                def store(e, u, n):
                    hold(sp, y_done, n + 2)
                    sp.dma_start(dram.ybuf[bass.ds(e * CAPW, CAPW), :].rearrange("(a p) d -> p a d", p=P),
                                 y[u][:, :, :]).then_inc(stored[u], 16)

                load(0, 0)
                load(1, 1)
                with sp.Fori(0, EX // 2 - 1) as i:
                    for u in range(2):
                        store(i * 2 + u, u, (i * 2 + u + 1) * A)
                        load(i * 2 + u + 2, u)
                for u in range(2):
                    sp.wait_ge(y_done, (EX - 2 + u + 1) * A + 2)
                    sp.dma_start(dram.ybuf[(EX - 2 + u) * CAPW:(EX - 1 + u) * CAPW, :].rearrange("(a p) d -> p a d", p=P),
                                 y[u][:, :, :]).then_inc(stored[u], 16)
                for u in range(2):
                    sp.wait_ge(stored[u], EX // 2 * 16)

            @block.tensor
            def _(pe):
                with pe.Fori(0, EX // 2) as i:
                    for u in range(2):
                        e = i * 2 + u
                        pe.wait_ge(loaded[u], (i + 1) * 64)
                        for k in range(C2):
                            for a in range(A):
                                last = nc.tensor.transpose(pX[k][:, a * P:(a + 1) * P],
                                                           xe[u][:, a, k * P:(k + 1) * P], c.ident[:, :])
                        last.then_inc(x_psum, 1)
                        pe.wait_ge(xT_ready, e + 1)
                        for f in range(FC):
                            pe.wait_ge(relu_done, e * FC + f + 1)
                            for k in range(C2):
                                last = nc.tensor.matmul(pH[f % 2][:, :], w1[u][:, k, f * P:(f + 1) * P], xT[:, k, :],
                                                        start=k == 0, stop=k == C2 - 1)
                            last.then_inc(h_psum, 1)
                        pe.wait_ge(relu_done, e * FC + FC + 2)
                        for a in range(A):
                            pe.wait_ge(y_done, e * A + a + 1)
                            for f in range(FC):
                                last = nc.tensor.matmul(pY[a % 2][:, :], hT[:, f, a * P:(a + 1) * P], w2[u][:, f, :],
                                                        start=f == 0, stop=f == FC - 1)
                            last.then_inc(y_psum, 1)

            @block.scalar
            def _(act):
                act.sem_inc(relu_done, 2)
                with act.Fori(0, EX // 2) as i:
                    for u in range(2):
                        e = i * 2 + u
                        hold(act, x_psum, e + 1)
                        nc.scalar.activation(xT[:, 0, :], pX[0][:, :], ACT.Copy)
                        nc.scalar.activation(xT[:, 1, :], pX[1][:, :], ACT.Copy).then_inc(xT_ready, 1)
                        for f in range(FC):
                            hold(act, h_psum, e * FC + f + 1)
                            nc.scalar.activation(hT[:, f, :], pH[f % 2][:, :], ACT.Relu,
                                                 bias=c.b1T[:, bass.ds(e * FC + f, 1)]).then_inc(relu_done, 1)

            @block.vector
            def _(dve):
                dve.sem_inc(y_done, 2)
                def pair(i, first=False):
                    for u in range(2):
                        e = i * 2 + u
                        if not first:
                            dve.wait_ge(stored[u], i * 16)
                        for a in range(A):
                            dve.wait_ge(y_psum, e * A + a + 1)
                            nc.vector.tensor_tensor(y[u][:, a, :], pY[a % 2][:, :], b2[u][:, :],
                                                    ALU.add).then_inc(y_done, 1)

                pair(0, first=True)
                with dve.Fori(1, EX // 2) as i:
                    pair(i)


def stage_combine(nc, c, sem, dram):
    T = "combine_"
    RING = 5
    LIMIT = 3.4028234e38
    with ExitStack() as ctx:
        def sb(name, shape, dt):
            return ctx.enter_context(nc.sbuf_tensor(T + name, shape, dt))

        y = sb("y", [P, RING, D], F32)
        ok = sb("ok", [P, RING, D], I32)
        clean = sb("clean", [P, RING, D], F32)
        limit = sb("limit", [P, 2, D], F32)
        got = [sem(T + f"got{r}") for r in range(RING)]
        made = sem(T + "limits_made")
        weighted = sem(T + "weighted")
        steps = sem(T + "dve_steps")
        used = sem(T + "used")
        with nc.Block() as block:

            @block.gpsimd
            def _(pool):
                for t in range(NT):
                    if t >= RING:
                        pool.wait_ge(used, t - RING + 1)
                    nc.gpsimd.indirect_dma_start(
                        out=y[:, t % RING, :], out_offset=None, in_=dram.ybuf,
                        in_offset=bass.IndirectOffsetOnAxis(ap=c.place[:, 1, t:t + 1], axis=0)).then_inc(got[t % RING], 16)

            @block.scalar
            def _(act):
                for t in range(NT):
                    act.wait_ge(got[t % RING], (t // RING + 1) * 16)
                    nc.scalar.activation(y[:, t % RING, :], y[:, t % RING, :], ACT.Copy,
                                         scale=c.weight[:, t:t + 1]).then_inc(weighted, 1)

            @block.vector
            def _(dve):
                nc.vector.memset(limit[:, 0, :], 1e4).then_inc(made, 1)
                nc.vector.memset(limit[:, 1, :], -1e4).then_inc(made, 1)
                dve.wait_ge(made, 2)
                st = Steps(dve, steps)
                for t in range(NT):
                    r = t % RING
                    dve.wait_ge(weighted, t + 1)
                    st(nc.vector.memset(clean[:, r, :], 0.0))
                    st.link(nc.vector.tensor_tensor(ok[:, r, :], y[:, r, :], y[:, r, :], ALU.is_equal))
                    st.link(nc.vector.copy_predicated(clean[:, r, :], ok[:, r, :], y[:, r, :]))
                    st.link(nc.vector.tensor_scalar(ok[:, r, :], clean[:, r, :], LIMIT, None, ALU.is_gt))
                    st.link(nc.vector.copy_predicated(clean[:, r, :], ok[:, r, :], limit[:, 0, :]))
                    st.link(nc.vector.tensor_scalar(ok[:, r, :], clean[:, r, :], -LIMIT, None, ALU.is_lt))
                    st.link(nc.vector.copy_predicated(clean[:, r, :], ok[:, r, :], limit[:, 1, :]))
                    nc.vector.tensor_tensor(c.x[:, t, :], c.x[:, t, :], clean[:, r, :], ALU.add).then_inc(used, 1)
                dve.wait_ge(used, NT)


KEEP = N // 2 - 1
G4 = 4 * P


def stage_last(nc, c, sem, dram, weights, out):
    T = "last_"
    wr_d, br_d, w1_d, b1_d, w2_d, b2_d = weights
    NP = TB * P
    with ExitStack() as ctx:
        def sb(name, shape, dt):
            return ctx.enter_context(nc.sbuf_tensor(T + name, shape, dt))

        def ps(name, shape, dt):
            return ctx.enter_context(nc.psum_tensor(T + name, shape, dt))

        h = [sb(f"h{u}", [P, D], F32) for u in range(2)]
        hT = sb("hT", [P, C2, NP], F32)
        wr = sb("wr", [P, C2], F32)
        br = sb("br", [P, 1], F32)
        w1 = sb("w1", [P, C2, FF], F32)
        w2 = sb("w2", [P, FC, D], F32)
        b1_rows = sb("b1_rows", [FC, P], F32)
        b1T = sb("b1T", [P, FC], F32)
        b2 = sb("b2", [1, D], F32)
        gT = sb("gT", [P, FC, G4], F32)
        y = sb("y", [P, TB, D], F32)
        wcol = sb("wcol", [P, TB], F32)
        wrow = sb("wrow", [TB, P], F32)
        wall = sb("wall", [P, N], F32)
        earlier = sb("earlier", [P, 2 * NP], BF16)
        flags = sb("flags", [P, N], F32)
        rank = sb("rank", [P, 2, TB], F32)
        coef = sb("coef", [P, 3, TB], F32)
        pT = [ps(f"pT{u}", [P, D], F32) for u in range(2)]
        pW = ps("pW", [P, TB], F32)
        pS = ps("pS", [P, P], F32)
        pH = [ps(f"pH{u}", [P, G4], F32) for u in range(2)]
        pY = [ps(f"pY{u}", [P, D], F32) for u in range(2)]
        loaded = sem(T + "w_loaded")
        norm = NormSemaphores(sem, T)
        mask_made = sem(T + "mask_made")
        h_ready = sem(T + "h_ready")
        h_psum = sem(T + "h_transposed")
        hT_ready = sem(T + "hT_ready")
        h_added = sem(T + "h_added")
        w_psum = sem(T + "w_psum")
        w_ready = sem(T + "w_ready")
        row_psum = sem(T + "w_transposed")
        row_ready = sem(T + "w_row_ready")
        b1_ready = sem(T + "b1_ready")
        row_out = sem(T + "w_row_stored")
        row_in = sem(T + "w_row_loaded")
        steps = sem(T + "dve_steps")
        hid_psum = sem(T + "hidden_psum")
        gelu_done = sem(T + "gelu_done")
        y_psum = sem(T + "y_psum")
        y_ready = sem(T + "y_ready")
        final = sem(T + "final")
        stored = sem(T + "stored")
        turns = [(i, 4) for i in range(NT // 4)] + [(NT // 4, NT % 4)]

        with nc.Block() as block:

            @block.sync
            def _(sp):
                sp.dma_start(wr[:, :], wr_d.rearrange("(c p) o -> p (c o)", p=P),
                             allow_slow_non_contiguous=True).then_inc(loaded, 16)
                sp.dma_start(br[:, :], br_d.rearrange("(o n) -> o n", o=1).broadcast_to([P, 1])).then_inc(loaded, 16)
                sp.dma_start(b1_rows[:, :], b1_d.rearrange("(f p) -> f p", p=P)).then_inc(loaded, 16)
                sp.dma_start(b2[:, :], b2_d.rearrange("(o n) -> o n", o=1)).then_inc(loaded, 16)
                sp.dma_start(w1[:, :, :], w1_d.rearrange("(c p) f -> p c f", p=P)).then_inc(loaded, 16)
                sp.dma_start(w2[:, :, :], w2_d.rearrange("(f p) d -> p f d", p=P)).then_inc(loaded, 16)
                sp.wait_ge(row_ready, 1)
                sp.dma_start(dram.wrow.rearrange("(t p) -> t p", p=P), wrow[:, :]).then_inc(row_out, 16)
                sp.wait_ge(row_out, 16)
                sp.dma_start(wall[:, :], dram.wrow[0:N].rearrange("(o n) -> o n", o=1).broadcast_to([P, N])).then_inc(row_in, 16)
                for t in range(0, NT - 1, 4):
                    sp.wait_ge(final, t + 4)
                    sp.dma_start(out[t * P:(t + 4) * P, :].rearrange("(t p) d -> p t d", p=P),
                                 y[:, t:t + 4, :]).then_inc(stored, 16)
                sp.wait_ge(final, NT)
                sp.dma_start(out[(NT - 1) * P:N, :], y[0:LAST, NT - 1, :]).then_inc(stored, 16)
                sp.wait_ge(stored, (NT - 1) // 4 * 16 + 16)

            @block.gpsimd
            def _(pool):
                nc.gpsimd.memset(earlier[:, :], 1.0).then_inc(mask_made, 1)
                pool.wait_ge(mask_made, 1)
                nc.gpsimd.affine_select(out=earlier[:, :], in_=earlier[:, :], compare_op=ALU.is_gt, fill=0.0,
                                        base=NP, pattern=[[-1, 2 * NP]], channel_multiplier=1).then_inc(mask_made, 1)
                with pool.Fori(0, TB // 2) as i:
                    for u in range(2):
                        t = i * 2 + u
                        hold(pool, h_ready, t + 1)
                        nc.gpsimd.tensor_tensor(c.x[:, t, :], c.x[:, t, :], h[u][:, :], ALU.add).then_inc(h_added, 1)

            @block.vector
            def _(dve):
                dve.sem_inc(h_added, 2)
                norm_vector(nc, dve, c, norm, c.x)
                st = Steps(dve, steps)
                dve.wait_ge(w_psum, TB)
                nc.vector.tensor_scalar(wcol[:, :], pW[:, :], br[:, 0:1], None, ALU.add).then_inc(w_ready, 1)
                dve.wait_ge(row_psum, 1)
                nc.vector.tensor_copy(wrow[:, :], pS[0:TB, :]).then_inc(row_ready, 1)
                dve.wait_ge(row_in, 16)
                dve.wait_ge(mask_made, 2)
                with dve.Fori(0, NT) as t:
                    nc.vector.tensor_scalar(flags[:, :], wall[:, :], wcol[:, bass.ds(t, 1)], 0.0, ALU.is_gt, ALU.add,
                                            accum_out=rank[:, 0, bass.ds(t, 1)]).then_inc(steps, 1)
                    dve.wait_ge(steps, t * 2 + 1)
                    nc.vector.scalar_tensor_tensor(flags[:, :], wall[:, :], wcol[:, bass.ds(t, 1)],
                                                   earlier[:, bass.ds(NP - t * P, N)], ALU.is_equal, ALU.mult,
                                                   accum_out=rank[:, 1, bass.ds(t, 1)]).then_inc(steps, 1)
                    dve.wait_ge(steps, t * 2 + 2)
                st.n = 2 * NT
                st.link(nc.vector.tensor_tensor(coef[:, 0, 0:NT], rank[:, 0, 0:NT], rank[:, 1, 0:NT], ALU.add))
                st.link(nc.vector.tensor_scalar(coef[:, 1, 0:NT], coef[:, 0, 0:NT], float(KEEP), None, ALU.is_lt))
                st.link(nc.vector.tensor_tensor(coef[:, 2, 0:NT], coef[:, 1, 0:NT], wcol[:, 0:NT], ALU.mult))
                dve.wait_ge(h_added, TB + 2)
                with dve.Fori(0, NT) as t:
                    dve.wait_ge(y_ready, t + 1 + 2)
                    nc.vector.scalar_tensor_tensor(y[:, t, :], y[:, t, :], coef[:, 2, bass.ds(t, 1)], c.x[:, t, :],
                                                   ALU.mult, ALU.add).then_inc(final, 1)

            @block.scalar
            def _(act):
                norm_scalar(nc, act, norm, c)
                act.wait_ge(norm.ready, 1)
                act.wait_ge(b1_ready, 1)
                nc.scalar.activation(b1T[:, :], pS[:, 0:FC], ACT.Copy).then_inc(b1_ready, 1)
                with act.Fori(0, TB // 2) as i:
                    for u in range(2):
                        t = i * 2 + u
                        hold(act, h_added, t + 1)
                        nc.scalar.activation(h[u][:, :], c.x[:, t, :], ACT.Identity, bias=c.shift[:, bass.ds(t, 1)],
                                             scale=c.rstd[:, bass.ds(t, 1)]).then_inc(h_ready, 1)
                        hold(act, h_psum, t + 1)
                        nc.scalar.activation(hT[:, :, bass.ds(t * P, P)],
                                             pT[u][:, :].rearrange("p (c n) -> p c n", n=P),
                                             ACT.Copy).then_inc(hT_ready, 1)
                act.sem_inc(gelu_done, 2)
                act.sem_inc(y_ready, 2)

                def mlp(g, tiles, wait):
                    for f in range(FC):
                        wait(act, hid_psum, g * FC + f + 1)
                        nc.scalar.activation(gT[:, f, 0:tiles * P], pH[f % 2][:, 0:tiles * P], ACT.Gelu_apprx_tanh,
                                             bias=b1T[:, f:f + 1]).then_inc(gelu_done, 1)
                    for a in range(tiles):
                        wait(act, y_psum, g * 4 + a + 1)
                        at = g * 4 + a
                        dst = y[:, at, :]
                        nc.scalar.activation(dst, pY[a % 2][:, :], ACT.Copy).then_inc(y_ready, 1)

                with act.Fori(0, NT // 4) as g:
                    mlp(g, 4, hold)
                mlp(NT // 4, NT % 4, lambda e, s, v: e.wait_ge(s, v))

            @block.tensor
            def _(pe):
                pe.wait_ge(loaded, 96)
                nc.tensor.transpose(pS[:, 0:FC], b1_rows[:, :], c.ident[0:FC, 0:FC]).then_inc(b1_ready, 1)
                with pe.Fori(0, TB // 2) as i:
                    for u in range(2):
                        t = i * 2 + u
                        pe.wait_ge(h_ready, t + 1)
                        for k in range(C2):
                            last = nc.tensor.transpose(pT[u][:, k * P:(k + 1) * P], h[u][:, k * P:(k + 1) * P],
                                                       c.ident[:, :])
                        last.then_inc(h_psum, 1)
                pe.wait_ge(hT_ready, TB)
                for t in range(TB):
                    for k in range(C2):
                        last = nc.tensor.matmul(pW[:, t:t + 1], hT[:, k, t * P:(t + 1) * P], wr[:, k:k + 1],
                                                start=k == 0, stop=k == C2 - 1)
                    last.then_inc(w_psum, 1)
                pe.wait_ge(w_ready, 1)
                pe.wait_ge(b1_ready, 2)
                nc.tensor.transpose(pS[0:TB, :], wcol[:, :], c.ident[:, :]).then_inc(row_psum, 1)

                def mlp(g, tiles):
                    cols = bass.ds(g * G4, tiles * P)
                    for f in range(FC):
                        pe.wait_ge(gelu_done, g * FC + f + 1)
                        for k in range(C2):
                            last = nc.tensor.matmul(pH[f % 2][:, 0:tiles * P], w1[:, k, f * P:(f + 1) * P],
                                                    hT[:, k, cols], start=k == 0, stop=k == C2 - 1)
                        last.then_inc(hid_psum, 1)
                    pe.wait_ge(gelu_done, g * FC + FC + 2)
                    for a in range(tiles):
                        pe.wait_ge(y_ready, g * 4 + a + 1)
                        nc.tensor.matmul(pY[a % 2][:, :], c.ones[0:1, :], b2[:, :], start=True, stop=False)
                        for f in range(FC):
                            last = nc.tensor.matmul(pY[a % 2][:, :], gT[:, f, a * P:(a + 1) * P], w2[:, f, :],
                                                    start=False, stop=f == FC - 1)
                        last.then_inc(y_psum, 1)

                with pe.Fori(0, NT // 4) as g:
                    mlp(g, 4)
                mlp(NT // 4, NT % 4)


class Dram:
    pass


def gnn_ffn_kernel(nc, a, out):
    with ExitStack() as ctx:
        def sb(name, shape, dt):
            return ctx.enter_context(nc.sbuf_tensor(name, shape, dt))

        open_sems = []

        def sem(name):
            open_sems.append(nc.alloc_semaphore(name))
            return open_sems[-1]

        def stage(program, *args):
            program(nc, c, sem, *args)
            nc.clear_and_free_semaphores(open_sems)
            open_sems.clear()
            nc.all_engine_barrier()

        c, dram = Consts(), Dram()
        dram.k = nc.dram_tensor("k_table", [TB * P, D], F32, kind="Internal").ap()
        dram.v = nc.dram_tensor("v_table", [TB * P, D], F32, kind="Internal").ap()
        dram.buf = nc.dram_tensor("expert_in", [EXPERTS * CAPW + TB * P, D], F32, kind="Internal").ap()
        dram.ybuf = nc.dram_tensor("expert_out", [EXPERTS * CAPW, D], F32, kind="Internal").ap()
        dram.wrow = nc.dram_tensor("node_weights", [TB * P], F32, kind="Internal").ap()
        dram.list = nc.dram_tensor("edge_list", [P * SW, 4], F32, kind="Internal").ap()
        c.ident = sb("ident", [P, P], F32)
        c.ident_b = sb("ident_b", [P, P], BF16)
        c.before = sb("before", [P, P], F32)
        c.upto = sb("upto", [P, P], F32)
        c.ones = sb("ones", [P, P], F32)
        c.spread = sb("spread", [SR, 2, HB // 2, P], BF16)
        c.iota_i = sb("iota_i", [P, 256], I32)
        c.iota = sb("iota", [P, 256], F32)
        c.x = sb("x", [P, TB, D], F32)
        c.stats = sb("stats", [P, TB, 6], F32)
        c.norm = sb("norm", [P, 4, TB], F32)
        c.rstd = sb("rstd", [P, TB], F32)
        c.shift = sb("shift", [P, TB], F32)
        c.zero = sb("zero", [P, TB], F32)
        c.spare = sb("spare", [P, TB], F32)
        c.spare_i = sb("spare_i", [P, TB], I32)
        attention = ctx.enter_context(ExitStack())

        def sb(name, shape, dt):
            return attention.enter_context(nc.sbuf_tensor(name, shape, dt))

        c.rec = sb("rec", [P, SW, 4], F32)
        c.gb = sb("group_bucket", [P, GW], I32)
        c.first = sb("first_of_bucket", [P, GW], F32)
        c.final = sb("last_of_bucket", [P, GW], F32)
        c.rel = sb("rel_parts", [P, 3, NREL], BF16)
        c.q_place = sb("q_place", [P, max(BK * EC, BB * 3 * D // 2)], F32)
        c.q = c.q_place[0:BN, 0:BB * 3 * D // 2].bitcast(BF16).rearrange("p (b k d) -> p b k d", k=3, d=D)
        stage(stage_constants, a["x"])
        for layer in range(2):
            tag = f"L{layer}_gnn_"
            ws = [a[tag + n] for n in ("Wq", "bq", "Wk", "bk", "Wv", "bv")]
            ws += [a[tag + "rel_w"], a[tag + "query_emb"]] if layer == 0 else [None, None]
            ends = (a["src"], a["dst"]) if layer == 0 else (a["dst"], a["src"])
            stage(stage_place_and_project, (*ends, a["edge_type_64"]), ws, dram, layer)
            lay = ctx.enter_context(ExitStack())
            c.s = lay.enter_context(nc.sbuf_tensor(f"scores{layer}", [P, SW * HB], F32))
            c.m = lay.enter_context(nc.sbuf_tensor(f"maxima{layer}", [BN, 2, NG, 2, (HA, HB)[layer] // 2], BF16))
            stage(stage_scores, dram, layer)
            with ExitStack() as agg:
                c.acc = agg.enter_context(nc.sbuf_tensor(f"sums{layer}", [P, TB, D + HB], F32))
                stage(stage_aggregate, dram, layer)
                ws = [a[tag + "Wo"], a[tag + "bo"]]
                ws += [a[tag + "gamma"], a[tag + "beta"]] if layer == 0 else [None, None]
                stage(stage_output, dram, ws, layer)
            lay.close()
            if layer == 0:
                with ExitStack() as moe:
                    c.b1T = moe.enter_context(nc.sbuf_tensor("b1T", [P, EXPERTS * FC], F32))
                    c.place = moe.enter_context(nc.sbuf_tensor("place", [P, 2, TB], I32))
                    c.weight = moe.enter_context(nc.sbuf_tensor("weight", [P, TB], F32))
                    stage(stage_gate, dram, (a["L0_ffn_gate_w"], a["L0_ffn_gate_b"], a["L0_ffn_b1"]))
                    stage(stage_experts, dram, (a["L0_ffn_w1"], a["L0_ffn_w2"], a["L0_ffn_b2"]))
                    stage(stage_combine, dram)
        attention.close()
        stage(stage_last, dram, [a["L1_ffn_" + n] for n in ("wr", "br", "w1", "b1", "w2", "b2")], out)


_INS = ['x', 'src', 'dst', 'edge_type_64', 'L0_gnn_query_emb', 'L0_gnn_Wq', 'L0_gnn_bq', 'L0_gnn_Wk', 'L0_gnn_bk',
        'L0_gnn_Wv', 'L0_gnn_bv', 'L0_gnn_rel_w', 'L0_gnn_Wo', 'L0_gnn_bo', 'L0_gnn_gamma', 'L0_gnn_beta',
        'L0_ffn_gate_w', 'L0_ffn_gate_b', 'L0_ffn_w1', 'L0_ffn_b1', 'L0_ffn_w2', 'L0_ffn_b2', 'L1_gnn_Wq',
        'L1_gnn_bq', 'L1_gnn_Wk', 'L1_gnn_bk', 'L1_gnn_Wv', 'L1_gnn_bv', 'L1_gnn_Wo', 'L1_gnn_bo',
        'L1_ffn_attention_mask', 'L1_ffn_wr', 'L1_ffn_br', 'L1_ffn_w1', 'L1_ffn_b1', 'L1_ffn_w2', 'L1_ffn_b2']


def laid_out(inputs):
    a = {name: np.ascontiguousarray(inputs[name]) for name in _INS}
    for n in ("Wq", "Wk", "Wv"):
        w = a["L1_gnn_" + n]
        a["L1_gnn_" + n] = np.ascontiguousarray(w.reshape(D, D // HB, HB).transpose(0, 2, 1).reshape(D, D))
        b = a["L1_gnn_b" + n[1]]
        a["L1_gnn_b" + n[1]] = np.ascontiguousarray(b.reshape(D // HB, HB).transpose(1, 0).reshape(D))
    w = a["L1_gnn_Wo"]
    a["L1_gnn_Wo"] = np.ascontiguousarray(w.reshape(D // HB, HB, D).transpose(1, 0, 2).reshape(D, D))
    return a


def kernel(**inputs):
    import concourse.bacc as bacc
    from concourse.bass_utils import run_bass_kernel_spmd

    nc = bacc.Bacc("TRN2", target_bir_lowering=False, num_devices=1)
    arrays, args = {}, {}
    for name, a in laid_out(inputs).items():
        arrays[f"in_{name}"] = a
        args[name] = nc.dram_tensor(f"in_{name}", a.shape, mybir.dt.from_np(a.dtype), kind="ExternalInput").ap()
    out = nc.dram_tensor("out_x", [N, D], F32, kind="ExternalOutput").ap()
    gnn_ffn_kernel(nc, args, out)
    r = run_bass_kernel_spmd(nc, [arrays], core_ids=[0])
    return r.results[0]["out_x"]
```

```python
from contextlib import ExitStack

import concourse.bass as bass
from concourse import mybir
import numpy as np

F32 = mybir.dt.float32
BF16 = mybir.dt.bfloat16
I32 = mybir.dt.int32
ALU = mybir.AluOpType
ACT = mybir.ActivationFunctionType
AX = mybir.AxisListType

P = 128
N = 3125
D = 256
C2 = D // P
E = 50000
NT = -(-N // P)
LAST = N - (NT - 1) * P
TB = NT + 1
EC = -(-E // P)
EFULL = E // EC
EREST = E - EFULL * EC
BN = 64
NB = -(-N // BN)
BB = 2 * TB
BK = NB + 1
GE = 2 * P
NG = (E - NB) // GE + NB
NS = 2 * NG
SPI = 8
GPI = SPI // 2
TURNS = NS // SPI
SW = NS + SPI
GW = SW // 2
NREL = 64
BIG = 1.0e30
assert NS % SPI == 0 and EREST > 0 and TB % 2 == 0

SCAT = 17
HALF = (12, 11)
EARLY = 3
BY_OUTPUT = 6
BY_GATE = BY_OUTPUT + 2
assert SCAT * sum(HALF) == EC
HA, HB = 4, 8
SR = BN + 2 * HB
EXPERTS, CAP, FF = 8, 489, 1024
CAPW = 512
FC = FF // P


class Steps:

    def __init__(self, eng, sem, start=0):
        self.eng, self.sem, self.n = eng, sem, start

    def __call__(self, ins):
        self.n += 1
        return ins.then_inc(self.sem, 1)

    def sync(self):
        self.eng.wait_ge(self.sem, self.n)

    def link(self, ins):
        self(ins)
        self.sync()


def hold(eng, sem, value):
    eng.wait_ge(sem, value)
    eng.nop(nofuse=True)


def need(eng, sem, value, wait=None):
    if not isinstance(value, int) or value > 0:
        (wait or eng.wait_ge)(*(() if wait is None else (eng,)), sem, value)


def pipeline(eng, step, ends):
    for q in range(GPI):
        step(0, q)
    with eng.Fori(1, TURNS) as i:
        for q in range(GPI):
            step(i, q)
    for q in range(ends):
        step(TURNS, q)


def tile_pipeline(eng, step):
    with eng.Fori(0, TB // 2 - 1) as i:
        for u in range(2):
            step(i * 2 + u, u)
    for u in range(2):
        step(TB - 2 + u, u)


def is_tile(t):
    return not isinstance(t, int) or t < TB


def lives(i, q, ahead=0):
    return not isinstance(i, int) or 0 <= i * GPI + q + ahead < NG


class Consts:
    pass


def stage_constants(nc, c, sem, x):
    made = sem("constants_made")
    pooled = sem("constants_pool")
    got = sem("x_loaded")
    summed = sem("constants_summed")
    halves = [(layer, part) for layer in range(2) for part in range(2)]
    with ExitStack() as ctx:
        member = ctx.enter_context(nc.sbuf_tensor("member", [SR, 2, BN], BF16))
        pick = ctx.enter_context(nc.sbuf_tensor("pick", [SR, 2, 2, HB // 2, 2, BN], BF16))
        _constants(nc, c, x, made, pooled, got, summed, halves, member, pick)


def _constants(nc, c, x, made, pooled, got, summed, halves, member, pick):
    with nc.Block() as block:

        @block.gpsimd
        def _(pool):
            st = Steps(pool, pooled)
            st(nc.gpsimd.memset(c.ident[:, :], 0.0))
            st(nc.gpsimd.memset(c.before[:, :], 1.0))
            st(nc.gpsimd.memset(c.upto[:, :], 1.0))
            st(nc.gpsimd.memset(c.ones[:, :], 1.0))
            st(nc.gpsimd.memset(member[:, :, :], 1.0))
            st(nc.gpsimd.memset(pick[:, :, :, :, :, :], 1.0))
            st(nc.gpsimd.memset(c.zero[:, :], 0.0))
            st(nc.gpsimd.iota(c.spare_i[:, :], pattern=[[P, TB]], base=EXPERTS * CAPW, channel_multiplier=1))
            st(nc.gpsimd.iota(c.iota_i[:, :], pattern=[[1, 256]], base=0, channel_multiplier=0))
            st.sync()
            st(nc.gpsimd.affine_select(out=c.ident[:, :], in_=c.ident[:, :], compare_op=ALU.not_equal, fill=1.0,
                                       base=0, pattern=[[-1, P]], channel_multiplier=1))
            st(nc.gpsimd.affine_select(out=c.before[:, :], in_=c.before[:, :], compare_op=ALU.is_gt, fill=0.0,
                                       base=0, pattern=[[1, P]], channel_multiplier=-1))
            st(nc.gpsimd.affine_select(out=c.upto[:, :], in_=c.upto[:, :], compare_op=ALU.is_ge, fill=0.0,
                                       base=0, pattern=[[1, P]], channel_multiplier=-1))
            st(nc.gpsimd.affine_select(out=member[:, :, :], in_=member[:, :, :], compare_op=ALU.is_equal, fill=0.0,
                                       base=0, pattern=[[0, 2], [-1, BN]], channel_multiplier=1))
            for layer, part in halves:
                HH = (HA, HB)[layer] // 2
                a = pick[:, layer, part, 0:HH, :, :]
                st(nc.gpsimd.affine_select(out=a, in_=a, compare_op=ALU.is_equal, fill=0.0, base=-BN - part * HB,
                                           pattern=[[-1, HH], [-HH, 2], [0, BN]], channel_multiplier=1))
            st.sync()
            nc.gpsimd.tensor_copy(c.spare[:, :], c.spare_i[:, :]).then_inc(made, 1)
            nc.gpsimd.tensor_copy(c.iota[:, :], c.iota_i[:, :]).then_inc(made, 1)

        @block.vector
        def _(dve):
            nc.vector.memset(c.x[:, NT - 1:TB, :], 0.0).then_inc(got, 1)
            dve.wait_ge(pooled, 17)
            nc.vector.tensor_copy(c.ident_b[:, :], c.ident[:, :]).then_inc(made, 1)
            st = Steps(dve, summed)
            for layer in range(2):
                for j in range((HA, HB)[layer] // 2):
                    out = c.spread[:, layer, j, :]
                    st.link(nc.vector.tensor_tensor(out, pick[:, layer, 0, j, :, :].rearrange("p f n -> p (f n)"),
                                                    pick[:, layer, 1, j, :, :].rearrange("p f n -> p (f n)"), ALU.add))
                    st.link(nc.vector.scalar_tensor_tensor(out, member[:, :, :].rearrange("p f n -> p (f n)"), BIG,
                                                           out, ALU.mult, ALU.add))

        @block.sync
        def _(sp):
            sp.dma_start(c.x[:, 0:NT - 1, :],
                         x[0:(NT - 1) * P, :].rearrange("(t p) d -> p t d", p=P)).then_inc(got, 16)
            sp.wait_ge(got, 17)
            sp.dma_start(c.x[0:LAST, NT - 1, :], x[(NT - 1) * P:N, :]).then_inc(got, 16)
            sp.wait_ge(got, 33)
            sp.wait_ge(made, 3)


class NormSemaphores:
    def __init__(self, sem, tag):
        self.stats = sem(tag + "norm_stats")
        self.var = sem(tag + "norm_var")
        self.std = sem(tag + "norm_std")
        self.ready = sem(tag + "norm_ready")


def norm_vector(nc, dve, c, norm, x):
    with dve.Fori(0, TB) as t:
        nc.vector.bn_stats(c.stats[:, t, :], x[:, t, :]).then_inc(norm.stats, 1)
    dve.wait_ge(norm.stats, TB)
    st = Steps(dve, norm.stats, TB)
    mean_e, m2_e, mean_o, m2_o = (c.stats[:, :, k] for k in (1, 2, 4, 5))
    st(nc.vector.tensor_tensor(c.norm[:, 0, :], mean_e, mean_o, ALU.add))
    st(nc.vector.tensor_tensor(c.norm[:, 1, :], mean_e, mean_o, ALU.subtract))
    st(nc.vector.tensor_tensor(c.norm[:, 2, :], m2_e, m2_o, ALU.add))
    st.sync()
    st.link(nc.vector.tensor_tensor(c.norm[:, 1, :], c.norm[:, 1, :], c.norm[:, 1, :], ALU.mult))
    st.link(nc.vector.scalar_tensor_tensor(c.norm[:, 2, :], c.norm[:, 1, :], D / 4.0, c.norm[:, 2, :],
                                           ALU.mult, ALU.add))
    nc.vector.tensor_scalar(c.norm[:, 3, :], c.norm[:, 2, :], 1.0 / D, 1e-5, ALU.mult, ALU.add).then_inc(norm.var, 1)
    dve.wait_ge(norm.std, 1)
    st.link(nc.vector.reciprocal(c.rstd[:, :], c.norm[:, 1, :]))
    nc.vector.scalar_tensor_tensor(c.shift[:, :], c.norm[:, 0, :], -0.5, c.rstd[:, :], ALU.mult,
                                   ALU.mult).then_inc(norm.ready, 1)


def norm_scalar(nc, act, norm, c):
    act.wait_ge(norm.var, 1)
    nc.scalar.activation(c.norm[:, 1, :], c.norm[:, 3, :], ACT.Sqrt).then_inc(norm.std, 1)


class PlacingSemaphores:

    def __init__(self, sem, tag):
        self.staged = sem(tag + "records_staged")
        self.scattered = [sem(tag + f"records_scattered{u}") for u in range(2)]


def placing_buffers(sb):
    return ([sb(f"stage_i{u}", [P, HALF[u]], I32) for u in range(2)],
            [sb(f"stage_r{u}", [P, HALF[u], 4], F32) for u in range(2)])


def place_records(nc, pool, sems, buffers, source, out, first, end, began=None):
    stage_i, stage_r = buffers
    record, row_i = source

    def turn(i, fresh=False):
        for u in range(2):
            col = i * sum(HALF) + u * HALF[0]
            if not fresh:
                hold(pool, sems.scattered[u], (i - zero) * (16 * HALF[u]))
            nc.gpsimd.tensor_copy(stage_i[u][:, :], row_i[:, bass.ds(col, HALF[u])]).then_inc(sems.staged, 1)
            nc.gpsimd.tensor_copy(stage_r[u][:, :, :], record[:, bass.ds(col, HALF[u]), :]).then_inc(sems.staged, 1)
            hold(pool, sems.staged, (i - zero) * 4 + u * 2 + 2)
            for j in range(HALF[u]):
                nc.gpsimd.indirect_dma_start(
                    out=out, out_offset=bass.IndirectOffsetOnAxis(ap=stage_i[u][:, j:j + 1], axis=0),
                    in_=stage_r[u][:, j, :], in_offset=None).then_inc(sems.scattered[u], 16)

    zero = first if began is None else began
    if began is None:
        turn(first, fresh=True)
        first += 1
    with pool.Fori(first, end) as i:
        turn(i)


def stage_place_and_project(nc, c, sem, edges, weights, dram, layer):
    H = HA if layer == 0 else HB
    T = f"L{layer}_"
    with ExitStack() as ctx:
        def sb(name, shape, dt):
            return ctx.enter_context(nc.sbuf_tensor(T + name, shape, dt))

        def ps(name, shape, dt):
            return ctx.enter_context(nc.psum_tensor(T + name, shape, dt))

        w = sb("wqkv", [P, C2, 3 * D], F32)
        bias = sb("bqkv", [P, 3 * D], F32)
        room = sb("room", [P, BK * EC // 2], F32)
        ends = np.cumsum([0, 2 * D, C2 * P, C2 * P, 6 * D, 2 * D, 3 * D])
        hn, hT0, hT1, qkv, rest, qp = (room[:, lo:hi] for lo, hi in zip(ends[:-1].tolist(), ends[1:].tolist()))
        hn = hn.rearrange("p (u d) -> p u d", u=2)
        hT = [a.rearrange("p (c n) -> p c n", c=C2) for a in (hT0, hT1)]
        qkv = qkv.rearrange("p (u d) -> p u d", u=2)
        rest = rest.rearrange("p (u d) -> p u d", u=2)
        qp = qp.bitcast(BF16).rearrange("p (u k d) -> p u k d", u=2, k=3)
        pT = [ps(f"pT{u}", [P, D], F32) for u in range(2)]
        pQK = ps("pQK", [P, 2, 2 * D], F32)
        pV = [ps(f"pV{u}", [P, D], F32) for u in range(2)]
        if layer == 0:
            rel_in = sb("rel_in", [P, NREL], F32)
            rel_rest = sb("rel_rest", [P, NREL], F32)
            q_col = sb("q_col", [P, C2], F32)
            q_cols = sb("q_cols", [P, C2, P], F32)
        if layer == 0:
            stage_i, stage_r = placing_buffers(sb)
            dst_i = sb("dst_i", [P, EC], I32)
            src_i = sb("src_i", [P, EC], I32)
            lo_i = sb("lo_i", [P, EC], I32)
            hi_i = sb("hi_i", [P, EC], I32)
            hi_f = sb("hi_f", [P, EC], F32)
            record = [sb("record", [P, EC, 4], F32), c.record]
            row_i = [sb("row_i", [P, EC], I32), c.row_i]
            typ_i = c.row_i
            pos, at, lane = hi_f, hi_i, lo_i
            is_b = room[:, :].bitcast(BF16).rearrange("p (b e) -> p b e", b=BK)
            rank = c.q_place[:, 0:BK * EC].rearrange("p (b e) -> p b e", b=BK)
            count = sb("count", [P, BK], F32)
            small = sb("small", [P, 6, BK], F32)
            small_i = sb("small_i", [P, 2, BK], I32)
            later = is_b[:, :, :].rearrange("p b e -> p (b e)")[:, 0:GW * NB].rearrange("p (g b) -> p g b", b=NB)
            blank = c.rec
            gb_f = sb("gb_f", [P, GW], F32)
            pC = ps("pC", [P, 2, BK], F32)

        loaded = sem(T + "w_loaded")
        edges_loaded = sem(T + "edges_loaded")
        edges_blank = sem(T + "edges_blank")
        blank_made = sem(T + "blank_made")
        blank_stored = sem(T + "blank_stored")
        v = sem(T + "dve_steps")
        counted = sem(T + "counted")
        summed = sem(T + "summed")
        placed = sem(T + "placed")
        list_in = sem(T + "list_in")
        place = PlacingSemaphores(sem, T)
        weights_ready = sem(T + "weights_ready")
        query_summed = sem(T + "query_summed")
        norm = NormSemaphores(sem, T)
        hn_ready = sem(T + "hn_ready")
        hT_psum = sem(T + "hT_psum")
        hT_ready = sem(T + "hT_ready")
        qkv_psum = sem(T + "qkv_psum")
        biased = sem(T + "biased")
        tile_steps = sem(T + "tile_steps")
        split = sem(T + "q_split")
        stored = [sem(T + f"stored{u}") for u in range(2)]
        q_stored = [sem(T + f"q_stored{u}") for u in range(2)]
        Wq, bq, Wk, bk, Wv, bv, rel, q_emb = weights

        with nc.Block() as block:

            @block.sync
            def _(sp):
                if layer == 0:
                    src, dst, typ = edges
                    sp.wait_ge(edges_blank, 3)
                    for tile, a in ((dst_i, dst), (src_i, src), (typ_i, typ)):
                        sp.dma_start(tile[0:EFULL, :],
                                     a[0:EFULL * EC].rearrange("(p e) -> p e", p=EFULL)).then_inc(edges_loaded, 16)
                        sp.dma_start(tile[EFULL:EFULL + 1, 0:EREST],
                                     a[EFULL * EC:E].rearrange("(p e) -> p e", p=1)).then_inc(edges_loaded, 16)
                for k, a in enumerate((Wq, Wk, Wv)):
                    sp.dma_start(w[:, :, k * D:(k + 1) * D],
                                 a.rearrange("(c p) n -> p c n", p=P)).then_inc(loaded, 16)
                for k, a in enumerate((bq, bk, bv)):
                    sp.dma_start(bias[:, k * D:(k + 1) * D],
                                 a.rearrange("(o n) -> o n", o=1).broadcast_to([P, D])).then_inc(loaded, 16)
                if layer == 0:
                    sp.wait_ge(blank_made, 3)
                    for a in dram.list:
                        sp.dma_start(a.rearrange("(p s) f -> p (s f)", p=P),
                                     blank[:, :, :].rearrange("p s f -> p (s f)")).then_inc(blank_stored, 16)
                    sp.dma_start(q_col[:, :], q_emb.rearrange("(c p) -> p c", p=P), allow_slow_non_contiguous=True).then_inc(loaded, 16)
                    sp.dma_start(rel_in[BN:P, :], rel).then_inc(loaded, 16)
                with sp.Fori(0, TB // 2) as i:
                    for u in range(2):
                        hold(sp, biased, i * 2 + u + 3)
                        rows = bass.ds((i * 2 + u) * P, P)
                        sp.dma_start(dram.k[rows, :], qkv[:, u, D:2 * D]).then_inc(stored[u], 16)
                        sp.dma_start(dram.v[rows, :], qkv[:, u, 2 * D:3 * D]).then_inc(stored[u], 16)
                        hold(sp, split, i * 2 + u + 1)
                        for part in range(2):
                            sp.dma_start(c.q[:, bass.ds(i * 4 + u * 2 + part, 1), :, :].rearrange("p o k d -> p (o k d)"),
                                         qp[part * BN:(part + 1) * BN, u, :, :].rearrange("p k d -> p (k d)")
                                         ).then_inc(q_stored[u], 16)
                for u in range(2):
                    sp.wait_ge(stored[u], TB // 2 * 32)
                    sp.wait_ge(q_stored[u], TB // 2 * 32)
                if layer == 0:
                    for u in range(2):
                        sp.wait_ge(place.scattered[u], SCAT * HALF[u] * 16)
                sp.dma_start(c.rec[:, :, :].rearrange("p s f -> p (s f)"),
                             dram.list[layer].rearrange("(p s) f -> p (s f)", p=P)).then_inc(list_in, 16)
                sp.wait_ge(list_in, 16)

            @block.gpsimd
            def _(pool):
                if layer != 0:
                    return
                nc.gpsimd.memset(dst_i[:, :], NB * BN).then_inc(edges_blank, 1)
                nc.gpsimd.memset(src_i[:, :], NB * BN).then_inc(edges_blank, 1)
                nc.gpsimd.memset(typ_i[:, :], 0).then_inc(edges_blank, 1)
                nc.gpsimd.memset(blank[:, :, 0], 0.0).then_inc(blank_made, 1)
                nc.gpsimd.memset(blank[:, :, 1], 200.0).then_inc(blank_made, 1)
                nc.gpsimd.memset(blank[:, :, 2:4], 100.0).then_inc(blank_made, 1)
                pool.wait_ge(blank_stored, 32)
                pool.wait_ge(placed, 1)
                place_records(nc, pool, place, (stage_i, stage_r), (record[0], row_i[0]), dram.list[0], 0, EARLY)
                pool.wait_ge(placed, 2)
                place_records(nc, pool, place, (stage_i, stage_r), (record[0], row_i[0]), dram.list[0], EARLY, SCAT, began=0)

            @block.vector
            def _(dve):
                st = Steps(dve, v)

                def positions(k, key_i, other_i, parts):
                    st(nc.vector.tensor_scalar(lo_i[:, :], key_i[:, :], BN - 1, None, ALU.bitwise_and))
                    st(nc.vector.tensor_scalar(hi_i[:, :], key_i[:, :], 6, None, ALU.arith_shift_right))
                    st(nc.vector.tensor_copy(record[k][:, :, 0].bitcast(I32), other_i[:, :]))
                    st.sync()
                    st(nc.vector.tensor_copy(record[k][:, :, 1], lo_i[:, :]))
                    st.link(nc.vector.tensor_copy(hi_f[:, :], hi_i[:, :]))
                    st.link(nc.vector.tensor_tensor(is_b[:, :, :],
                                                    hi_f[:, :].unsqueeze(1).broadcast_to([P, BK, EC]),
                                                    c.iota[:, 0:BK].unsqueeze(2).broadcast_to([P, BK, EC]),
                                                    ALU.is_equal))
                    flat = is_b[:, :, :].rearrange("p b e -> p (b e)")
                    st.link(nc.vector.tensor_tensor_scan(rank.rearrange("p b e -> p (b e)"), flat, flat,
                                                         0.0, ALU.add, ALU.bypass))
                    ends = rank[:, :, EC - 1]
                    st(nc.vector.tensor_copy(count[:, 0:1], ends[:, 0:1]))
                    st(nc.vector.tensor_tensor(count[:, 1:BK], ends[:, 1:BK], ends[:, 0:BK - 1], ALU.subtract))
                    st.sync()
                    nc.vector.tensor_tensor(small[:, 0, :], count[:, :], ends, ALU.subtract).then_inc(counted, 1)
                    dve.wait_ge(summed, 2 * k + 2)
                    dve.wait_ge(counted, k + 1)
                    st(nc.vector.tensor_tensor(small[:, 1, :], small[:, 0, :], pC[:, 0, :], ALU.add))
                    st.link(nc.vector.tensor_scalar(small_i[:, 0, :], pC[:, 1, :], float(GE - 1), None, ALU.add))
                    st.link(nc.vector.tensor_scalar(small_i[:, 1, :], small_i[:, 0, :], 8, None,
                                                    ALU.arith_shift_right))
                    st.link(nc.vector.tensor_copy(small[:, 2, :], small_i[:, 1, :]))
                    st.link(nc.vector.tensor_tensor_scan(small[:, 3, :], small[:, 2, :], small[:, 2, :], 0.0,
                                                         ALU.add, ALU.bypass))
                    st.link(nc.vector.tensor_tensor(small[:, 4, :], small[:, 3, :], small[:, 2, :], ALU.subtract))
                    st.link(nc.vector.tensor_scalar(small[:, 5, :], small[:, 4, :], float(GE), -1.0,
                                                    ALU.mult, ALU.add))
                    st.link(nc.vector.tensor_tensor(small[:, 4, :], small[:, 5, :], small[:, 1, :], ALU.add))
                    for at_first, at_end in parts:
                        n = at_end - at_first
                        cols = slice(at_first, at_end)
                        some = rank[:, :, cols]
                        st.link(nc.vector.tensor_tensor(some, some, small[:, 4, :].unsqueeze(2).broadcast_to([P, BK, n]),
                                                        ALU.add))
                        st.link(nc.vector.tensor_tensor(some, some, is_b[:, :, cols], ALU.mult))
                        st.link(nc.vector.tensor_reduce(pos[:, cols], some.rearrange("p b e -> p e b"), AX.X, ALU.add))
                        st.link(nc.vector.tensor_copy(at[:, cols], pos[:, cols]))
                        st(nc.vector.tensor_scalar(lane[:, cols], at[:, cols], P - 1, None, ALU.bitwise_and))
                        st.link(nc.vector.tensor_scalar(row_i[k][:, cols], at[:, cols], 7, None, ALU.arith_shift_right))
                        st.link(nc.vector.scalar_tensor_tensor(pos[:, cols], lane[:, cols], float(SW),
                                                               row_i[k][:, cols], ALU.mult, ALU.add))
                        nc.vector.tensor_copy(row_i[k][:, cols], pos[:, cols]).then_inc(placed, 1)
                    st.link(nc.vector.tensor_tensor(later,
                                                    small[:, 3, 0:NB].unsqueeze(1).broadcast_to([P, GW, NB]),
                                                    c.iota[:, 0:GW].unsqueeze(2).broadcast_to([P, GW, NB]),
                                                    ALU.is_le))
                    st.link(nc.vector.tensor_reduce(gb_f[:, :], later, AX.X, ALU.add))
                    st(nc.vector.tensor_copy(c.gb[k][:, :], gb_f[:, :]))
                    st(nc.vector.memset(c.first[k][:, :], -BIG))
                    st(nc.vector.memset(c.final[k][:, :], -BIG))
                    st.sync()
                    st(nc.vector.tensor_tensor(c.first[k][:, 1:NG], gb_f[:, 1:NG], gb_f[:, 0:NG - 1], ALU.not_equal))
                    st(nc.vector.tensor_tensor(c.final[k][:, 0:NG - 1], gb_f[:, 1:NG], gb_f[:, 0:NG - 1],
                                               ALU.not_equal))
                    st.sync()
                    st(nc.vector.tensor_scalar(c.first[k][:, 1:NG], c.first[k][:, 1:NG], -BIG, None, ALU.mult))
                    st(nc.vector.tensor_scalar(c.final[k][:, 0:NG - 1], c.final[k][:, 0:NG - 1], -BIG, None, ALU.mult))
                    st.sync()

                if layer == 0:
                    dve.wait_ge(edges_loaded, 96)
                    for k in range(2):
                        st(nc.vector.tensor_copy(record[k][:, :, 2], typ_i[:, :]))
                        st(nc.vector.memset(record[k][:, :, 3], 0.0))
                    early = EARLY * sum(HALF)
                    positions(0, dst_i, src_i, ((0, early), (early, EC)))
                    positions(1, src_i, dst_i, ((0, EC),))
                if layer == 0:
                    dve.wait_ge(loaded, 128)
                    st.link(nc.vector.tensor_scalar(rel_in[BN:P, :], rel_in[BN:P, :], 0.2, None, ALU.mult))
                    st.link(nc.vector.tensor_copy(c.rel[BN:P, 0, :], rel_in[BN:P, :]))
                    st.link(nc.vector.tensor_tensor(rel_rest[BN:P, :], rel_in[BN:P, :], c.rel[BN:P, 0, :], ALU.subtract))
                    st.link(nc.vector.tensor_copy(c.rel[BN:P, 1, :], rel_rest[BN:P, :]))
                    st(nc.vector.tensor_tensor(c.rel[BN:P, 2, :], rel_rest[BN:P, :], c.rel[BN:P, 1, :], ALU.subtract))
                    st(nc.vector.tensor_scalar(q_cols[:, :, :],
                                               q_col[:, :].unsqueeze(2).broadcast_to([P, C2, P]), 0.1, None,
                                               ALU.mult))
                else:
                    dve.wait_ge(loaded, 96)
                scale = float(D // H) ** -0.5
                st(nc.vector.tensor_scalar(w[:, :, 0:D], w[:, :, 0:D], scale, None, ALU.mult))
                st(nc.vector.tensor_scalar(bias[:, 0:D], bias[:, 0:D], scale, None, ALU.mult))
                st.sync()
                dve.sem_inc(weights_ready, 1)
                norm_vector(nc, dve, c, norm, c.x)
                if layer == 0:
                    dve.wait_ge(query_summed, 2)
                    st(nc.vector.tensor_tensor(bias[:, 0:2 * D], pQK[:, 0, :], bias[:, 0:2 * D], ALU.add))
                    st(nc.vector.tensor_tensor(bias[:, 2 * D:], pV[0][:, :], bias[:, 2 * D:], ALU.add))
                    st.sync()
                dve.sem_inc(biased, 2)
                def pair(i, first=False):
                    for u in range(2):
                        t = i * 2 + u
                        tick = i * 8 + u * 4
                        if not first:
                            dve.wait_ge(stored[u], i * 32)
                            dve.wait_ge(q_stored[u], i * 32)
                        dve.wait_ge(qkv_psum, t + 3)
                        nc.vector.tensor_tensor(qkv[:, u, 0:2 * D], pQK[:, u, :], bias[:, 0:2 * D],
                                                ALU.add).then_inc(tile_steps, 1)
                        nc.vector.tensor_tensor(qkv[:, u, 2 * D:], pV[u][:, :], bias[:, 2 * D:],
                                                ALU.add).then_inc(biased, 1)
                        dve.wait_ge(tile_steps, tick + 1)
                        nc.vector.tensor_copy(qp[:, u, 0, :], qkv[:, u, 0:D]).then_inc(tile_steps, 1)
                        dve.wait_ge(tile_steps, tick + 2)
                        nc.vector.tensor_tensor(rest[:, u, :], qkv[:, u, 0:D], qp[:, u, 0, :],
                                                ALU.subtract).then_inc(tile_steps, 1)
                        dve.wait_ge(tile_steps, tick + 3)
                        nc.vector.tensor_copy(qp[:, u, 1, :], rest[:, u, :]).then_inc(tile_steps, 1)
                        dve.wait_ge(tile_steps, tick + 4)
                        nc.vector.tensor_tensor(qp[:, u, 2, :], rest[:, u, :], qp[:, u, 1, :],
                                                ALU.subtract).then_inc(split, 1)

                pair(0, first=True)
                with dve.Fori(1, TB // 2) as i:
                    pair(i)

            @block.scalar
            def _(act):
                norm_scalar(nc, act, norm, c)
                act.wait_ge(norm.ready, 1)

                def normalised(t, u):
                    nc.scalar.activation(hn[:, u, :], c.x[:, t, :], ACT.Identity, bias=c.shift[:, bass.ds(t, 1)],
                                         scale=c.rstd[:, bass.ds(t, 1)]).then_inc(hn_ready, 1)

                def copy(t, u):
                    hold(act, hT_psum, t + 1)
                    hold(act, qkv_psum, t + 1)
                    nc.scalar.activation(hT[u], pT[u][:, :].rearrange("p (c n) -> p c n", c=C2),
                                         ACT.Copy).then_inc(hT_ready, 1)

                def step(t, u):
                    if is_tile(t + 2):
                        normalised(t + 2, u)
                    if is_tile(t + 1):
                        copy(t + 1, 1 - u)

                normalised(0, 0)
                normalised(1, 1)
                copy(0, 0)
                tile_pipeline(act, step)

            @block.tensor
            def _(pe):
                if layer == 0:
                    for k in range(2):
                        pe.wait_ge(counted, k + 1)
                        for out, m in ((pC[:, 0, :], c.before), (pC[:, 1, :], c.ones)):
                            nc.tensor.matmul(out, m[:, :], count[:, :], start=True, stop=True).then_inc(summed, 1)
                pe.wait_ge(weights_ready, 1)
                if layer == 0:
                    for out, lo, hi in ((pQK[:, 0, :], 0, 2 * D), (pV[0][:, :], 2 * D, 3 * D)):
                        for k in range(C2):
                            last = nc.tensor.matmul(out, q_cols[:, k, :], w[:, k, lo:hi], start=k == 0, stop=k == C2 - 1)
                        last.then_inc(query_summed, 1)
                pe.sem_inc(qkv_psum, 2)

                def turn(t, u):
                    pe.wait_ge(hn_ready, t + 1)
                    for k in range(C2):
                        last = nc.tensor.transpose(pT[u][:, k * P:(k + 1) * P], hn[:, u, k * P:(k + 1) * P],
                                                   c.ident[:, :])
                    last.then_inc(hT_psum, 1)

                def step(t, u):
                    if is_tile(t + 1):
                        turn(t + 1, 1 - u)
                    pe.wait_ge(hT_ready, t + 1)
                    pe.wait_ge(biased, t + 1)
                    for out, lo, hi in ((pQK[:, u, :], 0, 2 * D), (pV[u][:, :], 2 * D, 3 * D)):
                        for k in range(C2):
                            last = nc.tensor.matmul(out, hT[u][:, k, :], w[:, k, lo:hi], start=k == 0,
                                                    stop=k == C2 - 1)
                    last.then_inc(qkv_psum, 1)

                turn(0, 0)
                tile_pipeline(pe, step)


def gather_rows(nc, pool, sem, T, table, rec, stage, ring, gathered, used):
    staged = sem(T + "indices_staged")

    def turn(i, first=False):
        for half in range(2):
            if not first:
                hold(pool, used, i * GPI + 2 * half - 2)
            nc.gpsimd.tensor_copy(stage[half][:, :],
                                  rec[:, bass.ds(i * SPI + half * 4, 4), 0].bitcast(I32)).then_inc(staged, 1)
            hold(pool, staged, i * 2 + half + 1)
            for q in (2 * half, 2 * half + 1):
                for k in range(2):
                    nc.gpsimd.indirect_dma_start(
                        out=ring[:, 2 * q + k, :], out_offset=None, in_=table,
                        in_offset=bass.IndirectOffsetOnAxis(ap=stage[half][:, 2 * (q % 2) + k:2 * (q % 2) + k + 1],
                                                            axis=0)).then_inc(gathered[q], 16)

    turn(0, first=True)
    with pool.Fori(1, TURNS) as i:
        turn(i)


def stage_scores(nc, c, sem, dram, layer):
    H = HA if layer == 0 else HB
    HH = H // 2
    KINDS = 2 if layer == 0 else 1
    OWN = 1 if layer == 0 else 2
    T = f"L{layer}_score_"
    with ExitStack() as ctx:
        def sb(name, shape, dt):
            return ctx.enter_context(nc.sbuf_tensor(T + name, shape, dt))

        def ps(name, shape, dt):
            return ctx.enter_context(nc.psum_tensor(T + name, shape, dt))

        kg = sb("kg", [P, SPI, D], F32)
        stage = [sb(f"stage{u}", [P, 4], I32) for u in range(2)]
        oh = sb("oh", [P, SPI, KINDS, BN], BF16)
        ohT = sb("ohT", [P, GPI, GE], BF16)
        prod = sb("prod", [P, 2, 2 * D], F32)
        junk = sb("junk", [P, H, D // H], F32)
        sp2 = sb("sp2", [P, 2, 2, SR], BF16)
        rhs = sb("spread_rhs", [SR, GPI, GE], BF16)
        mp = sb("mp", [P, HH, GW], F32)
        fw = sb("fw", [P, HH, GW], F32)
        m2 = sb("m2", [P, NG, 2, HH], BF16)
        BT = 2 if layer == 0 else 1
        pT = [ps(f"pT{u}", [P, GE], BF16) for u in range(BT)]
        if layer == 0:
            pR = ps("pR", [P, 2, NREL], F32)
        pS = ps("pS", [SR, GE], BF16)
        pQ = [ps(f"pQ{u}", [P, 2 * D], F32) for u in range(2)]
        pM = [ps(f"pM{u}", [P, HH * GE], F32) for u in range(2)]

        gathered = [sem(T + f"k_gathered{q}") for q in range(GPI)]
        cleared = sem(T + "cleared")
        oh_made = sem(T + "onehot_made")
        tr_done = sem(T + "onehot_transposed")
        ohT_ready = sem(T + "onehotT_ready")
        mask_ready = sem(T + "mask_ready")
        qe_ready = sem(T + "q_of_edges_ready")
        rel_ready = sem(T + "relation_of_edges_ready")
        added = sem(T + "relation_added")
        prod_done = sem(T + "product_done")
        s_ready = sem(T + "scores_ready")
        half_summed = sem(T + "other_slot_summed")
        hi_ready = sem(T + "score_high_ready")
        lo_ready = sem(T + "score_low_ready")
        st_psum = sem(T + "scores_transposed")
        sT_ready = sem(T + "scoresT_ready")
        spread = sem(T + "scores_spread")
        max_done = sem(T + "maxima_done")
        joined = sem(T + "maxima_joined")
        moved = sem(T + "maxima_moved")

        with nc.Block() as block:

            @block.gpsimd
            def _(pool):
                gather_rows(nc, pool, sem, T, dram.k, c.rec, stage, kg, gathered, prod_done)

            @block.sync
            def _(sp):
                sp.wait_ge(joined, 2 * HH + 2)
                sp.dma_start(c.m[:, 1, :, :, :], m2[BN:P, :, :, :]).then_inc(moved, 16)
                sp.wait_ge(moved, 16)

            @block.vector
            def _(dve):
                def onehot(i, q, slots):
                    nc.vector.tensor_tensor(oh[:, 2 * q:2 * q + 2, :, :],
                                            c.iota[:, 0:BN].unsqueeze(1).unsqueeze(1).broadcast_to([P, 2, KINDS, BN]),
                                            c.rec[:, slots, 1:1 + KINDS].unsqueeze(3).broadcast_to([P, 2, KINDS, BN]),
                                            ALU.is_equal).then_inc(oh_made, 1)

                def low_part(i, q, ahead):
                    if not lives(i, q, ahead):
                        return
                    r = (q + ahead) % GPI
                    dve.wait_ge(hi_ready, i * GPI + q + ahead + 1)
                    nc.vector.tensor_tensor(
                        sp2[:, r % 2, :, BN + HB:BN + HB + H],
                        c.s[:, bass.ds((i * SPI + 2 * (q + ahead)) * H, 2 * H)].rearrange("p (s h) -> p s h", h=H),
                        sp2[:, r % 2, :, BN:BN + H], ALU.subtract).then_inc(lo_ready, 1)

                def maxima(i, q, ahead):
                    if not lives(i, q, ahead):
                        return
                    g = i * GPI + q + ahead
                    dve.wait_ge(spread, g + 1)
                    nc.vector.tensor_reduce(
                        mp[:, :, bass.ds(g, 1)].rearrange("p h o -> p (h o)"),
                        pM[(q + ahead) % 2][:, :].rearrange("p (h e) -> p h e", h=HH), AX.X,
                        ALU.max).then_inc(max_done, 1)

                def step(i, q):
                    t = i * GPI + q
                    main = lives(i, q)
                    if main and layer == 0:
                        dve.wait_ge(gathered[q], i * 32 + 32)
                        dve.wait_ge(rel_ready, t + 1)
                        k = kg[:, 2 * q:2 * q + 2, :].rearrange("p s (h d) -> p s h d", h=H)
                        r = pR[:, :, :].unsqueeze(2).broadcast_to([P, 2, H, D // H])
                        nc.vector.tensor_tensor(k, k, r, ALU.add).then_inc(added, 1)
                    low_part(i, q, -1)
                    if main:
                        if layer == 0:
                            dve.wait_ge(added, t + 1)
                        else:
                            dve.wait_ge(gathered[q], i * 32 + 32)
                        dve.wait_ge(qe_ready, t + 1)
                        if layer == 0:
                            need(dve, half_summed, t - 1)
                        nc.vector.tensor_tensor(prod[:, q % 2, :], pQ[q % 2][:, :],
                                                kg[:, 2 * q:2 * q + 2, :].rearrange("p s d -> p (s d)"),
                                                ALU.mult).then_inc(prod_done, 1)
                        if lives(i, q, GPI - 1):
                            dve.wait_ge(tr_done, t + 1)
                            onehot(i, q, bass.ds(i * SPI + 2 * q + SPI, 2))
                        dve.wait_ge(prod_done, t + 1)
                        nc.vector.tensor_reduce(c.s[:, bass.ds((i * SPI + 2 * q) * H, OWN * H)],
                                                prod[:, q % 2, 0:OWN * D].rearrange("p (g d) -> p g d", d=D // H),
                                                AX.X, ALU.add).then_inc(s_ready, 1)
                    maxima(i, q, -3)

                nc.vector.memset(sp2[:, :, :, :], 0.0).then_inc(cleared, 1)
                for q in range(GPI):
                    onehot(0, q, slice(2 * q, 2 * q + 2))
                pipeline(dve, step, 3)
                dve.wait_ge(max_done, NG)
                st = Steps(dve, joined)
                for h in range(HH):
                    st(nc.vector.tensor_tensor_scan(fw[:, h, 0:NG], c.first[layer][:, 0:NG], mp[:, h, 0:NG], -BIG,
                                                    ALU.add, ALU.max))
                st.sync()
                for h in range(HH):
                    st(nc.vector.tensor_tensor_scan(mp[:, h, 0:NG][:, ::-1], c.final[layer][:, 0:NG][:, ::-1],
                                                    fw[:, h, 0:NG][:, ::-1], -BIG, ALU.add, ALU.max))
                st.sync()
                joined_max = mp[:, :, 0:NG].rearrange("p h g -> p g h")
                st.link(nc.vector.tensor_copy(m2[:, :, 0, :], joined_max))
                st.link(nc.vector.tensor_tensor(m2[:, :, 1, :], joined_max, m2[:, :, 0, :], ALU.subtract))
                nc.vector.tensor_copy(c.m[:, 0, :, :, :], m2[0:BN, :, :, :]).then_inc(joined, 1)

            @block.scalar
            def _(act):
                def copy(i, q, ahead):
                    if not lives(i, q, ahead):
                        return
                    g = i * GPI + q + ahead
                    r = (q + ahead) % GPI
                    hold(act, tr_done, g + 1)
                    need(act, mask_ready, g - 3, hold)
                    need(act, qe_ready, g - 3, hold)
                    if layer == 0:
                        need(act, rel_ready, g - 3, hold)
                    rows = KINDS * BN
                    nc.scalar.activation(ohT[0:rows, r, :], pT[r % BT][0:rows, :], ACT.Copy).then_inc(ohT_ready, 1)

                def mask(i, q, ahead):
                    if not lives(i, q, ahead):
                        return
                    g = i * GPI + q + ahead
                    r = (q + ahead) % GPI
                    hold(act, ohT_ready, g + 1)
                    need(act, spread, g - 3, hold)
                    nc.scalar.activation(rhs[0:BN, r, :], ohT[0:BN, r, :], ACT.Copy, bias=-1.0).then_inc(mask_ready, 1)

                def scoresT(i, q, ahead):
                    if not lives(i, q, ahead):
                        return
                    g = i * GPI + q + ahead
                    r = (q + ahead) % GPI
                    hold(act, st_psum, g + 1)
                    nc.scalar.activation(rhs[BN:SR, r, :], pS[BN:SR, :], ACT.Copy).then_inc(sT_ready, 1)

                def head_sums(i, q, ahead):
                    if layer != 0 or not lives(i, q, ahead):
                        return
                    g = i * GPI + q + ahead
                    r = (q + ahead) % GPI
                    hold(act, prod_done, g + 1)
                    for h in range(H):
                        at = D + h * (D // H)
                        last = nc.scalar.activation(
                            junk[:, h, :], prod[:, r % 2, at:at + D // H], ACT.Copy,
                            accum_out=c.s[:, bass.ds((i * SPI + 2 * (q + ahead) + 1) * H + h, 1)])
                    last.then_inc(half_summed, 1)

                def high_part(i, q, ahead):
                    if not lives(i, q, ahead):
                        return
                    g = i * GPI + q + ahead
                    r = (q + ahead) % GPI
                    hold(act, s_ready, g + 1)
                    if layer == 0:
                        hold(act, half_summed, g + 1)
                    need(act, st_psum, g - 1, hold)
                    nc.scalar.activation(
                        sp2[:, r % 2, :, BN:BN + H],
                        c.s[:, bass.ds((i * SPI + 2 * (q + ahead)) * H, 2 * H)].rearrange("p (s h) -> p s h", h=H),
                        ACT.Copy).then_inc(hi_ready, 1)

                def step(i, q):
                    scoresT(i, q, -3)
                    copy(i, q, 1)
                    head_sums(i, q, -1)
                    mask(i, q, -1)
                    high_part(i, q, -1)

                act.wait_ge(cleared, 1)
                copy(0, 0, 0)
                pipeline(act, step, 3)

            @block.tensor
            def _(pe):
                def turn(i, q, ahead):
                    if not lives(i, q, ahead):
                        return
                    g = i * GPI + q + ahead
                    r = (q + ahead) % GPI
                    hold(pe, oh_made, g + 1)
                    need(pe, ohT_ready, g + 1 - BT, hold)
                    for k in range(2):
                        last = nc.tensor.transpose(pT[r % BT][0:KINDS * BN, k * P:(k + 1) * P],
                                                   oh[:, 2 * r + k, :, :].rearrange("p k n -> p (k n)"),
                                                   c.ident_b[:, :])
                    last.then_inc(tr_done, 1)

                def q_of_edges(i, q, b):
                    if not lives(i, q):
                        return
                    t = i * GPI + q
                    pe.wait_ge(ohT_ready, t + 1)
                    need(pe, prod_done, t - 1)
                    for k in range(2):
                        for part in range(3):
                            last = nc.tensor.matmul(pQ[q % 2][:, k * D:(k + 1) * D],
                                                    ohT[0:BN, q, k * P:(k + 1) * P],
                                                    c.q[:, bass.ds(b, 1), part, :].rearrange("p o d -> p (o d)"),
                                                    start=part == 0, stop=part == 2)
                    last.then_inc(qe_ready, 1)

                def relation_of_edges(i, q):
                    if layer != 0 or not lives(i, q):
                        return
                    t = i * GPI + q
                    need(pe, added, t)
                    for k in range(2):
                        for part in range(3):
                            last = nc.tensor.matmul(pR[:, k, :], ohT[BN:P, q, k * P:(k + 1) * P],
                                                    c.rel[BN:P, part, :], start=part == 0, stop=part == 2)
                    last.then_inc(rel_ready, 1)

                def turn_scores(i, q, ahead):
                    if not lives(i, q, ahead):
                        return
                    g = i * GPI + q + ahead
                    r = (q + ahead) % GPI
                    pe.wait_ge(lo_ready, g + 1)
                    need(pe, sT_ready, g)
                    for k in range(2):
                        last = nc.tensor.transpose(pS[:, k * P:(k + 1) * P], sp2[:, r % 2, k, :], c.ident_b[:, :])
                    last.then_inc(st_psum, 1)

                def spread_scores(i, q, ahead):
                    if not lives(i, q, ahead):
                        return
                    g = i * GPI + q + ahead
                    r = (q + ahead) % GPI
                    pe.wait_ge(sT_ready, g + 1)
                    pe.wait_ge(mask_ready, g + 1)
                    need(pe, max_done, g - 1)
                    for j in range(HH):
                        last = nc.tensor.matmul(pM[r % 2][:, j * GE:(j + 1) * GE], c.spread[:, layer, j, :],
                                                rhs[:, r, :], start=True, stop=True)
                    last.then_inc(spread, 1)

                def step(i, q):
                    b = None
                    if lives(i, q):
                        b = pe.value_load(c.gb[layer][0:1, bass.ds(i * GPI + q, 1)], min_val=0, max_val=BB - 1)
                    q_of_edges(i, q, b)
                    spread_scores(i, q, -3)
                    relation_of_edges(i, q)
                    turn(i, q, 2)
                    turn_scores(i, q, -2)

                turn(0, 0, 0)
                turn(0, 1, 0)
                pipeline(pe, step, 3)


def stage_aggregate(nc, c, sem, dram, layer):
    H = HA if layer == 0 else HB
    W = D + H
    T = f"L{layer}_sum_"
    with ExitStack() as ctx:
        def sb(name, shape, dt):
            return ctx.enter_context(nc.sbuf_tensor(T + name, shape, dt))

        def ps(name, shape, dt):
            return ctx.enter_context(nc.psum_tensor(T + name, shape, dt))

        vg = sb("vg", [P, SPI, D], F32)
        stage = [sb(f"stage{u}", [P, 4], I32) for u in range(2)]
        oh_b = sb("oh_b", [P, SPI, BN], BF16)
        oh = [sb(f"oh{q}", [P, 2, BN], F32) for q in range(GPI)]
        ohT = sb("ohT", [BN, 2, GE], BF16)
        diff = sb("diff", [P, 2, 2, H], F32)
        rhs = sb("rhs", [P, 4, 2, W], F32)
        sums = c.q_place[0:BN, 0:BB * W].rearrange("p (b w) -> p b w", w=W)
        pT = [ps(f"pT{u}", [BN, GE], BF16) for u in range(2)]
        pE = [ps(f"pE{u}", [P, 2, H], F32) for u in range(2)]
        pA = [ps(f"pA{u}", [BN, W], F32) for u in range(2)]

        gathered = [sem(T + f"v_gathered{q}") for q in range(GPI)]
        zeroed = sem(T + "sums_zeroed")
        oh_made = sem(T + "onehot_made")
        tr_done = sem(T + "onehot_transposed")
        ohT_ready = sem(T + "onehotT_ready")
        me_ready = sem(T + "maxima_of_edges_ready")
        diff_done = sem(T + "difference_done")
        exp_done = sem(T + "exp_done")
        v_done = sem(T + "weighted_v_done")
        agg_done = sem(T + "group_sum_done")
        acc_done = sem(T + "added_to_bucket")
        moved = sem(T + "sums_moved")

        with nc.Block() as block:

            @block.gpsimd
            def _(pool):
                gather_rows(nc, pool, sem, T, dram.v, c.rec, stage, vg, gathered, v_done)

            @block.sync
            def _(sp):
                sp.wait_ge(acc_done, NG)
                for part in range(2):
                    sp.dma_start(c.acc[part * BN:(part + 1) * BN, :, 0:W],
                                 sums.rearrange("p (t k) w -> p t k w", k=2)[:, :, part, :]
                                 ).then_inc(moved, 16)
                sp.wait_ge(moved, 32)

            @block.vector
            def _(dve):
                def onehot(out, slots):
                    return nc.vector.tensor_tensor(out, c.iota[:, 0:BN].unsqueeze(1).broadcast_to([P, 2, BN]),
                                                   c.rec[:, slots, 1].unsqueeze(2).broadcast_to([P, 2, BN]),
                                                   ALU.is_equal)

                def difference(i, q):
                    if not lives(i, q):
                        return
                    t = i * GPI + q
                    dve.wait_ge(me_ready, t + 1)
                    need(dve, exp_done, t - 1)
                    nc.vector.tensor_tensor(
                        diff[:, q % 2, :, :],
                        c.s[:, bass.ds((i * SPI + 2 * q) * H, 2 * H)].rearrange("p (s h) -> p s h", h=H),
                        pE[q % 2][:, :, :], ALU.subtract).then_inc(diff_done, 1)

                def weighted(i, q, ahead):
                    if not lives(i, q, ahead):
                        return
                    g = i * GPI + q + ahead
                    r = (q + ahead) % GPI
                    need(dve, agg_done, g - 3)
                    onehot(oh[r][:, :, :], bass.ds(i * SPI + 2 * (q + ahead), 2))
                    dve.wait_ge(gathered[r], (i + (q + ahead - r) // GPI) * 32 + 32)
                    dve.wait_ge(exp_done, g + 1)
                    for k in range(2):
                        ins = nc.vector.tensor_tensor(
                            rhs[:, r, k, 0:D].rearrange("p (h d) -> p h d", h=H),
                            vg[:, 2 * r + k, :].rearrange("p (h d) -> p h d", h=H),
                            rhs[:, r, k, D:W].unsqueeze(2).broadcast_to([P, H, D // H]), ALU.mult)
                    ins.then_inc(v_done, 1)

                def accumulate(i, q, ahead):
                    if not lives(i, q, ahead):
                        return
                    g = i * GPI + q + ahead
                    b = dve.value_load(c.gb[layer][0:1, bass.ds(g, 1)], min_val=0, max_val=BB - 1)
                    dve.wait_ge(agg_done, g + 1)
                    need(dve, acc_done, g)
                    row = sums[:, bass.ds(b, 1), :].rearrange("p o w -> p (o w)")
                    nc.vector.tensor_tensor(row, pA[(q + ahead) % 2][:, :], row, ALU.add).then_inc(acc_done, 1)

                def step(i, q):
                    difference(i, q)
                    if lives(i, q, 3):
                        need(dve, tr_done, i * GPI + q)
                        r = (q + 3) % GPI
                        onehot(oh_b[:, 2 * r:2 * r + 2, :], bass.ds(i * SPI + 2 * q + 6, 2)).then_inc(oh_made, 1)
                    weighted(i, q, -1)
                    accumulate(i, q, -3)

                nc.vector.memset(sums[:, :, :], 0.0).then_inc(zeroed, 1)
                dve.wait_ge(zeroed, 1)
                for r in range(3):
                    onehot(oh_b[:, 2 * r:2 * r + 2, :], slice(2 * r, 2 * r + 2)).then_inc(oh_made, 1)
                pipeline(dve, step, 3)

            @block.scalar
            def _(act):
                def copy(i, q, ahead):
                    if not lives(i, q, ahead):
                        return
                    g = i * GPI + q + ahead
                    r = (q + ahead) % 2
                    hold(act, tr_done, g + 1)
                    need(act, me_ready, g - 1, hold)
                    nc.scalar.activation(ohT[:, r, :], pT[r][:, :], ACT.Copy).then_inc(ohT_ready, 1)

                def exponent(i, q):
                    if not lives(i, q):
                        return
                    t = i * GPI + q
                    hold(act, diff_done, t + 1)
                    need(act, agg_done, t - 3, hold)
                    nc.scalar.activation(rhs[:, q, :, D:W], diff[:, q % 2, :, :], ACT.Exp).then_inc(exp_done, 1)

                def step(i, q):
                    copy(i, q, 1)
                    exponent(i, q)

                copy(0, 0, 0)
                pipeline(act, step, 0)

            @block.tensor
            def _(pe):
                def turn(i, q, ahead):
                    if not lives(i, q, ahead):
                        return
                    g = i * GPI + q + ahead
                    r = (q + ahead) % GPI
                    hold(pe, oh_made, g + 1)
                    need(pe, ohT_ready, g - 1, hold)
                    for k in range(2):
                        last = nc.tensor.transpose(pT[r % 2][:, k * P:(k + 1) * P], oh_b[:, 2 * r + k, :], c.ident_b[:, :])
                    last.then_inc(tr_done, 1)

                def maxima_of_edges(i, q):
                    if not lives(i, q):
                        return
                    t = i * GPI + q
                    pe.wait_ge(ohT_ready, t + 1)
                    need(pe, diff_done, t - 1)
                    for k in range(2):
                        for part in range(2):
                            last = nc.tensor.matmul(pE[q % 2][:, k, :], ohT[:, q % 2, k * P:(k + 1) * P],
                                                    c.m[:, :, bass.ds(t, 1), part, :].rearrange("p f o h -> p f (o h)"),
                                                    start=part == 0, stop=part == 1)
                    last.then_inc(me_ready, 1)

                def group_sum(i, q, ahead):
                    if not lives(i, q, ahead):
                        return
                    g = i * GPI + q + ahead
                    r = (q + ahead) % GPI
                    pe.wait_ge(v_done, g + 1)
                    need(pe, acc_done, g - 1)
                    for k in range(2):
                        last = nc.tensor.matmul(pA[r % 2][:, :], oh[r][:, k, :], rhs[:, r, k, :],
                                                start=k == 0, stop=k == 1)
                    last.then_inc(agg_done, 1)

                def step(i, q):
                    maxima_of_edges(i, q)
                    turn(i, q, 1)
                    group_sum(i, q, -2)

                turn(0, 0, 0)
                pipeline(pe, step, 2)


def stage_output(nc, c, sem, dram, weights, layer):
    H = HA if layer == 0 else HB
    T = f"L{layer}_out_"
    Wo, bo, gamma, beta = weights
    with ExitStack() as ctx:
        def sb(name, shape, dt):
            return ctx.enter_context(nc.sbuf_tensor(T + name, shape, dt))

        def ps(name, shape, dt):
            return ctx.enter_context(nc.psum_tensor(T + name, shape, dt))

        w = sb("wo", [P, C2, D], F32)
        b = sb("bo", [P, D], F32)
        z = sb("z", [P, TB, H], F32)
        empty = sb("empty", [P, TB, H], F32)
        msg = sb("msg", [P, 2, D], F32)
        mT = [sb(f"mT{u}", [P, C2, P], F32) for u in range(2)]
        hn = sb("hn", [P, 2, D], F32)
        part = sb("part", [P, 2, D], F32)
        if layer == 0:
            vt = sb("vt", [P, 2, D], F32)
            gb = sb("gamma_beta", [P, 2, D], F32)
            y = c.q_place[:, 0:TB * D].rearrange("p (t d) -> p t d", d=D)
        pT = [ps(f"pT{u}", [P, D], F32) for u in range(2)]
        pO = [ps(f"pO{u}", [P, D], F32) for u in range(2)]

        loaded = sem(T + "w_loaded")
        steps = sem(T + "dve_steps")
        v_loaded = [sem(T + f"v_loaded{u}") for u in range(2)]
        scaled = sem(T + "scaled")
        msg_done = sem(T + "messages_done")
        mT_psum = sem(T + "messages_transposed")
        mT_ready = sem(T + "messagesT_ready")
        hn_ready = sem(T + "hn_ready")
        out_psum = sem(T + "out_psum")
        projected = sem(T + "projected")
        out_done = sem(T + "out_done")
        norm = NormSemaphores(sem, T)
        scaled_y = sem(T + "normalised")
        affine = sem(T + "affine")

        if layer == 0:
            place = PlacingSemaphores(sem, T)
            buffers = placing_buffers(sb)

        with nc.Block() as block:

            @block.gpsimd
            def _(pool):
                if layer == 0:
                    place_records(nc, pool, place, buffers, (c.record, c.row_i), dram.list[1], 0, BY_OUTPUT)
                    for u in range(2):
                        pool.wait_ge(place.scattered[u], BY_OUTPUT * HALF[u] * 16)

            @block.sync
            def _(sp):
                sp.dma_start(w[:, :, :], Wo.rearrange("(c p) n -> p c n", p=P)).then_inc(loaded, 16)
                sp.dma_start(b[:, :], bo.rearrange("(o n) -> o n", o=1).broadcast_to([P, D])).then_inc(loaded, 16)
                if layer == 0:
                    for k, a in enumerate((gamma, beta)):
                        sp.dma_start(gb[:, k, :],
                                     a.rearrange("(o n) -> o n", o=1).broadcast_to([P, D])).then_inc(loaded, 16)
                    with sp.Fori(0, TB // 2) as i:
                        for u in range(2):
                            hold(sp, msg_done, i * 2 + u + 1)
                            sp.dma_start(vt[:, u, :], dram.v[bass.ds((i * 2 + u) * P, P), :]).then_inc(v_loaded[u], 16)

            @block.vector
            def _(dve):
                st = Steps(dve, steps)
                sums = c.acc[:, :, D:D + H]
                st(nc.vector.tensor_scalar(empty[:, :, :], sums, 0.0, None, ALU.is_equal))
                st.link(nc.vector.tensor_scalar(z[:, :, :], sums, 1e-30, None, ALU.max))
                st.link(nc.vector.reciprocal(z[:, :, :], z[:, :, :]))
                dve.wait_ge(loaded, 64 if layer == 0 else 32)
                dve.sem_inc(msg_done, 2)
                dve.sem_inc(out_done, 1)
                dve.sem_inc(projected, 2)

                def heads(a):
                    return a.rearrange("p (h d) -> p h d", h=H)

                def message(t, u):
                    def of_tile(a):
                        return a[:, bass.ds(t, 1), :].rearrange("p o h -> p (o h)").unsqueeze(2).broadcast_to(
                            [P, H, D // H])

                    acc = c.acc[:, bass.ds(t, 1), 0:D].rearrange("p o d -> p (o d)")
                    first = nc.vector.tensor_tensor(heads(msg[:, u, :]), heads(acc), of_tile(z), ALU.mult)
                    if layer == 0:
                        first.then_inc(scaled, 1)
                        dve.wait_ge(v_loaded[u], (t - u) * 8 + 16)
                        nc.vector.tensor_tensor(heads(vt[:, u, :]), heads(vt[:, u, :]), of_tile(empty),
                                                ALU.mult).then_inc(scaled, 1)
                        dve.wait_ge(scaled, 2 * t + 2)
                        first = nc.vector.tensor_tensor(msg[:, u, :], msg[:, u, :], vt[:, u, :], ALU.add)
                    first.then_inc(msg_done, 1)

                def step(t, u):
                    if is_tile(t + 2):
                        dve.wait_ge(mT_psum, t + 1)
                        message(t + 2, u)
                    dve.wait_ge(out_psum, t + 3)
                    nc.vector.tensor_tensor(part[:, u, :], pO[u][:, :], b[:, :], ALU.add).then_inc(projected, 1)
                    dve.wait_ge(projected, t + 3)
                    other = c.x[:, t, :]
                    if layer == 0:
                        dve.wait_ge(hn_ready, t + 1)
                        other = hn[:, u, :]
                    out = y[:, t, :] if layer == 0 else c.x[:, t, :]
                    nc.vector.tensor_tensor(out, part[:, u, :], other, ALU.add).then_inc(out_done, 1)

                message(0, 0)
                message(1, 1)
                tile_pipeline(dve, step)
                dve.wait_ge(out_done, TB + 1)
                if layer == 0:
                    norm_vector(nc, dve, c, norm, y)
                    with dve.Fori(0, NT) as t:
                        dve.wait_ge(scaled_y, t + 1)
                        nc.vector.tensor_tensor(y[:, t, :], y[:, t, :], gb[:, 0, :], ALU.mult).then_inc(affine, 1)
                        nc.vector.tensor_tensor(c.x[:, t, :], c.x[:, t, :], gb[:, 1, :], ALU.add).then_inc(affine, 1)
                        dve.wait_ge(affine, 3 * t + 2)
                        nc.vector.tensor_tensor(c.x[:, t, :], c.x[:, t, :], y[:, t, :], ALU.add).then_inc(affine, 1)
                    dve.wait_ge(affine, 3 * NT)

            @block.scalar
            def _(act):
                def copy(t, u):
                    hold(act, mT_psum, t + 1)
                    hold(act, out_psum, t + 1)
                    nc.scalar.activation(mT[u][:, :, :].rearrange("p c n -> p (c n)"), pT[u][:, :],
                                         ACT.Copy).then_inc(mT_ready, 1)

                def normalised(t, u):
                    nc.scalar.activation(hn[:, u, :], c.x[:, t, :], ACT.Identity, bias=c.shift[:, bass.ds(t, 1)],
                                         scale=c.rstd[:, bass.ds(t, 1)]).then_inc(hn_ready, 1)

                def step(t, u):
                    if is_tile(t + 1):
                        copy(t + 1, 1 - u)
                        if layer == 0:
                            hold(act, out_done, t + 1)
                            normalised(t + 1, 1 - u)

                copy(0, 0)
                if layer == 0:
                    normalised(0, 0)
                tile_pipeline(act, step)
                if layer == 0:
                    norm_scalar(nc, act, norm, c)
                    act.wait_ge(norm.ready, 1)
                    with act.Fori(0, NT) as t:
                        nc.scalar.activation(y[:, t, :], y[:, t, :], ACT.Identity, bias=c.shift[:, bass.ds(t, 1)],
                                             scale=c.rstd[:, bass.ds(t, 1)]).then_inc(scaled_y, 1)

            @block.tensor
            def _(pe):
                pe.wait_ge(loaded, 64 if layer == 0 else 32)

                pe.sem_inc(out_psum, 2)

                def turn(t, u):
                    pe.wait_ge(msg_done, t + 3)
                    for k in range(C2):
                        last = nc.tensor.transpose(pT[u][:, k * P:(k + 1) * P], msg[:, u, k * P:(k + 1) * P],
                                                   c.ident[:, :])
                    last.then_inc(mT_psum, 1)

                def step(t, u):
                    if is_tile(t + 1):
                        turn(t + 1, 1 - u)
                    pe.wait_ge(mT_ready, t + 1)
                    pe.wait_ge(projected, t + 1)
                    for k in range(C2):
                        last = nc.tensor.matmul(pO[u][:, :], mT[u][:, k, :], w[:, k, :], start=k == 0,
                                                stop=k == C2 - 1)
                    last.then_inc(out_psum, 1)

                turn(0, 0)
                tile_pipeline(pe, step)


def stage_gate(nc, c, sem, dram, weights):
    T = "gate_"
    EX = EXPERTS
    gate_w, gate_b, b1 = weights
    with ExitStack() as ctx:
        def sb(name, shape, dt):
            return ctx.enter_context(nc.sbuf_tensor(T + name, shape, dt))

        def ps(name, shape, dt):
            return ctx.enter_context(nc.psum_tensor(T + name, shape, dt))

        h = sb("h", [P, TB, D], F32)
        hn = sb("hn", [P, 2, D], F32)
        gw = sb("gw", [P, C2, EX], F32)
        gb = sb("gb", [P, EX], F32)
        b1_rows = sb("b1_rows", [EX * FC, P], F32)
        hT = [sb(f"hT{u}", [P, C2, P], F32) for u in range(2)]
        zeros = sb("zeros", [P, 8 * D], F32)
        lg = sb("logits", [P, TB, EX], F32)
        one = sb("one_hot", [P, TB, EX], F32)
        tmp = sb("tmp", [P, TB, EX], F32)
        before = sb("before_tile", [P, EX, TB], F32)
        col = sb("columns", [P, 8, TB], F32)
        pT = [ps(f"pT{u}", [P, D], F32) for u in range(2)]
        pG = ps("pG", [P, TB, EX], F32)
        pC = ps("pC", [P, TB, EX], F32)
        pN = ps("pN", [P, TB, EX], F32)
        pB = ps("pB", [P, EX * FC], F32)
        loaded = sem(T + "w_loaded")
        zeroed = sem(T + "zeros_made")
        cleared = sem(T + "buffers_cleared")
        norm = NormSemaphores(sem, T)
        hn_ready = sem(T + "h_ready")
        hT_psum = sem(T + "h_transposed")
        hT_ready = sem(T + "hT_ready")
        logits_done = sem(T + "logits_done")
        b1_psum = sem(T + "b1_transposed")
        steps = sem(T + "dve_steps")
        shifted = sem(T + "logits_shifted")
        exp_done = sem(T + "exp_done")
        chosen = sem(T + "expert_chosen")
        counted = sem(T + "counted")
        placed = sem(T + "placed")
        sent = sem(T + "h_sent")

        place = PlacingSemaphores(sem, T)
        buffers = placing_buffers(sb)

        with nc.Block() as block:

            @block.sync
            def _(sp):
                sp.dma_start(gw[:, :, :], gate_w.rearrange("(c p) e -> p c e", p=P)).then_inc(loaded, 16)
                sp.dma_start(gb[:, :], gate_b.rearrange("(o n) -> o n", o=1).broadcast_to([P, EX])).then_inc(loaded, 16)
                sp.dma_start(b1_rows[:, :], b1.rearrange("e (f p) -> (e f) p", p=P)).then_inc(loaded, 16)
                sp.wait_ge(zeroed, 1)
                for k in range(EX * CAPW // (8 * P)):
                    sp.dma_start(dram.buf[k * 8 * P:(k + 1) * 8 * P, :].rearrange("(p r) d -> p (r d)", r=8),
                                 zeros[:, :]).then_inc(cleared, 16)

            @block.gpsimd
            def _(pool):
                nc.gpsimd.memset(zeros[:, :], 0.0).then_inc(zeroed, 1)
                place_records(nc, pool, place, buffers, (c.record, c.row_i), dram.list[1], BY_OUTPUT, BY_GATE)
                for u in range(2):
                    pool.wait_ge(place.scattered[u], (BY_GATE - BY_OUTPUT) * HALF[u] * 16)
                pool.wait_ge(placed, 1)
                pool.wait_ge(cleared, EX * CAPW // (8 * P) * 16)
                for t in range(NT):
                    nc.gpsimd.indirect_dma_start(out=dram.buf, out_offset=bass.IndirectOffsetOnAxis(
                        ap=c.place[:, 0, t:t + 1], axis=0), in_=h[:, t, :], in_offset=None).then_inc(sent, 16)
                pool.wait_ge(sent, NT * 16)

            @block.vector
            def _(dve):
                norm_vector(nc, dve, c, norm, c.x)
                st = Steps(dve, steps)
                shape = [P, TB, EX]
                def each(a):
                    return a.unsqueeze(2).broadcast_to(shape)
                numbers = c.iota[:, 0:EX].unsqueeze(1).broadcast_to(shape)
                dve.wait_ge(loaded, 48)
                dve.wait_ge(b1_psum, 1)
                st(nc.vector.tensor_copy(c.b1T[:, :], pB[:, :]))
                dve.wait_ge(logits_done, TB + 2)
                st.link(nc.vector.tensor_tensor(lg[:, :, :], pG[:, :, :], gb[:, :].unsqueeze(1).broadcast_to(shape), ALU.add))
                st.link(nc.vector.tensor_reduce(col[:, 0, :], lg[:, :, :], AX.X, ALU.max))
                nc.vector.tensor_tensor(lg[:, :, :], lg[:, :, :], each(col[:, 0, :]), ALU.subtract).then_inc(shifted, 1)
                dve.wait_ge(exp_done, 1)
                st.link(nc.vector.tensor_reduce(col[:, 1, :], lg[:, :, :], AX.X, ALU.add))
                st(nc.vector.reciprocal(col[:, 2, :], col[:, 1, :]))
                st(nc.vector.tensor_scalar(one[:, :, :], lg[:, :, :], 1.0, None, ALU.is_ge))
                st.link(nc.vector.tensor_scalar(tmp[:, :, :], numbers, -1.0, float(EX), ALU.mult, ALU.add))
                st.link(nc.vector.tensor_tensor(tmp[:, :, :], tmp[:, :, :], one[:, :, :], ALU.mult))
                st.link(nc.vector.tensor_reduce(col[:, 3, :], tmp[:, :, :], AX.X, ALU.max))
                nc.vector.tensor_tensor(one[:, :, :], tmp[:, :, :], each(col[:, 3, :]), ALU.is_equal).then_inc(chosen, 1)
                dve.wait_ge(counted, 2)
                dve.wait_ge(chosen, 1)
                for e in range(EX):
                    st(nc.vector.tensor_tensor_scan(before[:, e, :], pN[:, :, e], c.zero[:, 0:TB], 0.0, ALU.add,
                                                    ALU.add))
                st.sync()
                st.link(nc.vector.tensor_tensor(tmp[:, :, :], before[:, :, :].rearrange("p e t -> p t e"),
                                                pN[:, :, :], ALU.subtract))
                st.link(nc.vector.tensor_tensor(tmp[:, :, :], tmp[:, :, :], pC[:, :, :], ALU.add))
                st.link(nc.vector.tensor_tensor(tmp[:, :, :], tmp[:, :, :], one[:, :, :], ALU.mult))
                st.link(nc.vector.tensor_reduce(col[:, 4, :], tmp[:, :, :], AX.X, ALU.add))
                st(nc.vector.tensor_scalar(col[:, 0, :], col[:, 3, :], -float(CAPW), float(CAPW * EX), ALU.mult, ALU.add))
                st(nc.vector.tensor_scalar(col[:, 1, :], col[:, 4, :], float(CAP), None, ALU.is_le))
                st(nc.vector.tensor_scalar(col[:, 5, :], col[:, 4, :], float(CAP), -1.0, ALU.min, ALU.add))
                st.sync()
                st(nc.vector.tensor_tensor(c.weight[:, :], col[:, 2, :], col[:, 1, :], ALU.mult))
                st.link(nc.vector.tensor_tensor(col[:, 5, :], col[:, 5, :], col[:, 0, :], ALU.add))
                st(nc.vector.tensor_copy(c.place[:, 1, :], col[:, 5, :]))
                st.link(nc.vector.tensor_tensor(col[:, 6, :], col[:, 5, :], c.spare[:, :], ALU.subtract))
                st.link(nc.vector.tensor_tensor(col[:, 6, :], col[:, 6, :], col[:, 1, :], ALU.mult))
                st.link(nc.vector.tensor_tensor(col[:, 7, :], col[:, 6, :], c.spare[:, :], ALU.add))
                nc.vector.tensor_copy(c.place[:, 0, :], col[:, 7, :]).then_inc(placed, 1)

            @block.scalar
            def _(act):
                norm_scalar(nc, act, norm, c)
                act.wait_ge(norm.ready, 1)

                def normalised(t, u):
                    for out in (h[:, t, :], hn[:, u, :]):
                        last = nc.scalar.activation(out, c.x[:, t, :], ACT.Identity, bias=c.shift[:, bass.ds(t, 1)],
                                                    scale=c.rstd[:, bass.ds(t, 1)])
                    last.then_inc(hn_ready, 1)

                def copy(t, u):
                    hold(act, hT_psum, t + 1)
                    hold(act, logits_done, t + 1)
                    nc.scalar.activation(hT[u][:, :, :].rearrange("p c n -> p (c n)"), pT[u][:, :],
                                         ACT.Copy).then_inc(hT_ready, 1)

                def step(t, u):
                    if is_tile(t + 2):
                        normalised(t + 2, u)
                    if is_tile(t + 1):
                        copy(t + 1, 1 - u)

                normalised(0, 0)
                normalised(1, 1)
                copy(0, 0)
                tile_pipeline(act, step)
                act.wait_ge(shifted, 1)
                nc.scalar.activation(lg[:, :, :], lg[:, :, :], ACT.Exp).then_inc(exp_done, 1)

            @block.tensor
            def _(pe):
                pe.wait_ge(loaded, 48)
                nc.tensor.transpose(pB[:, :], b1_rows[:, :], c.ident[0:EX * FC, 0:EX * FC]).then_inc(b1_psum, 1)
                pe.sem_inc(logits_done, 2)

                def turn(t, u):
                    pe.wait_ge(hn_ready, t + 1)
                    for k in range(C2):
                        last = nc.tensor.transpose(pT[u][:, k * P:(k + 1) * P], hn[:, u, k * P:(k + 1) * P],
                                                   c.ident[:, :])
                    last.then_inc(hT_psum, 1)

                def step(t, u):
                    if is_tile(t + 1):
                        turn(t + 1, 1 - u)
                    pe.wait_ge(hT_ready, t + 1)
                    for k in range(C2):
                        last = nc.tensor.matmul(pG[:, bass.ds(t, 1), :].rearrange("p o e -> p (o e)"),
                                                hT[u][:, k, :], gw[:, k, :], start=k == 0, stop=k == C2 - 1)
                    last.then_inc(logits_done, 1)

                turn(0, 0)
                tile_pipeline(pe, step)
                pe.wait_ge(chosen, 1)
                for out, m in ((pC, c.upto), (pN, c.ones)):
                    nc.tensor.matmul(out[:, :, :].rearrange("p t e -> p (t e)"), m[:, :],
                                     one[:, :, :].rearrange("p t e -> p (t e)"), start=True,
                                     stop=True).then_inc(counted, 1)


def stage_experts(nc, c, sem, dram, weights):
    T = "experts_"
    EX = EXPERTS
    w1_d, w2_d, b2_d = weights
    A = CAPW // P
    with ExitStack() as ctx:
        def sb(name, shape, dt):
            return ctx.enter_context(nc.sbuf_tensor(T + name, shape, dt))

        def ps(name, shape, dt):
            return ctx.enter_context(nc.psum_tensor(T + name, shape, dt))

        w1 = [sb(f"w1_{u}", [P, C2, FF], F32) for u in range(2)]
        w2 = [sb(f"w2_{u}", [P, FC, D], F32) for u in range(2)]
        b2 = [sb(f"b2_{u}", [P, D], F32) for u in range(2)]
        xe = [sb(f"x_{u}", [P, A, D], F32) for u in range(2)]
        xT = sb("xT", [P, C2, CAPW], F32)
        hT = sb("hT", [P, FC, CAPW], F32)
        y = [sb(f"y_{u}", [P, A, D], F32) for u in range(2)]
        pX = [ps(f"pX{k}", [P, CAPW], F32) for k in range(C2)]
        pH = [ps(f"pH{u}", [P, CAPW], F32) for u in range(2)]
        pY = [ps(f"pY{u}", [P, D], F32) for u in range(2)]
        loaded = [sem(T + f"loaded{u}") for u in range(2)]
        x_psum = sem(T + "x_transposed")
        xT_ready = sem(T + "xT_ready")
        h_psum = sem(T + "hidden_psum")
        relu_done = sem(T + "relu_done")
        y_psum = sem(T + "y_psum")
        y_done = sem(T + "y_done")
        stored = [sem(T + f"stored{u}") for u in range(2)]

        place = PlacingSemaphores(sem, T)
        buffers = placing_buffers(sb)

        with nc.Block() as block:

            @block.gpsimd
            def _(pool):
                place_records(nc, pool, place, buffers, (c.record, c.row_i), dram.list[1], BY_GATE, SCAT)
                for u in range(2):
                    pool.wait_ge(place.scattered[u], (SCAT - BY_GATE) * HALF[u] * 16)

            @block.sync
            def _(sp):
                def load(e, u):
                    sp.dma_start(w1[u][:, :, :],
                                 w1_d[bass.ds(e, 1), :, :].rearrange("o (c p) f -> p (o c) f", p=P)).then_inc(loaded[u], 16)
                    sp.dma_start(w2[u][:, :, :],
                                 w2_d[bass.ds(e, 1), :, :].rearrange("o (f p) d -> p (o f) d", p=P)).then_inc(loaded[u], 16)
                    sp.dma_start(b2[u][:, :], b2_d[bass.ds(e, 1), :].broadcast_to([P, D])).then_inc(loaded[u], 16)
                    sp.dma_start(xe[u][:, :, :], dram.buf[bass.ds(e * CAPW, CAPW), :].rearrange(
                        "(a p) d -> p a d", p=P)).then_inc(loaded[u], 16)

                def store(e, u, n):
                    hold(sp, y_done, n + 2)
                    sp.dma_start(dram.ybuf[bass.ds(e * CAPW, CAPW), :].rearrange("(a p) d -> p a d", p=P),
                                 y[u][:, :, :]).then_inc(stored[u], 16)

                load(0, 0)
                load(1, 1)
                with sp.Fori(0, EX // 2 - 1) as i:
                    for u in range(2):
                        store(i * 2 + u, u, (i * 2 + u + 1) * A)
                        load(i * 2 + u + 2, u)
                for u in range(2):
                    sp.wait_ge(y_done, (EX - 2 + u + 1) * A + 2)
                    sp.dma_start(dram.ybuf[(EX - 2 + u) * CAPW:(EX - 1 + u) * CAPW, :].rearrange("(a p) d -> p a d", p=P),
                                 y[u][:, :, :]).then_inc(stored[u], 16)
                for u in range(2):
                    sp.wait_ge(stored[u], EX // 2 * 16)

            @block.tensor
            def _(pe):
                with pe.Fori(0, EX // 2) as i:
                    for u in range(2):
                        e = i * 2 + u
                        pe.wait_ge(loaded[u], (i + 1) * 64)
                        for k in range(C2):
                            for a in range(A):
                                last = nc.tensor.transpose(pX[k][:, a * P:(a + 1) * P],
                                                           xe[u][:, a, k * P:(k + 1) * P], c.ident[:, :])
                        last.then_inc(x_psum, 1)
                        pe.wait_ge(xT_ready, e + 1)
                        for f in range(FC):
                            pe.wait_ge(relu_done, e * FC + f + 1)
                            for k in range(C2):
                                last = nc.tensor.matmul(pH[f % 2][:, :], w1[u][:, k, f * P:(f + 1) * P], xT[:, k, :],
                                                        start=k == 0, stop=k == C2 - 1)
                            last.then_inc(h_psum, 1)
                        pe.wait_ge(relu_done, e * FC + FC + 2)
                        for a in range(A):
                            pe.wait_ge(y_done, e * A + a + 1)
                            for f in range(FC):
                                last = nc.tensor.matmul(pY[a % 2][:, :], hT[:, f, a * P:(a + 1) * P], w2[u][:, f, :],
                                                        start=f == 0, stop=f == FC - 1)
                            last.then_inc(y_psum, 1)

            @block.scalar
            def _(act):
                act.sem_inc(relu_done, 2)
                with act.Fori(0, EX // 2) as i:
                    for u in range(2):
                        e = i * 2 + u
                        hold(act, x_psum, e + 1)
                        nc.scalar.activation(xT[:, 0, :], pX[0][:, :], ACT.Copy)
                        nc.scalar.activation(xT[:, 1, :], pX[1][:, :], ACT.Copy).then_inc(xT_ready, 1)
                        for f in range(FC):
                            hold(act, h_psum, e * FC + f + 1)
                            nc.scalar.activation(hT[:, f, :], pH[f % 2][:, :], ACT.Relu,
                                                 bias=c.b1T[:, bass.ds(e * FC + f, 1)]).then_inc(relu_done, 1)

            @block.vector
            def _(dve):
                dve.sem_inc(y_done, 2)
                def pair(i, first=False):
                    for u in range(2):
                        e = i * 2 + u
                        if not first:
                            dve.wait_ge(stored[u], i * 16)
                        for a in range(A):
                            dve.wait_ge(y_psum, e * A + a + 1)
                            nc.vector.tensor_tensor(y[u][:, a, :], pY[a % 2][:, :], b2[u][:, :],
                                                    ALU.add).then_inc(y_done, 1)

                pair(0, first=True)
                with dve.Fori(1, EX // 2) as i:
                    pair(i)


def stage_combine(nc, c, sem, dram):
    T = "combine_"
    G = 5
    LIMIT = 3.4028234e38
    assert NT % G == 0
    with ExitStack() as ctx:
        def sb(name, shape, dt):
            return ctx.enter_context(nc.sbuf_tensor(T + name, shape, dt))

        y = sb("y", [P, 2, G, D], F32)
        ok = sb("ok", [P, G, D], I32)
        clean = sb("clean", [P, 2, G, D], F32)
        limit = sb("limit", [P, 2, G, D], F32)
        got = [sem(T + f"got{r}") for r in range(2 * G)]
        made = sem(T + "limits_made")
        weighted = sem(T + "weighted")
        steps = sem(T + "dve_steps")
        cleaned = sem(T + "cleaned")
        added = sem(T + "added")
        with nc.Block() as block:

            @block.gpsimd
            def _(pool):
                for t in range(NT):
                    if t >= 2 * G:
                        pool.wait_ge(cleaned, t // G - 1)
                    nc.gpsimd.indirect_dma_start(
                        out=y[:, t // G % 2, t % G, :], out_offset=None, in_=dram.ybuf,
                        in_offset=bass.IndirectOffsetOnAxis(ap=c.place[:, 1, t:t + 1],
                                                            axis=0)).then_inc(got[t % (2 * G)], 16)

            @block.scalar
            def _(act):
                for t in range(NT):
                    act.wait_ge(got[t % (2 * G)], (t // (2 * G) + 1) * 16)
                    tile = y[:, t // G % 2, t % G, :]
                    nc.scalar.activation(tile, tile, ACT.Copy, scale=c.weight[:, t:t + 1]).then_inc(weighted, 1)

            @block.vector
            def _(dve):
                nc.vector.memset(limit[:, 0, :, :], 1e4).then_inc(made, 1)
                nc.vector.memset(limit[:, 1, :, :], -1e4).then_inc(made, 1)
                dve.wait_ge(made, 2)
                st = Steps(dve, steps)
                for b in range(NT // G):
                    whole, good, kept = y[:, b % 2, :, :], ok[:, :, :], clean[:, b % 2, :, :]
                    st(nc.vector.memset(kept, 0.0))
                    dve.wait_ge(weighted, (b + 1) * G)
                    st.link(nc.vector.tensor_tensor(good, whole, whole, ALU.is_equal))
                    st.link(nc.vector.copy_predicated(kept, good, whole))
                    st.link(nc.vector.tensor_scalar(good, kept, LIMIT, None, ALU.is_gt))
                    st.link(nc.vector.copy_predicated(kept, good, limit[:, 0, :, :]))
                    st.link(nc.vector.tensor_scalar(good, kept, -LIMIT, None, ALU.is_lt))
                    st(nc.vector.copy_predicated(kept, good, limit[:, 1, :, :]))
                    st.sync()
                    dve.sem_inc(cleaned, 1)
                    x = c.x[:, b * G:(b + 1) * G, :]
                    nc.vector.tensor_tensor(x, x, kept, ALU.add).then_inc(added, 1)
                dve.wait_ge(added, NT // G)


KEEP = N // 2 - 1
G4 = 4 * P


def stage_last(nc, c, sem, dram, weights, out):
    T = "last_"
    wr_d, br_d, w1_d, b1_d, w2_d, b2_d = weights
    NP = TB * P
    with ExitStack() as ctx:
        def sb(name, shape, dt):
            return ctx.enter_context(nc.sbuf_tensor(T + name, shape, dt))

        def ps(name, shape, dt):
            return ctx.enter_context(nc.psum_tensor(T + name, shape, dt))

        h = [sb(f"h{u}", [P, D], F32) for u in range(2)]
        hT = sb("hT", [P, C2, NP], F32)
        wr = sb("wr", [P, C2], F32)
        br = sb("br", [P, 1], F32)
        w1 = sb("w1", [P, C2, FF], F32)
        w2 = sb("w2", [P, FC, D], F32)
        b1_rows = sb("b1_rows", [FC, P], F32)
        b1T = sb("b1T", [P, FC], F32)
        b2 = sb("b2", [1, D], F32)
        gT = sb("gT", [P, FC, G4], F32)
        y = sb("y", [P, TB, D], F32)
        wcol = sb("wcol", [P, TB], F32)
        wrow = sb("wrow", [TB, P], F32)
        wall = sb("wall", [P, N], F32)
        earlier = sb("earlier", [P, P], F32)
        flags = sb("flags", [P, N], F32)
        flags_tile = sb("flags_tile", [P, P], F32)
        rank = sb("rank", [P, 3, TB], F32)
        coef = sb("coef", [P, 3, TB], F32)
        pT = [ps(f"pT{u}", [P, D], F32) for u in range(2)]
        pW = ps("pW", [P, TB], F32)
        pS = ps("pS", [P, P], F32)
        pH = [ps(f"pH{u}", [P, G4], F32) for u in range(2)]
        pY = [ps(f"pY{u}", [P, D], F32) for u in range(2)]
        loaded = sem(T + "w_loaded")
        norm = NormSemaphores(sem, T)
        mask_made = sem(T + "mask_made")
        h_ready = sem(T + "h_ready")
        h_psum = sem(T + "h_transposed")
        hT_ready = sem(T + "hT_ready")
        h_added = sem(T + "h_added")
        w_psum = sem(T + "w_psum")
        w_ready = sem(T + "w_ready")
        row_psum = sem(T + "w_transposed")
        row_ready = sem(T + "w_row_ready")
        b1_ready = sem(T + "b1_ready")
        row_out = sem(T + "w_row_stored")
        row_in = sem(T + "w_row_loaded")
        steps = sem(T + "dve_steps")
        hid_psum = sem(T + "hidden_psum")
        gelu_done = sem(T + "gelu_done")
        y_psum = sem(T + "y_psum")
        y_ready = sem(T + "y_ready")
        final = sem(T + "final")
        stored = sem(T + "stored")

        with nc.Block() as block:

            @block.sync
            def _(sp):
                sp.dma_start(wr[:, :], wr_d.rearrange("(c p) o -> p (c o)", p=P),
                             allow_slow_non_contiguous=True).then_inc(loaded, 16)
                sp.dma_start(br[:, :], br_d.rearrange("(o n) -> o n", o=1).broadcast_to([P, 1])).then_inc(loaded, 16)
                sp.dma_start(b1_rows[:, :], b1_d.rearrange("(f p) -> f p", p=P)).then_inc(loaded, 16)
                sp.dma_start(b2[:, :], b2_d.rearrange("(o n) -> o n", o=1)).then_inc(loaded, 16)
                sp.dma_start(w1[:, :, :], w1_d.rearrange("(c p) f -> p c f", p=P)).then_inc(loaded, 16)
                sp.dma_start(w2[:, :, :], w2_d.rearrange("(f p) d -> p f d", p=P)).then_inc(loaded, 16)
                sp.wait_ge(row_ready, 1)
                sp.dma_start(dram.wrow.rearrange("(t p) -> t p", p=P), wrow[:, :]).then_inc(row_out, 16)
                sp.wait_ge(row_out, 16)
                sp.dma_start(wall[:, :], dram.wrow[0:N].rearrange("(o n) -> o n", o=1).broadcast_to([P, N])).then_inc(row_in, 16)
                for t in range(0, NT - 1, 4):
                    sp.wait_ge(final, t + 4)
                    sp.dma_start(out[t * P:(t + 4) * P, :].rearrange("(t p) d -> p t d", p=P),
                                 y[:, t:t + 4, :]).then_inc(stored, 16)
                sp.wait_ge(final, NT)
                sp.dma_start(out[(NT - 1) * P:N, :], y[0:LAST, NT - 1, :]).then_inc(stored, 16)
                sp.wait_ge(stored, (NT - 1) // 4 * 16 + 16)

            @block.gpsimd
            def _(pool):
                nc.gpsimd.memset(earlier[:, :], 1.0).then_inc(mask_made, 1)
                pool.wait_ge(mask_made, 1)
                nc.gpsimd.affine_select(out=earlier[:, :], in_=earlier[:, :], compare_op=ALU.is_gt, fill=0.0,
                                        base=0, pattern=[[-1, P]], channel_multiplier=1).then_inc(mask_made, 1)
                with pool.Fori(0, TB // 2) as i:
                    for u in range(2):
                        t = i * 2 + u
                        hold(pool, h_ready, t + 1)
                        nc.gpsimd.tensor_tensor(c.x[:, t, :], c.x[:, t, :], h[u][:, :], ALU.add).then_inc(h_added, 1)

            @block.vector
            def _(dve):
                norm_vector(nc, dve, c, norm, c.x)
                st = Steps(dve, steps)
                dve.wait_ge(w_psum, TB)
                nc.vector.tensor_scalar(wcol[:, :], pW[:, :], br[:, 0:1], None, ALU.add).then_inc(w_ready, 1)
                dve.wait_ge(row_psum, 1)
                nc.vector.tensor_copy(wrow[:, :], pS[0:TB, :]).then_inc(row_ready, 1)
                dve.wait_ge(row_in, 16)
                dve.wait_ge(mask_made, 2)
                st.link(nc.vector.memset(rank[:, :, :], 0.0))
                for t in range(NT):
                    at, n = t * P, min(P, N - t * P)
                    mine = wcol[:, t:t + 1]
                    if t:
                        st(nc.vector.tensor_scalar(flags[:, 0:at], wall[:, 0:at], mine, 0.0, ALU.is_ge, ALU.add,
                                                   accum_out=rank[:, 0, t:t + 1]))
                    st(nc.vector.tensor_scalar(flags[:, at:N], wall[:, at:N], mine, 0.0, ALU.is_gt, ALU.add,
                                               accum_out=rank[:, 1, t:t + 1]))
                    st.link(nc.vector.scalar_tensor_tensor(flags_tile[:, 0:n], wall[:, at:at + n], mine,
                                                           earlier[:, 0:n], ALU.is_equal, ALU.mult,
                                                           accum_out=rank[:, 2, t:t + 1]))
                st.link(nc.vector.tensor_tensor(coef[:, 0, 0:NT], rank[:, 0, 0:NT], rank[:, 1, 0:NT], ALU.add))
                st.link(nc.vector.tensor_tensor(coef[:, 0, 0:NT], coef[:, 0, 0:NT], rank[:, 2, 0:NT], ALU.add))
                st.link(nc.vector.tensor_scalar(coef[:, 1, 0:NT], coef[:, 0, 0:NT], float(KEEP), None, ALU.is_lt))
                st.link(nc.vector.tensor_tensor(coef[:, 2, 0:NT], coef[:, 1, 0:NT], wcol[:, 0:NT], ALU.mult))
                dve.wait_ge(h_added, TB)
                with dve.Fori(0, NT) as t:
                    dve.wait_ge(y_ready, t + 1 + 2)
                    nc.vector.scalar_tensor_tensor(y[:, t, :], y[:, t, :], coef[:, 2, bass.ds(t, 1)], c.x[:, t, :],
                                                   ALU.mult, ALU.add).then_inc(final, 1)

            @block.scalar
            def _(act):
                norm_scalar(nc, act, norm, c)
                act.wait_ge(norm.ready, 1)
                act.wait_ge(b1_ready, 1)
                nc.scalar.activation(b1T[:, :], pS[:, 0:FC], ACT.Copy).then_inc(b1_ready, 1)

                def normalised(t, u):
                    nc.scalar.activation(h[u][:, :], c.x[:, t, :], ACT.Identity, bias=c.shift[:, bass.ds(t, 1)],
                                         scale=c.rstd[:, bass.ds(t, 1)]).then_inc(h_ready, 1)

                def copy(t, u):
                    hold(act, h_psum, t + 1)
                    nc.scalar.activation(hT[:, :, bass.ds(t * P, P)], pT[u][:, :].rearrange("p (c n) -> p c n", n=P),
                                         ACT.Copy).then_inc(hT_ready, 1)

                def step(t, u):
                    if is_tile(t + 2):
                        hold(act, h_added, t + 1)
                        normalised(t + 2, u)
                    if is_tile(t + 1):
                        copy(t + 1, 1 - u)

                normalised(0, 0)
                normalised(1, 1)
                copy(0, 0)
                tile_pipeline(act, step)
                act.sem_inc(gelu_done, 2)
                act.sem_inc(y_ready, 2)

                def mlp(g, tiles, wait):
                    for f in range(FC):
                        wait(act, hid_psum, g * FC + f + 1)
                        nc.scalar.activation(gT[:, f, 0:tiles * P], pH[f % 2][:, 0:tiles * P], ACT.Gelu_apprx_tanh,
                                             bias=b1T[:, f:f + 1]).then_inc(gelu_done, 1)
                    for a in range(tiles):
                        wait(act, y_psum, g * 4 + a + 1)
                        at = g * 4 + a
                        dst = y[:, at, :]
                        nc.scalar.activation(dst, pY[a % 2][:, :], ACT.Copy).then_inc(y_ready, 1)

                with act.Fori(0, NT // 4) as g:
                    mlp(g, 4, hold)
                mlp(NT // 4, NT % 4, lambda e, s, v: e.wait_ge(s, v))

            @block.tensor
            def _(pe):
                pe.wait_ge(loaded, 96)
                nc.tensor.transpose(pS[:, 0:FC], b1_rows[:, :], c.ident[0:FC, 0:FC]).then_inc(b1_ready, 1)

                def turn(t, u):
                    pe.wait_ge(h_ready, t + 1)
                    for k in range(C2):
                        last = nc.tensor.transpose(pT[u][:, k * P:(k + 1) * P], h[u][:, k * P:(k + 1) * P],
                                                   c.ident[:, :])
                    last.then_inc(h_psum, 1)

                def step(t, u):
                    if is_tile(t + 2):
                        pe.wait_ge(hT_ready, t + 1)
                        turn(t + 2, u)

                turn(0, 0)
                turn(1, 1)
                tile_pipeline(pe, step)
                def mlp(g, tiles):
                    cols = bass.ds(g * G4, tiles * P)
                    for f in range(FC):
                        pe.wait_ge(gelu_done, g * FC + f + 1)
                        for k in range(C2):
                            last = nc.tensor.matmul(pH[f % 2][:, 0:tiles * P], w1[:, k, f * P:(f + 1) * P],
                                                    hT[:, k, cols], start=k == 0, stop=k == C2 - 1)
                        last.then_inc(hid_psum, 1)
                    pe.wait_ge(gelu_done, g * FC + FC + 2)
                    for a in range(tiles):
                        pe.wait_ge(y_ready, g * 4 + a + 1)
                        nc.tensor.matmul(pY[a % 2][:, :], c.ones[0:1, :], b2[:, :], start=True, stop=False)
                        for f in range(FC):
                            last = nc.tensor.matmul(pY[a % 2][:, :], gT[:, f, a * P:(a + 1) * P], w2[:, f, :],
                                                    start=False, stop=f == FC - 1)
                        last.then_inc(y_psum, 1)

                pe.wait_ge(hT_ready, TB)
                mlp(0, 4)
                for t in range(TB):
                    for k in range(C2):
                        last = nc.tensor.matmul(pW[:, t:t + 1], hT[:, k, t * P:(t + 1) * P], wr[:, k:k + 1],
                                                start=k == 0, stop=k == C2 - 1)
                    last.then_inc(w_psum, 1)
                pe.wait_ge(w_ready, 1)
                pe.wait_ge(b1_ready, 2)
                nc.tensor.transpose(pS[0:TB, :], wcol[:, :], c.ident[:, :]).then_inc(row_psum, 1)
                with pe.Fori(1, NT // 4) as g:
                    mlp(g, 4)
                mlp(NT // 4, NT % 4)


class Dram:
    pass


def gnn_ffn_kernel(nc, a, out):
    with ExitStack() as ctx:
        def sb(name, shape, dt):
            return ctx.enter_context(nc.sbuf_tensor(name, shape, dt))

        open_sems = []

        def sem(name):
            open_sems.append(nc.alloc_semaphore(name))
            return open_sems[-1]

        def stage(program, *args):
            program(nc, c, sem, *args)
            nc.clear_and_free_semaphores(open_sems)
            open_sems.clear()
            nc.all_engine_barrier()

        c, dram = Consts(), Dram()
        dram.k = nc.dram_tensor("k_table", [TB * P, D], F32, kind="Internal").ap()
        dram.v = nc.dram_tensor("v_table", [TB * P, D], F32, kind="Internal").ap()
        dram.buf = nc.dram_tensor("expert_in", [EXPERTS * CAPW + TB * P, D], F32, kind="Internal").ap()
        dram.ybuf = nc.dram_tensor("expert_out", [EXPERTS * CAPW, D], F32, kind="Internal").ap()
        dram.wrow = nc.dram_tensor("node_weights", [TB * P], F32, kind="Internal").ap()
        dram.list = [nc.dram_tensor(f"edge_list{k}", [P * SW, 4], F32, kind="Internal").ap() for k in range(2)]
        c.ident = sb("ident", [P, P], F32)
        c.ident_b = sb("ident_b", [P, P], BF16)
        c.before = sb("before", [P, P], F32)
        c.upto = sb("upto", [P, P], F32)
        c.ones = sb("ones", [P, P], F32)
        c.spread = sb("spread", [SR, 2, HB // 2, P], BF16)
        c.iota_i = sb("iota_i", [P, 256], I32)
        c.iota = sb("iota", [P, 256], F32)
        c.x = sb("x", [P, TB, D], F32)
        c.stats = sb("stats", [P, TB, 6], F32)
        c.norm = sb("norm", [P, 4, TB], F32)
        c.rstd = sb("rstd", [P, TB], F32)
        c.shift = sb("shift", [P, TB], F32)
        c.zero = sb("zero", [P, TB], F32)
        c.spare = sb("spare", [P, TB], F32)
        c.spare_i = sb("spare_i", [P, TB], I32)
        attention = ctx.enter_context(ExitStack())

        def sb(name, shape, dt):
            return attention.enter_context(nc.sbuf_tensor(name, shape, dt))

        c.rec = sb("rec", [P, SW, 4], F32)
        c.gb = [sb(f"group_bucket{k}", [P, GW], I32) for k in range(2)]
        c.first = [sb(f"first_of_bucket{k}", [P, GW], F32) for k in range(2)]
        c.final = [sb(f"last_of_bucket{k}", [P, GW], F32) for k in range(2)]
        c.record = sb("record1", [P, EC, 4], F32)
        c.row_i = sb("row1_i", [P, EC], I32)
        c.rel = sb("rel_parts", [P, 3, NREL], BF16)
        c.q_place = sb("q_place", [P, max(BK * EC, BB * 3 * D // 2)], F32)
        c.q = c.q_place[0:BN, 0:BB * 3 * D // 2].bitcast(BF16).rearrange("p (b k d) -> p b k d", k=3, d=D)
        stage(stage_constants, a["x"])
        for layer in range(2):
            tag = f"L{layer}_gnn_"
            ws = [a[tag + n] for n in ("Wq", "bq", "Wk", "bk", "Wv", "bv")]
            ws += [a[tag + "rel_w"], a[tag + "query_emb"]] if layer == 0 else [None, None]
            stage(stage_place_and_project, (a["src"], a["dst"], a["edge_type_64"]), ws, dram, layer)
            lay = ctx.enter_context(ExitStack())
            c.s = lay.enter_context(nc.sbuf_tensor(f"scores{layer}", [P, SW * HB], F32))
            c.m = lay.enter_context(nc.sbuf_tensor(f"maxima{layer}", [BN, 2, NG, 2, (HA, HB)[layer] // 2], BF16))
            stage(stage_scores, dram, layer)
            with ExitStack() as agg:
                c.acc = agg.enter_context(nc.sbuf_tensor(f"sums{layer}", [P, TB, D + HB], F32))
                stage(stage_aggregate, dram, layer)
                ws = [a[tag + "Wo"], a[tag + "bo"]]
                ws += [a[tag + "gamma"], a[tag + "beta"]] if layer == 0 else [None, None]
                stage(stage_output, dram, ws, layer)
            lay.close()
            if layer == 0:
                with ExitStack() as moe:
                    c.b1T = moe.enter_context(nc.sbuf_tensor("b1T", [P, EXPERTS * FC], F32))
                    c.place = moe.enter_context(nc.sbuf_tensor("place", [P, 2, TB], I32))
                    c.weight = moe.enter_context(nc.sbuf_tensor("weight", [P, TB], F32))
                    stage(stage_gate, dram, (a["L0_ffn_gate_w"], a["L0_ffn_gate_b"], a["L0_ffn_b1"]))
                    stage(stage_experts, dram, (a["L0_ffn_w1"], a["L0_ffn_w2"], a["L0_ffn_b2"]))
                    stage(stage_combine, dram)
        attention.close()
        stage(stage_last, dram, [a["L1_ffn_" + n] for n in ("wr", "br", "w1", "b1", "w2", "b2")], out)


_INS = ['x', 'src', 'dst', 'edge_type_64', 'L0_gnn_query_emb', 'L0_gnn_Wq', 'L0_gnn_bq', 'L0_gnn_Wk', 'L0_gnn_bk',
        'L0_gnn_Wv', 'L0_gnn_bv', 'L0_gnn_rel_w', 'L0_gnn_Wo', 'L0_gnn_bo', 'L0_gnn_gamma', 'L0_gnn_beta',
        'L0_ffn_gate_w', 'L0_ffn_gate_b', 'L0_ffn_w1', 'L0_ffn_b1', 'L0_ffn_w2', 'L0_ffn_b2', 'L1_gnn_Wq',
        'L1_gnn_bq', 'L1_gnn_Wk', 'L1_gnn_bk', 'L1_gnn_Wv', 'L1_gnn_bv', 'L1_gnn_Wo', 'L1_gnn_bo',
        'L1_ffn_attention_mask', 'L1_ffn_wr', 'L1_ffn_br', 'L1_ffn_w1', 'L1_ffn_b1', 'L1_ffn_w2', 'L1_ffn_b2']


def laid_out(inputs):
    a = {name: np.ascontiguousarray(inputs[name]) for name in _INS}
    for n in ("Wq", "Wk", "Wv"):
        w = a["L1_gnn_" + n]
        a["L1_gnn_" + n] = np.ascontiguousarray(w.reshape(D, D // HB, HB).transpose(0, 2, 1).reshape(D, D))
        b = a["L1_gnn_b" + n[1]]
        a["L1_gnn_b" + n[1]] = np.ascontiguousarray(b.reshape(D // HB, HB).transpose(1, 0).reshape(D))
    w = a["L1_gnn_Wo"]
    a["L1_gnn_Wo"] = np.ascontiguousarray(w.reshape(D // HB, HB, D).transpose(1, 0, 2).reshape(D, D))
    return a


def kernel(**inputs):
    import concourse.bacc as bacc
    from concourse.bass_utils import run_bass_kernel_spmd

    nc = bacc.Bacc("TRN2", target_bir_lowering=False, num_devices=1)
    arrays, args = {}, {}
    for name, a in laid_out(inputs).items():
        arrays[f"in_{name}"] = a
        args[name] = nc.dram_tensor(f"in_{name}", a.shape, mybir.dt.from_np(a.dtype), kind="ExternalInput").ap()
    out = nc.dram_tensor("out_x", [N, D], F32, kind="ExternalOutput").ap()
    gnn_ffn_kernel(nc, args, out)
    r = run_bass_kernel_spmd(nc, [arrays], core_ids=[0])
    return r.results[0]["out_x"]
```
